# Optimizing a Trainium2 kernel written in Bass

```python
import numpy as np
import jax
import jax.numpy as jnp

def _softmax(x, axis=-1):
    return jax.nn.softmax(x, axis=axis)

def _gelu(x):
    return jax.nn.gelu(x, approximate=True)

def _silu(x):
    return jax.nn.silu(x)

def _sigmoid(x):
    return jax.nn.sigmoid(x)

def _layernorm(x, axis=-1, eps=1e-05):
    m = jnp.mean(x, axis=axis, keepdims=True)
    v = jnp.var(x, axis=axis, keepdims=True)
    return (x - m) / jnp.sqrt(v + eps)

def _scatter_add(tgt, idx, src, axis=0):
    return tgt.at[idx].add(src)

def _segment_sum(src, seg, n):
    return jax.ops.segment_sum(src, seg, n)
kernel_name = 'mk_prb_d2_jaxref_r8_03c680'

def setup_inputs(seed: int=0):
    np.random.seed(seed)
    _w = jnp.asarray

    def _L0_attn_setup():
        import jax, jax.numpy as jnp
        import numpy as np
        DIM = 128
        HEADS = 16
        HEAD_DIM = DIM // HEADS
        COLLAPSE_THRESHOLD = 0.27
        SHARPNESS = 15.0
        LN_EPS = 1e-05
        NORM_EPS = 1e-12

        def _layernorm(x, gamma, beta):
            mu = jnp.mean(x, axis=-1, keepdims=True)
            var = jnp.mean(jnp.square(x - mu), axis=-1, keepdims=True)
            return (x - mu) * jax.lax.rsqrt(var + LN_EPS) * gamma + beta

        def _l2_normalize(x):
            n = jnp.sqrt(jnp.sum(jnp.square(x), axis=-1, keepdims=True))
            return x / jnp.maximum(n, NORM_EPS)
        key = jax.random.key(seed)
        ks = jax.random.split(key, 9)
        B, T = (2, 256)
        s = 1.0 / np.sqrt(DIM)
        sh = 1.0 / np.sqrt(HEAD_DIM)
        return {'x': jax.random.normal(ks[0], (B, T, DIM), dtype=jnp.float32), 'w_q': jax.random.normal(ks[1], (DIM, DIM), dtype=jnp.float32) * s, 'w_k': jax.random.normal(ks[2], (DIM, DIM), dtype=jnp.float32) * s, 'w_v': jax.random.normal(ks[3], (DIM, DIM), dtype=jnp.float32) * s, 'g_q': jax.random.normal(ks[4], (HEAD_DIM,), dtype=jnp.float32) * sh, 'g_k': jax.random.normal(ks[5], (HEAD_DIM,), dtype=jnp.float32) * sh, 'w_o': jax.random.normal(ks[6], (DIM, DIM), dtype=jnp.float32) * s, 'b_o': jnp.zeros((DIM,), dtype=jnp.float32), 'gamma': jnp.ones((DIM,), dtype=jnp.float32), 'beta': jnp.zeros((DIM,), dtype=jnp.float32)}
    _L0_attn_in = _L0_attn_setup()

    def _L0_ffn_setup():
        import jax, jax.numpy as jnp
        import numpy as np
        DIM = 128
        DEPTH = 6
        HEADS = 16
        DIM_HEAD = 64
        WINDOW = 32
        INNER = HEADS * DIM_HEAD
        DIM_INNER = int(DIM * 4 * 2 / 3)
        QK_SCALE = 8.0

        def shift_tokens(t):
            a, s = jnp.split(t, 2, -1)
            s = jnp.pad(s, ((0, 0), (1, 0), (0, 0)))[:, :-1]
            return jnp.concatenate([a, s], -1)

        def l2norm(t):
            return t / jnp.maximum(jnp.linalg.norm(t, axis=-1, keepdims=True), 1e-12)

        def rotate_half(x):
            x1, x2 = jnp.split(x, 2, -1)
            return jnp.concatenate([-x2, x1], -1)

        def rotary_tables(n):
            half = jnp.arange(0, DIM_HEAD, 2, dtype=jnp.float32)
            inv_freq = 1.0 / 10000.0 ** (half / DIM_HEAD)
            t = jnp.arange(n, dtype=jnp.float32)
            freqs = t[:, None] * inv_freq[None, :]
            freqs = jnp.concatenate([freqs, freqs], -1)
            base_scale = (half + 0.4 * DIM_HEAD) / (1.4 * DIM_HEAD)
            power = (t - n // 2) / (WINDOW // 2)
            scale = base_scale[None, :] ** power[:, None]
            scale = jnp.concatenate([scale, scale], -1)
            return (freqs, scale)

        def local_attention(q, k, v):
            b, h, n, d = q.shape
            w = WINDOW
            nw = n // w
            bq = q.reshape(b, h, nw, w, d)
            bk = k.reshape(b, h, nw, w, d)
            bv = v.reshape(b, h, nw, w, d)

            def look(t):
                p = jnp.pad(t, ((0, 0), (0, 0), (1, 0), (0, 0), (0, 0)))
                return jnp.concatenate([p[:, :, :nw], p[:, :, 1:]], axis=3)
            bk2, bv2 = (look(bk), look(bv))
            seq = jnp.arange(n).reshape(nw, w)
            seq_p = jnp.pad(seq, ((1, 0), (0, 0)), constant_values=-1)
            jt = jnp.concatenate([seq_p[:nw], seq_p[1:]], axis=1)
            it = seq[:, :, None]
            jb = jt[:, None, :]
            mask = (it < jb) | (it > jb + w) | (jb == -1)
            sim = jnp.einsum('bhwie,bhwje->bhwij', bq, bk2) * QK_SCALE
            sim = jnp.where(mask, -jnp.finfo(sim.dtype).max, sim)
            attn = jax.nn.softmax(sim, -1)
            out = jnp.einsum('bhwij,bhwje->bhwie', attn, bv2)
            return out.reshape(b, h, n, d)

        def attn_layer(x, Wqkv, qs, ksc, Wo):
            b, n, _ = x.shape
            qkv = x @ Wqkv
            q, k, v = jnp.split(qkv, 3, -1)
            sh = lambda t: t.reshape(b, n, HEADS, DIM_HEAD).transpose(0, 2, 1, 3)
            q, k, v = (sh(q), sh(k), sh(v))
            q = l2norm(q) * qs
            k = l2norm(k) * ksc
            freqs, scale = rotary_tables(n)
            cos, sin = (jnp.cos(freqs), jnp.sin(freqs))
            q = q * cos * scale + rotate_half(q) * sin * scale
            inv = 1.0 / scale
            k = k * cos * inv + rotate_half(k) * sin * inv
            out = local_attention(q, k, v)
            out = out.transpose(0, 2, 1, 3).reshape(b, n, INNER)
            return out @ Wo

        def ffn_layer(x, g, bln, W1, b1, W2, b2):
            mu = x.mean(-1, keepdims=True)
            var = ((x - mu) ** 2).mean(-1, keepdims=True)
            xn = (x - mu) / jnp.sqrt(var + 1e-05) * g + bln
            hg = xn @ W1 + b1
            a, gate = jnp.split(hg, 2, -1)
            return a * jax.nn.gelu(gate, approximate=False) @ W2 + b2
        key = jax.random.key(seed)
        ks = jax.random.split(key, 8)
        B, N = (2, 256)
        init = lambda k, shape: jax.random.normal(k, shape, jnp.float32) * 0.02
        return {'x': jax.random.normal(ks[0], (B, N, DIM), jnp.float32), 'Wqkv': init(ks[1], (DEPTH, DIM, 3 * INNER)), 'q_scale': jnp.ones((DEPTH, DIM_HEAD), jnp.float32), 'k_scale': jnp.ones((DEPTH, DIM_HEAD), jnp.float32), 'Wo': init(ks[2], (DEPTH, INNER, DIM)), 'ln_g': jnp.ones((DEPTH, DIM), jnp.float32), 'ln_b': jnp.zeros((DEPTH, DIM), jnp.float32), 'W1': init(ks[3], (DEPTH, DIM, 2 * DIM_INNER)), 'b1': jnp.zeros((DEPTH, 2 * DIM_INNER), jnp.float32), 'W2': init(ks[4], (DEPTH, DIM_INNER, DIM)), 'b2': jnp.zeros((DEPTH, DIM), jnp.float32)}
    _L0_ffn_in = _L0_ffn_setup()

    def _L1_attn_setup():
        import jax, jax.numpy as jnp
        import numpy as np
        B, T, C = (64, 32, 128)
        N_HEAD, HEAD_SIZE, KV_RANK = (16, 64, 128)
        BLOCK_SIZE = 32
        key = jax.random.key(seed)
        ks = jax.random.split(key, 5)
        HD = N_HEAD * HEAD_SIZE

        def init(k, shape):
            fan_in = shape[0]
            bound = 1.0 / np.sqrt(fan_in)
            return jax.random.uniform(k, shape, jnp.float32, -bound, bound)
        return {'x': jax.random.normal(ks[0], (B, T, C), jnp.float32), 'w_kv_down': init(ks[1], (C, KV_RANK)), 'w_kv_up': init(ks[2], (KV_RANK, 2 * HD)), 'w_q': init(ks[3], (C, HD)), 'w_out': init(ks[4], (HD, C))}
    _L1_attn_in = _L1_attn_setup()

    def _L1_ffn_setup():
        import jax, jax.numpy as jnp
        import numpy as np
        E, G, TOPK = (32, 16, 2)
        HID, INTER, A_INTER = (128, 256, 128)
        CAP_FACTOR = 1.25
        SCALE = 0.05

        def _stats(x):
            mean = x.mean(-1, keepdims=True)
            std = jnp.std(x, axis=-1, keepdims=True, ddof=1)
            mn = x.min(-1, keepdims=True)
            mx = x.max(-1, keepdims=True)
            l2 = jnp.linalg.norm(x, axis=-1, keepdims=True)
            sp = (jnp.abs(x) < 1e-06).astype(x.dtype).mean(-1, keepdims=True)
            return jnp.concatenate([mean, std, mn, mx, l2, sp], -1)
        key = jax.random.key(seed)
        ks = jax.random.split(key, 8)
        B, N = (4, 128)
        s = lambda k, shape, sc: jax.random.normal(k, shape, jnp.float32) * sc
        return {'x': jax.random.normal(ks[0], (B, N, HID), jnp.float32), 'r1_w': s(ks[1], (HID // 2, HID + 6), 0.02), 'r1_b': jnp.zeros((HID // 2,), jnp.float32), 'r2_w': s(ks[2], (E, HID // 2), 0.02), 'w_up': s(ks[3], (E, 2 * INTER, HID), 0.02), 'w_down': s(ks[4], (E, HID, INTER), 0.02), 'a_up': s(ks[5], (G, 2 * A_INTER, HID), 0.02), 'a_down': s(ks[6], (G, HID, A_INTER), 0.02)}
    _L1_ffn_in = _L1_ffn_setup()
    _d = {'L0_attn_x': _L0_attn_in['x'], 'L0_attn_w_q': _L0_attn_in['w_q'], 'L0_attn_w_k': _L0_attn_in['w_k'], 'L0_attn_w_v': _L0_attn_in['w_v'], 'L0_attn_g_q': _L0_attn_in['g_q'], 'L0_attn_g_k': _L0_attn_in['g_k'], 'L0_attn_w_o': _L0_attn_in['w_o'], 'L0_attn_b_o': _L0_attn_in['b_o'], 'L0_attn_gamma': _L0_attn_in['gamma'], 'L0_attn_beta': _L0_attn_in['beta'], 'L0_ffn_Wqkv': _L0_ffn_in['Wqkv'], 'L0_ffn_q_scale': _L0_ffn_in['q_scale'], 'L0_ffn_k_scale': _L0_ffn_in['k_scale'], 'L0_ffn_Wo': _L0_ffn_in['Wo'], 'L0_ffn_ln_g': _L0_ffn_in['ln_g'], 'L0_ffn_ln_b': _L0_ffn_in['ln_b'], 'L0_ffn_W1': _L0_ffn_in['W1'], 'L0_ffn_b1': _L0_ffn_in['b1'], 'L0_ffn_W2': _L0_ffn_in['W2'], 'L0_ffn_b2': _L0_ffn_in['b2'], 'L1_attn_w_kv_down': _L1_attn_in['w_kv_down'], 'L1_attn_w_kv_up': _L1_attn_in['w_kv_up'], 'L1_attn_w_q': _L1_attn_in['w_q'], 'L1_attn_w_out': _L1_attn_in['w_out'], 'L1_ffn_r1_w': _L1_ffn_in['r1_w'], 'L1_ffn_r1_b': _L1_ffn_in['r1_b'], 'L1_ffn_r2_w': _L1_ffn_in['r2_w'], 'L1_ffn_w_up': _L1_ffn_in['w_up'], 'L1_ffn_w_down': _L1_ffn_in['w_down'], 'L1_ffn_a_up': _L1_ffn_in['a_up'], 'L1_ffn_a_down': _L1_ffn_in['a_down']}
    _x0 = _d['L0_attn_x']
    _d['L0_attn_x'] = jax.random.normal(jax.random.fold_in(jax.random.key(seed), 1), (8, 512, 128), dtype=_x0.dtype)
    del _x0
    return _d

def reference(L0_attn_x, L0_attn_w_q, L0_attn_w_k, L0_attn_w_v, L0_attn_g_q, L0_attn_g_k, L0_attn_w_o, L0_attn_b_o, L0_attn_gamma, L0_attn_beta, L0_ffn_Wqkv, L0_ffn_q_scale, L0_ffn_k_scale, L0_ffn_Wo, L0_ffn_ln_g, L0_ffn_ln_b, L0_ffn_W1, L0_ffn_b1, L0_ffn_W2, L0_ffn_b2, L1_attn_w_kv_down, L1_attn_w_kv_up, L1_attn_w_q, L1_attn_w_out, L1_ffn_r1_w, L1_ffn_r1_b, L1_ffn_r2_w, L1_ffn_w_up, L1_ffn_w_down, L1_ffn_a_up, L1_ffn_a_down):

    def _L0_attn_ref(x, w_q, w_k, w_v, g_q, g_k, w_o, b_o, gamma, beta):
        import jax, jax.numpy as jnp
        import numpy as np
        DIM = 128
        HEADS = 16
        HEAD_DIM = DIM // HEADS
        COLLAPSE_THRESHOLD = 0.27
        SHARPNESS = 15.0
        LN_EPS = 1e-05
        NORM_EPS = 1e-12

        def _layernorm(x, gamma, beta):
            mu = jnp.mean(x, axis=-1, keepdims=True)
            var = jnp.mean(jnp.square(x - mu), axis=-1, keepdims=True)
            return (x - mu) * jax.lax.rsqrt(var + LN_EPS) * gamma + beta

        def _l2_normalize(x):
            n = jnp.sqrt(jnp.sum(jnp.square(x), axis=-1, keepdims=True))
            return x / jnp.maximum(n, NORM_EPS)
        B, T, D = x.shape
        x_norm = _layernorm(x, gamma, beta)
        q = (x_norm @ w_q).reshape(B, T, HEADS, HEAD_DIM).transpose(0, 2, 1, 3)
        k = (x_norm @ w_k).reshape(B, T, HEADS, HEAD_DIM).transpose(0, 2, 1, 3)
        v = (x @ w_v).reshape(B, T, HEADS, HEAD_DIM).transpose(0, 2, 1, 3)
        q = _l2_normalize(q)
        k = _l2_normalize(k)
        align = jnp.einsum('bhqd,bhkd->bhqk', q, k)
        resonance = 0.5 + 0.5 * jnp.tanh((align - COLLAPSE_THRESHOLD) * SHARPNESS)
        gate_q = 0.25 + 0.75 * jax.nn.sigmoid(jnp.einsum('bhtd,d->bht', q, g_q))
        gate_k = 0.25 + 0.75 * jax.nn.sigmoid(jnp.einsum('bhtd,d->bht', k, g_k))
        modulation = resonance * gate_q[..., :, None] * gate_k[..., None, :]
        fused = jnp.einsum('bhqk,bhkd->bhqd', modulation, v)
        fused = fused.transpose(0, 2, 1, 3).reshape(B, T, HEADS * HEAD_DIM)
        return fused @ w_o + b_o

    def _L0_ffn_ref(x, Wqkv, q_scale, k_scale, Wo, ln_g, ln_b, W1, b1, W2, b2):
        import jax, jax.numpy as jnp
        import numpy as np
        DIM = 128
        DEPTH = 6
        HEADS = 16
        DIM_HEAD = 64
        WINDOW = 32
        INNER = HEADS * DIM_HEAD
        DIM_INNER = int(DIM * 4 * 2 / 3)
        QK_SCALE = 8.0

        def shift_tokens(t):
            a, s = jnp.split(t, 2, -1)
            s = jnp.pad(s, ((0, 0), (1, 0), (0, 0)))[:, :-1]
            return jnp.concatenate([a, s], -1)

        def l2norm(t):
            return t / jnp.maximum(jnp.linalg.norm(t, axis=-1, keepdims=True), 1e-12)

        def rotate_half(x):
            x1, x2 = jnp.split(x, 2, -1)
            return jnp.concatenate([-x2, x1], -1)

        def rotary_tables(n):
            half = jnp.arange(0, DIM_HEAD, 2, dtype=jnp.float32)
            inv_freq = 1.0 / 10000.0 ** (half / DIM_HEAD)
            t = jnp.arange(n, dtype=jnp.float32)
            freqs = t[:, None] * inv_freq[None, :]
            freqs = jnp.concatenate([freqs, freqs], -1)
            base_scale = (half + 0.4 * DIM_HEAD) / (1.4 * DIM_HEAD)
            power = (t - n // 2) / (WINDOW // 2)
            scale = base_scale[None, :] ** power[:, None]
            scale = jnp.concatenate([scale, scale], -1)
            return (freqs, scale)

        def local_attention(q, k, v):
            b, h, n, d = q.shape
            w = WINDOW
            nw = n // w
            bq = q.reshape(b, h, nw, w, d)
            bk = k.reshape(b, h, nw, w, d)
            bv = v.reshape(b, h, nw, w, d)

            def look(t):
                p = jnp.pad(t, ((0, 0), (0, 0), (1, 0), (0, 0), (0, 0)))
                return jnp.concatenate([p[:, :, :nw], p[:, :, 1:]], axis=3)
            bk2, bv2 = (look(bk), look(bv))
            seq = jnp.arange(n).reshape(nw, w)
            seq_p = jnp.pad(seq, ((1, 0), (0, 0)), constant_values=-1)
            jt = jnp.concatenate([seq_p[:nw], seq_p[1:]], axis=1)
            it = seq[:, :, None]
            jb = jt[:, None, :]
            mask = (it < jb) | (it > jb + w) | (jb == -1)
            sim = jnp.einsum('bhwie,bhwje->bhwij', bq, bk2) * QK_SCALE
            sim = jnp.where(mask, -jnp.finfo(sim.dtype).max, sim)
            attn = jax.nn.softmax(sim, -1)
            out = jnp.einsum('bhwij,bhwje->bhwie', attn, bv2)
            return out.reshape(b, h, n, d)

        def attn_layer(x, Wqkv, qs, ksc, Wo):
            b, n, _ = x.shape
            qkv = x @ Wqkv
            q, k, v = jnp.split(qkv, 3, -1)
            sh = lambda t: t.reshape(b, n, HEADS, DIM_HEAD).transpose(0, 2, 1, 3)
            q, k, v = (sh(q), sh(k), sh(v))
            q = l2norm(q) * qs
            k = l2norm(k) * ksc
            freqs, scale = rotary_tables(n)
            cos, sin = (jnp.cos(freqs), jnp.sin(freqs))
            q = q * cos * scale + rotate_half(q) * sin * scale
            inv = 1.0 / scale
            k = k * cos * inv + rotate_half(k) * sin * inv
            out = local_attention(q, k, v)
            out = out.transpose(0, 2, 1, 3).reshape(b, n, INNER)
            return out @ Wo

        def ffn_layer(x, g, bln, W1, b1, W2, b2):
            mu = x.mean(-1, keepdims=True)
            var = ((x - mu) ** 2).mean(-1, keepdims=True)
            xn = (x - mu) / jnp.sqrt(var + 1e-05) * g + bln
            hg = xn @ W1 + b1
            a, gate = jnp.split(hg, 2, -1)
            return a * jax.nn.gelu(gate, approximate=False) @ W2 + b2
        for i in range(DEPTH):
            x = attn_layer(shift_tokens(x), Wqkv[i], q_scale[i], k_scale[i], Wo[i]) + x
            x = ffn_layer(shift_tokens(x), ln_g[i], ln_b[i], W1[i], b1[i], W2[i], b2[i]) + x
        return x

    def _L1_attn_ref(x, w_kv_down, w_kv_up, w_q, w_out):
        import jax, jax.numpy as jnp
        import numpy as np
        B, T, C = (64, 32, 128)
        N_HEAD, HEAD_SIZE, KV_RANK = (16, 64, 128)
        BLOCK_SIZE = 32
        Bx, Tx, Cx = x.shape
        HD = N_HEAD * HEAD_SIZE
        latent_kv = x @ w_kv_down
        kv = latent_kv @ w_kv_up
        k, v = (kv[..., :HD], kv[..., HD:])
        k = k.reshape(Bx, Tx, N_HEAD, HEAD_SIZE)
        v = v.reshape(Bx, Tx, N_HEAD, HEAD_SIZE)
        q = (x @ w_q).reshape(Bx, Tx, N_HEAD, HEAD_SIZE)
        scale = HEAD_SIZE ** (-0.5)
        att = jnp.einsum('bqhd,bkhd->bhqk', q, k) * scale
        causal = jnp.tril(jnp.ones((Tx, Tx), dtype=bool))
        att = jnp.where(causal, att, -jnp.inf)
        att = jax.nn.softmax(att, axis=-1)
        y = jnp.einsum('bhqk,bkhd->bqhd', att, v)
        y = y.reshape(Bx, Tx, HD)
        return y @ w_out

    def _L1_ffn_ref(x, r1_w, r1_b, r2_w, w_up, w_down, a_up, a_down):
        import jax, jax.numpy as jnp
        import numpy as np
        E, G, TOPK = (32, 16, 2)
        HID, INTER, A_INTER = (128, 256, 128)
        CAP_FACTOR = 1.25
        SCALE = 0.05

        def _stats(x):
            mean = x.mean(-1, keepdims=True)
            std = jnp.std(x, axis=-1, keepdims=True, ddof=1)
            mn = x.min(-1, keepdims=True)
            mx = x.max(-1, keepdims=True)
            l2 = jnp.linalg.norm(x, axis=-1, keepdims=True)
            sp = (jnp.abs(x) < 1e-06).astype(x.dtype).mean(-1, keepdims=True)
            return jnp.concatenate([mean, std, mn, mx, l2, sp], -1)
        B, N, C = x.shape
        xf = x.reshape(-1, C)
        T = xf.shape[0]
        cap = int(CAP_FACTOR * T / E)
        ri = jnp.concatenate([xf, _stats(xf)], -1)
        h = jax.nn.gelu(ri @ r1_w.T + r1_b, approximate=False)
        probs = jax.nn.softmax(h @ r2_w.T, -1)
        topp, topi = jax.lax.top_k(probs, TOPK)
        wnorm = topp / topp.sum(-1, keepdims=True)
        eids = jnp.arange(E)
        hit = topi[..., None] == eids
        routed = hit.any(1)
        Wc = jnp.where(hit, wnorm[..., None], 0.0).sum(1)
        score = jnp.where(routed, probs, -jnp.inf)
        idx = jnp.argsort(-score, axis=0)[:cap].T
        valid = jnp.take_along_axis(routed.T, idx, 1)
        w = jnp.take_along_axis(Wc.T, idx, 1) * valid
        xe = xf[idx]
        up = jnp.einsum('eci,eji->ecj', xe, w_up)
        gate, upv = jnp.split(up, 2, axis=-1)
        hact = jax.nn.silu(gate) * upv
        ye = jnp.einsum('ecj,eoj->eco', hact, w_down)
        out = jnp.zeros((T, C), xf.dtype).at[idx.reshape(-1)].add((w[..., None] * ye).reshape(-1, C))
        Wmask = jnp.zeros((T, E), xf.dtype).at[idx, eids[:, None]].add(w)
        gw = SCALE * Wmask.reshape(T, G, E // G).sum(-1)
        aup = jnp.einsum('tc,gjc->tgj', xf, a_up)
        ag, av = jnp.split(aup, 2, axis=-1)
        ah = jax.nn.silu(ag) * av
        ay = jnp.einsum('tgj,goj->tgo', ah, a_down)
        out = out + jnp.einsum('tg,tgo->to', gw, ay)
        return out.reshape(B, N, C)
    x = L0_attn_x
    xn = _layernorm(x, axis=-1)
    x = x + _L0_attn_ref(xn, L0_attn_w_q, L0_attn_w_k, L0_attn_w_v, L0_attn_g_q, L0_attn_g_k, L0_attn_w_o, L0_attn_b_o, L0_attn_gamma, L0_attn_beta) + _L0_ffn_ref(xn, L0_ffn_Wqkv, L0_ffn_q_scale, L0_ffn_k_scale, L0_ffn_Wo, L0_ffn_ln_g, L0_ffn_ln_b, L0_ffn_W1, L0_ffn_b1, L0_ffn_W2, L0_ffn_b2)
    xn = _layernorm(x, axis=-1)
    x = x + _L1_attn_ref(xn, L1_attn_w_kv_down, L1_attn_w_kv_up, L1_attn_w_q, L1_attn_w_out) + _L1_ffn_ref(xn, L1_ffn_r1_w, L1_ffn_r1_b, L1_ffn_r2_w, L1_ffn_w_up, L1_ffn_w_down, L1_ffn_a_up, L1_ffn_a_down)
    return x

_drawn_inputs = setup_inputs


def setup_inputs(seed=0):
    import zlib

    import numpy as np

    out = dict(_drawn_inputs(seed))
    spreads = {'L0_attn_b_o': (0.0, 2.0),
     'L0_attn_gamma': (1.0, 0.6),
     'L0_attn_beta': (0.0, 0.8),
     'L0_ffn_q_scale': (1.0, 0.6),
     'L0_ffn_k_scale': (1.0, 0.6),
     'L0_ffn_ln_g': (1.0, 0.6),
     'L0_ffn_ln_b': (0.0, 0.8),
     'L0_ffn_b1': (0.0, 0.8),
     'L0_ffn_b2': (0.0, 0.423),
     'L1_ffn_r1_b': (0.0, 2.0)}
    factors = {'L0_ffn_Wqkv': 3.727,
     'L0_ffn_Wo': 3.776,
     'L0_ffn_W1': 8.0,
     'L0_ffn_W2': 8.0,
     'L1_attn_w_kv_down': 6.166,
     'L1_attn_w_kv_up': 5.925,
     'L1_attn_w_q': 8.0,
     'L1_attn_w_out': 5.824,
     'L1_ffn_r1_w': 64.0,
     'L1_ffn_r2_w': 64.0,
     'L1_ffn_w_up': 64.0,
     'L1_ffn_w_down': 64.0,
     'L1_ffn_a_up': 64.0,
     'L1_ffn_a_down': 64.0,
     'L0_attn_w_q': 4.519,
     'L0_attn_w_k': 4.287,
     'L0_attn_w_v': 4.3,
     'L0_attn_g_q': 8.0,
     'L0_attn_g_k': 8.0,
     'L0_attn_w_o': 4.283}
    for name, (base, spread) in spreads.items():
        noise = np.random.default_rng([zlib.crc32(name.encode()), seed]).standard_normal(out[name].shape)
        drawn = base * np.exp(spread * noise) if base else spread * noise
        out[name] = jnp.asarray(drawn.astype(out[name].dtype))
    for name, factor in factors.items():
        out[name] = (out[name] * factor).astype(out[name].dtype)
    return out
```

```python
from contextlib import ExitStack, contextmanager

import concourse.bass as bass
from concourse import mybir

F32 = mybir.dt.float32
BF16 = mybir.dt.bfloat16
U32 = mybir.dt.uint32
ALU = mybir.AluOpType
ACT = mybir.ActivationFunctionType
AX = mybir.AxisListType

P = 128
D = 128
B, T = 8, 512
N = B * T
NT = N // P
LN_EPS = 1e-5
NORM_MAX = 1e12
MASKED = -1e30

H0, HD0 = 16, 8
KT = T // P
SHARP, COLLAPSE = 15.0, 0.27

DEPTH, HL, HDL, WIN = 6, 16, 64, 32
INNER = HL * HDL
QK_SCALE = 8.0
DIN = int(D * 4 * 2 / 3)
QW = P - WIN
QT = [QW] * (T // QW) + ([T % QW] if T % QW else [])
NQ = len(QT)
G4 = HL // 4
FK = [P, P, DIN - 2 * P]

H1, HD1 = 16, 64
R1 = 128
HDT = H1 * HD1

E, TOPK, INTER, AINT = 32, 2, 256, 128
GRP = 16
CAP = int(1.25 * N / E)
SLOTS = E * CAP
RH = D // 2
NSTAT = 6
ADAPT = 0.05


class Memory:
    pass


@contextmanager
def stage(nc, label, *names):
    with ExitStack() as ctx:
        sems = {n: ctx.enter_context(nc.semaphore(f"{label}_{n}")) for n in names}
        with nc.Block() as block:
            yield block, sems
        for s in sems.values():
            nc.gpsimd.sem_clear(s)
        nc.all_engine_barrier()


def load_constants(nc, m, d):
    loads = [
        (m.ident, d["c_ident"]), (m.bones8, d["c_bones8"]), (m.bones64, d["c_bones64"]), (m.hmask, d["c_hmask"]),
        (m.mcausal_f, d["c_causal"]), (m.mlocal_f, d["c_local"]),
        (m.w_q0, d["L0_attn_w_q"]), (m.w_k0, d["L0_attn_w_k"]), (m.w_v0, d["L0_attn_w_v"]), (m.w_o0, d["L0_attn_w_o"]),
        (m.g_q0, d["p_g_q"]), (m.g_k0, d["p_g_k"]), (m.b_o0, d["p_b_o"]), (m.gamma0, d["p_gamma"]), (m.beta0, d["p_beta"]),
    ]
    with stage(nc, "const", "loaded", "set", "done") as (block, s):
        @block.sync
        def _(sp):
            for dst, src in loads:
                sp.dma_start(dst, src).then_inc(s["loaded"], 16)

        @block.vector
        def _(dve):
            dve.memset(m.onesm, 1.0 / D)
            dve.memset(m.ones, 1.0)
            dve.memset(m.eps, LN_EPS)
            dve.memset(m.zcol, 0.0)
            dve.memset(m.tbias, -SHARP * COLLAPSE)
            dve.memset(m.vbd, 0.0).then_inc(s["set"], 1)
            dve.wait_ge(s["loaded"], 16 * len(loads))
            dve.tensor_copy(m.ident16, m.ident)
            dve.tensor_copy(m.mcausal, m.mcausal_f)
            dve.tensor_copy(m.mlocal, m.mlocal_f)
            dve.tensor_scalar(m.gq_blk, m.bones8, m.g_q0, None, ALU.mult)
            dve.tensor_scalar(m.gk_blk, m.bones8, m.g_k0, None, ALU.mult).then_inc(s["done"], 1)


def load_x(nc, m, d):
    with stage(nc, "loadx", "loaded", "turned", "kept") as (block, s):
        x_v = d["x"].rearrange("b (t p) d -> b p t d", p=P)

        @block.sync
        def _(sp):
            for b in range(B):
                sp.dma_start(m.xrow[:, b * KT:(b + 1) * KT, :], x_v[b]).then_inc(s["loaded"], 16)

        @block.tensor
        def _(pe):
            for b in range(B):
                pe.wait_ge(s["loaded"], 16 * B if b else 16 * B)
                if b >= 4:
                    pe.wait_ge(s["kept"], b - 3)
                for t in range(KT):
                    mm = pe.transpose(m.ps[b % 4][:, t * P:(t + 1) * P], m.xrow[:, b * KT + t, :], m.ident)
                mm.then_inc(s["turned"], 1)

        @block.vector
        def _(dve):
            for b in range(B):
                dve.wait_ge(s["turned"], b + 1)
                dve.tensor_copy(m.xsum[:, b * T:(b + 1) * T], m.ps[b % 4][:, :]).then_inc(s["kept"], 1)


def layer_norm_all(nc, m, src, dst, gamma=None, beta=None, add=None, label="ln"):
    with stage(nc, label, "summed", "mean", "xc", "sq", "var", "sd", "rs", "out") as (block, s):
        cs = [slice(c * T, (c + 1) * T) for c in range(B)]

        @block.tensor
        def _(pe):
            def var(c):
                pe.wait_ge(s["sq"], c + 1)
                if c >= 2:
                    pe.wait_ge(s["sd"], c - 1)
                pe.matmul(m.ps[2 + c % 2][:, :], m.onesm, m.sq[:, c % 2, :], start=True, stop=True).then_inc(s["var"], 1)

            for c in range(B):
                if add is not None:
                    pe.wait_ge(s["summed"], c + 1)
                if c >= 2:
                    pe.wait_ge(s["xc"], c - 1)
                pe.matmul(m.ps[c % 2][:, :], m.onesm, src[:, cs[c]], start=True, stop=True).then_inc(s["mean"], 1)
                if c:
                    var(c - 1)
            var(B - 1)

        @block.scalar
        def _(act):
            for c in range(B):
                act.wait_ge(s["xc"], c + 1)
                if c >= 2:
                    act.wait_ge(s["var"], c - 1)
                act.activation(m.sq[:, c % 2, :], m.xc[:, c % 2, :], ACT.Square).then_inc(s["sq"], 1)
                act.wait_ge(s["var"], c + 1)
                if c >= 2:
                    act.wait_ge(s["rs"], c - 1)
                act.activation(m.sd[:, c % 2, :], m.ps[2 + c % 2][:, :], ACT.Sqrt, bias=m.eps).then_inc(s["sd"], 1)

        @block.vector
        def _(dve):
            def finish(c):
                dve.wait_ge(s["sd"], c + 1)
                dve.reciprocal(m.rs[:, c % 2, :], m.sd[:, c % 2, :]).then_inc(s["rs"], 1)
                dve.wait_ge(s["rs"], c + 1)
                dve.tensor_tensor(dst[:, cs[c]], m.xc[:, c % 2, :], m.rs[:, c % 2, :], ALU.mult).then_inc(s["out"], 1)
                if gamma is not None:
                    dve.wait_ge(s["out"], 2 * c + 1)
                    dve.tensor_scalar(dst[:, cs[c]], dst[:, cs[c]], gamma, beta, ALU.mult, ALU.add).then_inc(s["out"], 1)

            if add is not None:
                for c in range(B):
                    dve.tensor_tensor(src[:, cs[c]], src[:, cs[c]], add[:, cs[c]], ALU.add).then_inc(s["summed"], 1)
                dve.wait_ge(s["summed"], B)
            for c in range(B):
                dve.wait_ge(s["mean"], c + 1)
                if c >= 2:
                    dve.wait_ge(s["out"], (c - 1) * (1 if gamma is None else 2))
                dve.tensor_tensor(m.xc[:, c % 2, :], src[:, cs[c]], m.ps[c % 2][:, :], ALU.subtract).then_inc(s["xc"], 1)
                if c:
                    finish(c - 1)
            finish(B - 1)


def resonance_attention(nc, m, b):
    here = bass.ds(b * T, T)
    pairs = [(h, u) for h in range(H0) for u in range(2)]
    NI = len(pairs)
    with stage(nc, "res", "xin", "proj", "sq", "ss", "nrm", "rn", "unit", "gate", "th", "g", "vp", "vbd",
               "km", "score", "tanh", "pv", "fused", "wo", "out") as (block, s):
        q_ps, k_ps, v_ps, ssq, ssk, gq_ps, gk_ps, acc = (m.ps[i] for i in range(8))

        @block.vector
        def _(dve):
            dve.tensor_copy(m.xq_b, m.xq[:, here]).then_inc(s["xin"], 1)
            dve.tensor_copy(m.xn_b, m.xn[:, here]).then_inc(s["xin"], 1)
            for i, (ps, unit) in enumerate(((q_ps, m.qh), (k_ps, m.kh))):
                dve.wait_ge(s["nrm"], i + 1)
                dve.reciprocal(m.rs[:, i, :], m.sd[:, i, :]).then_inc(s["rn"], 1)
                dve.wait_ge(s["rn"], i + 1)
                dve.scalar_tensor_tensor(out=unit, in0=m.rs[:, i, :], scalar=NORM_MAX, in1=ps[:, :],
                                         op0=ALU.min, op1=ALU.mult).then_inc(s["unit"], 1)
            dve.wait_ge(s["th"], 2)
            dve.tensor_scalar(m.gateq, m.xc[:, 0, :], 0.375, 0.625, ALU.mult, ALU.add).then_inc(s["g"], 1)
            dve.tensor_scalar(m.gatek, m.xc[:, 1, :], 0.1875, 0.3125, ALU.mult, ALU.add).then_inc(s["g"], 1)
            dve.wait_ge(s["g"], 2)
            dve.tensor_tensor(m.vp, v_ps[:, :], m.gatek, ALU.mult).then_inc(s["vp"], 1)
            dve.wait_ge(s["vp"], 1)
            for kt in range(KT):
                blocks = m.vbd[:, kt, :].rearrange("p (h c) -> p h c", c=P + HD0)[:, :, 0:HD0]
                dve.tensor_copy(blocks, m.vp[:, kt * P:(kt + 1) * P].rearrange("p (h c) -> p h c", c=HD0))\
                   .then_inc(s["vbd"], 1)
            for h in range(H0):
                if h >= 3:
                    dve.wait_ge(s["score"], 2 * (h - 2))
                dve.tensor_scalar(m.km[:, h % 3, :], m.kh, m.hmask[:, h:h + 1], None, ALU.mult).then_inc(s["km"], 1)
            dve.wait_ge(s["pv"], NI + 1)
            dve.tensor_tensor(m.fused, acc[:, :], m.gateq, ALU.mult).then_inc(s["fused"], 1)
            dve.wait_ge(s["wo"], 1)
            dve.scalar_tensor_tensor(out=m.xsum[:, here], in0=q_ps[:, :], scalar=m.b_o0, in1=m.xsum[:, here],
                                     op0=ALU.add, op1=ALU.add).then_inc(s["out"], 1)

        @block.scalar
        def _(act):
            for i, ps in enumerate((q_ps, k_ps)):
                act.wait_ge(s["proj"], i + 1)
                act.activation(m.sq[:, i, :], ps[:, :], ACT.Square).then_inc(s["sq"], 1)
            for i, ps in enumerate((ssq, ssk)):
                act.wait_ge(s["ss"], i + 1)
                act.activation(m.sd[:, i, :], ps[:, :], ACT.Sqrt, bias=m.zcol).then_inc(s["nrm"], 1)
            for i, ps in enumerate((gq_ps, gk_ps)):
                act.wait_ge(s["gate"], i + 1)
                act.activation(m.xc[:, i, :], ps[:, :], ACT.Tanh, scale=0.5).then_inc(s["th"], 1)
            for i in range(NI):
                act.wait_ge(s["score"], i + 1)
                if i >= 3:
                    act.wait_ge(s["pv"], i - 2)
                act.activation(m.tanh[:, i % 3, :, :], m.ps2[i % 3][:, :, :], ACT.Tanh, bias=m.tbias, scale=SHARP)\
                   .then_inc(s["tanh"], 1)

        @block.tensor
        def _(pe):
            pe.wait_ge(s["xin"], 2)
            pe.matmul(q_ps[:, :], m.w_q0, m.xq_b, start=True, stop=True).then_inc(s["proj"], 1)
            pe.matmul(k_ps[:, :], m.w_k0, m.xq_b, start=True, stop=True).then_inc(s["proj"], 1)
            for kt in range(KT):
                mm = pe.matmul(v_ps[:, kt * P:(kt + 1) * P], m.xn_b[:, kt * P:(kt + 1) * P], m.w_v0,
                               start=True, stop=True)
            mm.then_inc(s["proj"], 1)
            for i, ps in enumerate((ssq, ssk)):
                pe.wait_ge(s["sq"], i + 1)
                pe.matmul(ps[:, :], m.bones8, m.sq[:, i, :], start=True, stop=True).then_inc(s["ss"], 1)
            pe.wait_ge(s["unit"], 1)
            pe.matmul(gq_ps[:, :], m.gq_blk, m.qh, start=True, stop=True).then_inc(s["gate"], 1)
            pe.wait_ge(s["unit"], 2)
            for kt in range(KT):
                mm = pe.matmul(gk_ps[:, kt * P:(kt + 1) * P], m.kh[:, kt * P:(kt + 1) * P], m.gk_blk,
                               start=True, stop=True)
            mm.then_inc(s["gate"], 1)
            pe.wait_ge(s["vp"], 1)
            for kt in range(KT):
                mm = pe.matmul(acc[:, :], m.vp[:, kt * P:(kt + 1) * P], m.ones, start=(kt == 0), stop=False,
                               skip_group_check=True)
            mm.then_inc(s["pv"], 1)
            pe.wait_ge(s["th"], 2)

            def scores(i):
                h, u = pairs[i]
                pe.wait_ge(s["km"], h + 1)
                if i >= 3:
                    pe.wait_ge(s["tanh"], i - 2)
                for j in range(2):
                    kt = 2 * u + j
                    mm = pe.matmul(m.ps2[i % 3][:, j, :], m.km[:, h % 3, kt * P:(kt + 1) * P], m.qh,
                                   start=True, stop=True)
                mm.then_inc(s["score"], 1)

            def values(i):
                h, u = pairs[i]
                pe.wait_ge(s["tanh"], i + 1)
                pe.wait_ge(s["vbd"], KT)
                for j in range(2):
                    mm = pe.matmul(acc[:, :], m.vbd[:, 2 * u + j, h * P:(h + 1) * P], m.tanh[:, i % 3, j, :],
                                   start=False, stop=(i == NI - 1 and j == 1), skip_group_check=True)
                mm.then_inc(s["pv"], 1)

            for i in range(NI + 2):
                if i < NI:
                    scores(i)
                if i >= 2:
                    values(i - 2)
            pe.wait_ge(s["fused"], 1)
            pe.matmul(q_ps[:, :], m.w_o0, m.fused, start=True, stop=True).then_inc(s["wo"], 1)


def load_layer(nc, m, d, layer):
    with stage(nc, "layer", "loaded", "made") as (block, s):
        loads = [
            (m.wqkv, d["L0_ffn_Wqkv"][layer, :, :]),
            (m.wo, d["L0_ffn_Wo"][layer, :, :].rearrange("(k p) d -> p k d", p=P)),
            (m.w1, d["L0_ffn_W1"][layer, :, :]),
            (m.w2, d["p_W2"][layer, :, :].rearrange("(k p) d -> p k d", p=P)),
            (m.b1, d["p_b1"][layer, :, :]), (m.lnp, d["p_lnp"][layer, :, :]), (m.qks, d["p_qks"][layer, :, :]),
        ]

        @block.sync
        def _(sp):
            for dst, src in loads:
                sp.dma_start(dst, src).then_inc(s["loaded"], 16)

        @block.vector
        def _(dve):
            dve.wait_ge(s["loaded"], 16 * len(loads))
            for i in range(4):
                dve.tensor_scalar(m.rot[:, i, :], m.rot0[:, i, :], m.qks[:, i:i + 1], QK_SCALE if i < 2 else 1.0,
                                  ALU.mult, ALU.mult)
            src = m.wqkv[:, 0:2 * INNER].rearrange("p (h a c) -> p h a c", a=2, c=HDL // 2)
            dst = m.wrot.rearrange("p (h a c) -> p h a c", a=2, c=HDL // 2)
            dve.tensor_copy(dst[:, :, 0, :], src[:, :, 1, :])
            dve.tensor_copy(dst[:, :, 1, :], src[:, :, 0, :]).then_inc(s["made"], 1)


def local_attention(nc, m, b):
    here = bass.ds(b * T, T)
    half = D // 2
    NU = 2 * (HL // 2)
    items = [(j, g) for j in range(NQ) for g in range(G4)]
    NI = len(items)
    with stage(nc, "loc", "xs", "v", "vev", "a", "r", "sq", "ss", "sd", "t1", "t2", "sum", "rn", "unit",
               "score", "nm", "exp", "turn", "pt", "pv", "ri", "norm", "at", "atev", "wo", "out") as (block, s):
        a_ps, r_ps, n_ps, v_ps = m.ps[0:2], m.ps[2:4], m.ps[4:6], m.ps[6:8]
        s_ps, pt_ps, pv_ps, at_ps = m.ps2[0:2], m.ps[4:6], m.ps[6], m.ps[7]
        NV = 2 * NQ

        def keys(j):
            return QT[j] + WIN

        @block.vector
        def _(dve):
            dve.tensor_copy(m.xs[0:half, WIN:], m.xn[0:half, here]).then_inc(s["xs"], 1)
            dve.tensor_copy(m.xs[half:D, WIN + 1:], m.xn[half:D, bass.ds(b * T, T - 1)]).then_inc(s["xs"], 1)

            def unit(n):
                p, z = n // 2, n % 2
                dst = m.qr[:, p, :] if z == 0 else m.kr[:, p, WIN:]
                dve.wait_ge(s["sd"], n + 1)
                dve.reciprocal(m.rs[:, n % 2, :], m.sd[:, n % 2, :]).then_inc(s["rn"], 1)
                dve.wait_ge(s["rn"], n + 1)
                dve.wait_ge(s["sum"], n + 1)
                dve.scalar_tensor_tensor(out=dst, in0=m.rs[:, n % 2, :], scalar=NORM_MAX, in1=m.t3[:, n % 2, :],
                                         op0=ALU.min, op1=ALU.mult).then_inc(s["unit"], 1)

            for n in range(NU):
                z = n % 2
                if n >= 2:
                    dve.wait_ge(s["sum"], n - 1)
                dve.wait_ge(s["r"], n + 1)
                dve.tensor_tensor(m.t2[:, n % 2, :], r_ps[n % 2][:, :], m.rot[:, 2 * z + 1, :], ALU.mult)\
                   .then_inc(s["t2"], 1)
                dve.wait_ge(s["sq"], n + 1)
                dve.tensor_tensor(m.t1[:, n % 2, :], a_ps[n % 2][:, :], m.rot[:, 2 * z, :], ALU.mult).then_inc(s["t1"], 1)
                if n:
                    unit(n - 1)
            unit(NU - 1)

            def negmax(i):
                j, g = items[i]
                q, k = QT[j], keys(j)
                dve.wait_ge(s["score"], i + 1)
                if i >= 2:
                    dve.wait_ge(s["exp"], i - 1)
                dve.tensor_reduce(m.nm[0:q, i % 2, :], s_ps[i % 2][0:q, :, 0:2 * k].rearrange("p a (h k) -> p a h k", h=2),
                                  AX.X, ALU.max, negate=True).then_inc(s["nm"], 1)

            def probs_t(i):
                j, g = items[i]
                q, k = QT[j], keys(j)
                dve.wait_ge(s["turn"], i + 1)
                if i >= 2:
                    dve.wait_ge(s["pv"], i - 1)
                dve.tensor_copy(m.pt[0:k, i % 2, 0:4 * q], pt_ps[i % 2][0:k, 0:4 * q]).then_inc(s["pt"], 1)

            def normed(i):
                j, g = items[i]
                q = QT[j]
                pv = pv_ps[0:q, 0:4 * (HDL + 1)].rearrange("p (h c) -> p h c", h=4)
                dve.wait_ge(s["pv"], i + 1)
                dve.reciprocal(m.ri[0:q, i % 2, :], pv[:, :, HDL]).then_inc(s["ri"], 1)
                dve.wait_ge(s["ri"], i + 1)
                if g == 0 and j >= 2:
                    dve.wait_ge(s["at"], 2 * (j - 1))
                dve.tensor_tensor(m.an[0:q, j % 2, g * 4 * HDL:(g + 1) * 4 * HDL].rearrange("p (h c) -> p h c", h=4),
                                  pv[:, :, 0:HDL], m.ri[0:q, i % 2, :].unsqueeze(2).to_broadcast([q, 4, HDL]),
                                  ALU.mult).then_inc(s["norm"], 1)

            for i in range(NI + 2):
                if i < NI:
                    negmax(i)
                if 1 <= i <= NI:
                    probs_t(i - 1)
                if i >= 2:
                    normed(i - 2)
            dve.wait_ge(s["wo"], 1)
            dve.tensor_tensor(m.xn[:, here], m.ps[0], m.xn[:, here], ALU.add).then_inc(s["out"], 1)

        @block.gpsimd
        def _(pool):
            for n in range(NU):
                pool.wait_ge(s["t2"], n + 1)
                pool.wait_ge(s["t1"], n + 1)
                if n >= 2:
                    pool.wait_ge(s["unit"], n - 1)
                pool.tensor_tensor(m.t3[:, n % 2, :], m.t1[:, n % 2, :], m.t2[:, n % 2, :], ALU.add).then_inc(s["sum"], 1)

        @block.scalar
        def _(act):
            def v_rows(i):
                j, c = i // 2, i % 2
                act.wait_ge(s["v"], i + 1)
                k = keys(j)
                act.activation(m.v[0:k, j, 8 * c:8 * c + 8, 0:HDL],
                               v_ps[i % 2][0:k, :].rearrange("p (h c) -> p h c", h=8), ACT.Copy).then_inc(s["vev"], 1)

            def root(n):
                act.wait_ge(s["ss"], n + 1)
                if n >= 2:
                    act.wait_ge(s["rn"], n - 1)
                act.activation(m.sd[:, n % 2, :], n_ps[n % 2][:, :], ACT.Sqrt, bias=m.zcol).then_inc(s["sd"], 1)

            for n in range(NU):
                act.wait_ge(s["a"], n + 1)
                if n >= 2:
                    act.wait_ge(s["ss"], n - 1)
                act.activation(m.sq[:, n % 2, :], a_ps[n % 2][:, :], ACT.Square).then_inc(s["sq"], 1)
                if n < NV:
                    v_rows(n)
                if n:
                    root(n - 1)
            root(NU - 1)

            def turned_rows(j):
                q = QT[j]
                for c in range(2):
                    act.wait_ge(s["at"], 2 * j + c + 1)
                    act.activation(m.attnT[:, 4 * c:4 * c + 4, QW * j:QW * j + q],
                                   at_ps[:, 0:4 * q].rearrange("p (k q) -> p k q", k=4), ACT.Copy)\
                       .then_inc(s["atev"], 1)

            for i, (j, g) in enumerate(items):
                q, k = QT[j], keys(j)
                act.wait_ge(s["nm"], i + 1)
                if i >= 2:
                    act.wait_ge(s["turn"], i - 1)
                for h in range(4):
                    last = act.activation(m.pr[0:q, i % 2, h * k:(h + 1) * k], s_ps[i % 2][0:q, h // 2, h % 2 * k:(h % 2 + 1) * k],
                                          ACT.Exp, bias=m.nm[0:q, i % 2, h:h + 1])
                last.then_inc(s["exp"], 1)
                if i % 4 == 2 and i > 2:
                    turned_rows((i - 6) // 4)
            turned_rows(NQ - 1)

        @block.tensor
        def _(pe):
            def v_proj(i):
                j, c = i // 2, i % 2
                k = keys(j)
                if i >= 2:
                    pe.wait_ge(s["vev"], i - 1)
                pe.matmul(v_ps[i % 2][0:k, :], m.xs[:, QW * j:QW * j + k],
                          m.wqkv[:, 2 * INNER + 512 * c:2 * INNER + 512 * (c + 1)], start=True, stop=True)\
                  .then_inc(s["v"], 1)

            def sums(n):
                pe.wait_ge(s["sq"], n + 1)
                if n >= 2:
                    pe.wait_ge(s["sd"], n - 1)
                pe.matmul(n_ps[n % 2][:, :], m.bones64, m.sq[:, n % 2, :], start=True, stop=True).then_inc(s["ss"], 1)

            pe.wait_ge(s["xs"], 2)
            for n in range(NU):
                p, z = n // 2, n % 2
                col = z * INNER + p * P
                if n >= 2:
                    pe.wait_ge(s["t1"], n - 1)
                    pe.wait_ge(s["sq"], n - 1)
                pe.matmul(a_ps[n % 2][:, :], m.wqkv[:, col:col + P], m.xs[:, WIN:], start=True, stop=True)\
                  .then_inc(s["a"], 1)
                if n >= 2:
                    pe.wait_ge(s["t2"], n - 1)
                pe.matmul(r_ps[n % 2][:, :], m.wrot[:, col:col + P], m.xs[:, WIN:], start=True, stop=True)\
                  .then_inc(s["r"], 1)
                if n < NV:
                    v_proj(n)
                if n:
                    sums(n - 1)
            sums(NU - 1)

            def scores(i):
                j, g = items[i]
                q, k = QT[j], keys(j)
                if i == 0:
                    pe.wait_ge(s["unit"], NU)
                if i >= 2:
                    pe.wait_ge(s["exp"], i - 1)
                mask = m.mlocal[0:q, 0 if j == 0 else 1, :].rearrange("p (h k) -> p h k", h=2)[:, :, 0:k]
                for a in range(2):
                    pe.matmul(s_ps[i % 2][0:q, a, 0:2 * k], m.ident16[0:q, 0:q], mask, start=True, stop=False,
                              skip_group_check=True)
                for h in range(4):
                    p, r = 2 * g + h // 2, HDL * (h % 2)
                    mm = pe.matmul(s_ps[i % 2][0:q, h % 2, h // 2 * k:(h // 2 + 1) * k], m.qr[r:r + HDL, p, QW * j:QW * j + q],
                                   m.kr[r:r + HDL, p, QW * j:QW * j + k], start=False, stop=(h >= 2),
                                   skip_group_check=True)
                mm.then_inc(s["score"], 1)

            def turn(i):
                j, g = items[i]
                q, k = QT[j], keys(j)
                pe.wait_ge(s["exp"], i + 1)
                if i >= 2:
                    pe.wait_ge(s["pt"], i - 1)
                for h in range(4):
                    mm = pe.transpose(pt_ps[i % 2][0:k, h * q:(h + 1) * q], m.pr[0:q, i % 2, h * k:(h + 1) * k],
                                      m.ident[0:q, 0:q])
                mm.then_inc(s["turn"], 1)

            def values(i):
                j, g = items[i]
                q, k = QT[j], keys(j)
                pe.wait_ge(s["pt"], i + 1)
                if i == 0:
                    pe.wait_ge(s["vev"], NV)
                if i >= 1:
                    pe.wait_ge(s["norm"], i)
                for h in range(4):
                    slot = h % 2 * 2 + h // 2
                    mm = pe.matmul(pv_ps[0:q, h * (HDL + 1):(h + 1) * (HDL + 1)],
                                   m.pt[0:k, i % 2, slot * q:(slot + 1) * q], m.v[0:k, j, 4 * g + h, :],
                                   start=True, stop=True)
                mm.then_inc(s["pv"], 1)

            def turn_rows(j):
                q = QT[j]
                pe.wait_ge(s["norm"], 4 * j + 4)
                for c in range(2):
                    if j or c:
                        pe.wait_ge(s["atev"], 2 * j + c)
                    for k in range(4):
                        kp = 4 * c + k
                        mm = pe.transpose(at_ps[:, k * q:(k + 1) * q], m.an[0:q, j % 2, kp * P:(kp + 1) * P],
                                          m.ident[0:q, 0:q])
                    mm.then_inc(s["at"], 1)

            for i in range(NI + 2):
                if i < NI:
                    scores(i)
                if 1 <= i <= NI:
                    turn(i - 1)
                if i >= 2:
                    values(i - 2)
                if i % 4 == 2 and i > 2:
                    turn_rows((i - 6) // 4)
            turn_rows(NQ - 1)
            pe.wait_ge(s["atev"], 2 * NQ)
            for kp in range(HL // 2):
                mm = pe.matmul(m.ps[0], m.wo[:, kp, :], m.attnT[:, kp, :], start=(kp == 0),
                               stop=(kp == HL // 2 - 1))
            mm.then_inc(s["wo"], 1)


def feed_forward(nc, m):
    half = D // 2
    NK = len(FK)
    NU = B * NK
    with stage(nc, "ffn", "xs", "mean", "xc", "sq", "var", "sd", "rs", "ln", "g", "a", "ge", "h", "w2",
               "out") as (block, s):
        cs = [slice(c * T, (c + 1) * T) for c in range(B)]
        acc = m.ps[4:6]

        @block.tensor
        def _(pe):
            def var(c):
                pe.wait_ge(s["sq"], c + 1)
                if c >= 2:
                    pe.wait_ge(s["sd"], c - 1)
                pe.matmul(m.ps[2 + c % 2][:, :], m.onesm, m.sq[:, c % 2, :], start=True, stop=True).then_inc(s["var"], 1)

            for c in range(B):
                pe.wait_ge(s["xs"], 2 * c + 2)
                if c >= 2:
                    pe.wait_ge(s["xc"], c - 1)
                pe.matmul(m.ps[c % 2][:, :], m.onesm, m.xsh[:, c % 2, :], start=True, stop=True).then_inc(s["mean"], 1)
                if c:
                    var(c - 1)
            var(B - 1)

            def up(u):
                c, k = divmod(u, NK)
                f = FK[k]
                if k == 0:
                    pe.wait_ge(s["ln"], 2 * c + 2)
                if u == 0:
                    pe.wait_ge(s["xc"], B)
                    pe.wait_ge(s["sd"], B)
                if u >= 2:
                    pe.wait_ge(s["ge"], u - 1)
                pe.matmul(m.ps[u % 2][0:f, :], m.w1[:, DIN + k * P:DIN + k * P + f], m.xq[:, cs[c]],
                          start=True, stop=True).then_inc(s["g"], 1)
                if u >= 2:
                    pe.wait_ge(s["h"], u - 1)
                pe.matmul(m.ps[2 + u % 2][0:f, :], m.w1[:, k * P:k * P + f], m.xq[:, cs[c]],
                          start=True, stop=True).then_inc(s["a"], 1)

            def down(u):
                c, k = divmod(u, NK)
                f = FK[k]
                pe.wait_ge(s["h"], u + 1)
                if k == 0 and c >= 2:
                    pe.wait_ge(s["out"], c - 1)
                pe.matmul(acc[c % 2][:, :], m.w2[0:f, k, :], m.hid[0:f, u % 3, :], start=(k == 0),
                          stop=(k == NK - 1)).then_inc(s["w2"], 1)

            for u in range(NU + 2):
                if u < NU:
                    up(u)
                if u >= 2:
                    down(u - 2)

        @block.scalar
        def _(act):
            for c in range(B):
                act.wait_ge(s["xc"], c + 1)
                if c >= 2:
                    act.wait_ge(s["var"], c - 1)
                act.activation(m.sq[:, c % 2, :], m.xc[:, c % 2, :], ACT.Square).then_inc(s["sq"], 1)
                act.wait_ge(s["var"], c + 1)
                if c >= 2:
                    act.wait_ge(s["rs"], c - 1)
                act.activation(m.sd[:, c % 2, :], m.ps[2 + c % 2][:, :], ACT.Sqrt, bias=m.eps).then_inc(s["sd"], 1)
            for u in range(NU):
                k = u % NK
                f = FK[k]
                act.wait_ge(s["g"], u + 1)
                if u >= 2:
                    act.wait_ge(s["h"], u - 1)
                act.activation(m.ge[0:f, u % 2, :], m.ps[u % 2][0:f, :], ACT.Gelu, bias=m.b1[0:f, NK + k:NK + k + 1])\
                   .then_inc(s["ge"], 1)

        @block.vector
        def _(dve):
            def shifted(c):
                if c >= 2:
                    dve.wait_ge(s["xc"], c - 1)
                    dve.wait_ge(s["mean"], c - 1)
                dve.tensor_copy(m.xsh[0:half, c % 2, :], m.xn[0:half, cs[c]]).then_inc(s["xs"], 1)
                dve.tensor_copy(m.xsh[half:D, c % 2, 1:T], m.xn[half:D, c * T:(c + 1) * T - 1]).then_inc(s["xs"], 1)

            def finish(c):
                dve.wait_ge(s["sd"], c + 1)
                dve.reciprocal(m.rs[:, c % 2, :], m.sd[:, c % 2, :]).then_inc(s["rs"], 1)
                dve.wait_ge(s["rs"], c + 1)
                dve.tensor_tensor(m.xq[:, cs[c]], m.xc[:, c % 2, :], m.rs[:, c % 2, :], ALU.mult).then_inc(s["ln"], 1)
                dve.wait_ge(s["ln"], 2 * c + 1)
                dve.tensor_scalar(m.xq[:, cs[c]], m.xq[:, cs[c]], m.lnp[:, 0:1], m.lnp[:, 1:2], ALU.mult, ALU.add)\
                   .then_inc(s["ln"], 1)

            for c in range(B):
                shifted(c)
                dve.wait_ge(s["xs"], 2 * c + 2)
                dve.wait_ge(s["mean"], c + 1)
                if c >= 2:
                    dve.wait_ge(s["ln"], 2 * c - 2)
                    dve.wait_ge(s["sq"], c - 1)
                dve.tensor_tensor(m.xc[:, c % 2, :], m.xsh[:, c % 2, :], m.ps[c % 2][:, :], ALU.subtract)\
                   .then_inc(s["xc"], 1)
                if c:
                    finish(c - 1)
            finish(B - 1)

            def out(c):
                dve.wait_ge(s["w2"], NK * (c + 1))
                dve.scalar_tensor_tensor(out=m.xn[:, cs[c]], in0=acc[c % 2][:, :], scalar=m.lnp[:, 2:3],
                                         in1=m.xn[:, cs[c]], op0=ALU.add, op1=ALU.add).then_inc(s["out"], 1)

            for u in range(NU):
                c, k = divmod(u, NK)
                f = FK[k]
                dve.wait_ge(s["ge"], u + 1)
                dve.wait_ge(s["a"], u + 1)
                if u >= 3:
                    dve.wait_ge(s["w2"], u - 2)
                dve.scalar_tensor_tensor(out=m.hid[0:f, u % 3, :], in0=m.ps[2 + u % 2][0:f, :],
                                         scalar=m.b1[0:f, k:k + 1], in1=m.ge[0:f, u % 2, :],
                                         op0=ALU.add, op1=ALU.mult).then_inc(s["h"], 1)
                if k == 2 and c:
                    out(c - 1)
            out(B - 1)


def latent_attention(nc, m, b):
    here = bass.ds(b * T, T)
    NP_ = H1 // 2
    items = [(qt, h) for qt in range(KT) for h in range(H1)]
    NI = len(items)
    V0 = HDT
    with stage(nc, "lat", "xin", "lat", "latc", "v", "vev", "q", "qev", "k", "kev", "score", "nm", "exp", "turn",
               "pta", "ptd", "pv", "ri", "norm", "at", "atev", "wo", "out") as (block, s):
        a_ps, b_ps, v_ps = m.ps[0:2], m.ps[2:4], m.ps[4:6]
        s_ps, pt_ps, pv_ps, at_ps = m.ps[0:3], m.ps[3:6], m.ps[6], m.ps[7]
        NV = 2 * KT

        def by_act(i):
            return i % 2 == 0

        @block.vector
        def _(dve):
            dve.tensor_copy(m.xn_b, m.xn[:, here]).then_inc(s["xin"], 1)
            for p in range(NP_):
                dve.wait_ge(s["k"], p + 1)
                dve.tensor_copy(m.k1[:, p, :], b_ps[p % 2]).then_inc(s["kev"], 1)

            def negmax(i):
                qt, h = items[i]
                dve.wait_ge(s["score"], i + 1)
                if i >= 3:
                    dve.wait_ge(s["exp"], i - 2)
                dve.tensor_reduce(m.nm[:, i % 3:i % 3 + 1], s_ps[i % 3][:, 0:(qt + 1) * P], AX.X, ALU.max,
                                  negate=True).then_inc(s["nm"], 1)

            def probs_t(i):
                qt, h = items[i]
                if by_act(i):
                    return
                dve.wait_ge(s["turn"], i + 1)
                if i >= 3:
                    dve.wait_ge(s["pv"], i - 2)
                dve.tensor_copy(m.pt[:, i % 3, 0:(qt + 1) * P], pt_ps[i % 3][:, 0:(qt + 1) * P]).then_inc(s["ptd"], 1)

            def normed(g):
                qt, h = items[4 * g]
                pv = pv_ps[:, 0:4 * (HD1 + 1)].rearrange("p (h c) -> p h c", h=4)
                dve.wait_ge(s["pv"], 4 * g + 4)
                dve.reciprocal(m.ri[:, g % 2, :], pv[:, :, HD1]).then_inc(s["ri"], 1)
                dve.wait_ge(s["ri"], g + 1)
                if h == 0 and qt >= 2:
                    dve.wait_ge(s["at"], 2 * (qt - 1))
                dve.tensor_tensor(m.an[:, qt % 2, h * HD1:(h + 4) * HD1].rearrange("p (h c) -> p h c", h=4),
                                  pv[:, :, 0:HD1], m.ri[:, g % 2, :].unsqueeze(2).to_broadcast([P, 4, HD1]),
                                  ALU.mult).then_inc(s["norm"], 1)

            for i in range(NI + 3):
                if i < NI:
                    negmax(i)
                if 1 <= i <= NI:
                    probs_t(i - 1)
                if i >= 3 and (i - 3) % 4 == 3:
                    normed((i - 3) // 4)
            dve.wait_ge(s["wo"], 1)
            dve.tensor_tensor(m.xsum[:, here], m.ps[0], m.xsum[:, here], ALU.add).then_inc(s["out"], 1)

        @block.scalar
        def _(act):
            act.wait_ge(s["lat"], 1)
            act.activation(m.lat, m.ps[7], ACT.Copy).then_inc(s["latc"], 1)
            for p in range(NP_):
                act.wait_ge(s["q"], p + 1)
                act.activation(m.q1[:, p, :], a_ps[p % 2], ACT.Copy, scale=float(HD1) ** -0.5).then_inc(s["qev"], 1)
                act.wait_ge(s["v"], p + 1)
                kt, c = p // 2, p % 2
                act.activation(m.v1[:, kt, 8 * c:8 * c + 8, 0:HD1], v_ps[p % 2].rearrange("p (h c) -> p h c", h=8),
                               ACT.Copy).then_inc(s["vev"], 1)

            def probs_t(i):
                qt, h = items[i]
                if not by_act(i):
                    return
                act.wait_ge(s["turn"], i + 1)
                if i >= 3:
                    act.wait_ge(s["pv"], i - 2)
                act.activation(m.pt[:, i % 3, 0:(qt + 1) * P], pt_ps[i % 3][:, 0:(qt + 1) * P], ACT.Copy)\
                   .then_inc(s["pta"], 1)

            def turned_rows(qt):
                for c in range(2):
                    act.wait_ge(s["at"], 2 * qt + c + 1)
                    act.activation(m.attnT[:, 4 * c:4 * c + 4, qt * P:(qt + 1) * P],
                                   at_ps.rearrange("p (k q) -> p k q", k=4), ACT.Copy).then_inc(s["atev"], 1)

            for i in range(NI + 1):
                if i < NI:
                    qt, h = items[i]
                    act.wait_ge(s["nm"], i + 1)
                    if i >= 3:
                        act.wait_ge(s["turn"], i - 2)
                    act.activation(m.pr[:, i % 3, 0:(qt + 1) * P], s_ps[i % 3][:, 0:(qt + 1) * P], ACT.Exp,
                                   bias=m.nm[:, i % 3:i % 3 + 1]).then_inc(s["exp"], 1)
                if i >= 1:
                    probs_t(i - 1)
                if i % H1 == 5 and i > H1:
                    turned_rows(i // H1 - 1)
            turned_rows(KT - 1)

        @block.tensor
        def _(pe):
            pe.wait_ge(s["xin"], 1)
            pe.matmul(m.ps[7], m.w_kvd, m.xn_b, start=True, stop=True).then_inc(s["lat"], 1)
            pe.wait_ge(s["latc"], 1)
            for p in range(NP_):
                if p >= 2:
                    pe.wait_ge(s["qev"], p - 1)
                pe.matmul(a_ps[p % 2], m.w_q1[:, p * P:(p + 1) * P], m.xn_b, start=True, stop=True).then_inc(s["q"], 1)
                if p >= 2:
                    pe.wait_ge(s["kev"], p - 1)
                pe.matmul(b_ps[p % 2], m.w_kvu[:, p * P:(p + 1) * P], m.lat, start=True, stop=True).then_inc(s["k"], 1)
                if p >= 2:
                    pe.wait_ge(s["vev"], p - 1)
                kt, c = p // 2, p % 2
                pe.matmul(v_ps[p % 2], m.lat[:, kt * P:(kt + 1) * P], m.w_kvu[:, V0 + 512 * c:V0 + 512 * (c + 1)],
                          start=True, stop=True).then_inc(s["v"], 1)

            def scores(i):
                qt, h = items[i]
                p, r = h // 2, HD1 * (h % 2)
                nk = (qt + 1) * P
                if i == 0:
                    pe.wait_ge(s["qev"], NP_)
                    pe.wait_ge(s["kev"], NP_)
                    pe.wait_ge(s["vev"], NV)
                if i >= 3:
                    pe.wait_ge(s["exp"], i - 2)
                pe.matmul(s_ps[i % 3][:, 0:nk], m.q1[r:r + HD1, p, qt * P:(qt + 1) * P], m.k1[r:r + HD1, p, 0:nk],
                          start=True, stop=False, skip_group_check=True)
                pe.matmul(s_ps[i % 3][:, qt * P:nk], m.ident16, m.mcausal, start=False, stop=True,
                          skip_group_check=True).then_inc(s["score"], 1)

            def turn(i):
                qt, h = items[i]
                pe.wait_ge(s["exp"], i + 1)
                if i >= 3:
                    if by_act(i - 3):
                        pe.wait_ge(s["pta"], (i - 3) // 2 + 1)
                    else:
                        pe.wait_ge(s["ptd"], (i - 3) // 2 + 1)
                for kt in range(qt + 1):
                    mm = pe.transpose(pt_ps[i % 3][:, kt * P:(kt + 1) * P], m.pr[:, i % 3, kt * P:(kt + 1) * P],
                                      m.ident)
                mm.then_inc(s["turn"], 1)

            def values(i):
                qt, h = items[i]
                if by_act(i):
                    pe.wait_ge(s["pta"], i // 2 + 1)
                else:
                    pe.wait_ge(s["ptd"], i // 2 + 1)
                if h % 4 == 0 and i:
                    pe.wait_ge(s["norm"], i // 4)
                c = h % 4 * (HD1 + 1)
                for kt in range(qt + 1):
                    mm = pe.matmul(pv_ps[:, c:c + HD1 + 1], m.pt[:, i % 3, kt * P:(kt + 1) * P], m.v1[:, kt, h, :],
                                   start=(kt == 0), stop=(kt == qt), skip_group_check=True)
                mm.then_inc(s["pv"], 1)

            def turn_rows(qt):
                pe.wait_ge(s["norm"], 4 * qt + 4)
                for c in range(2):
                    if qt or c:
                        pe.wait_ge(s["atev"], 2 * qt + c)
                    for k in range(4):
                        kp = 4 * c + k
                        mm = pe.transpose(at_ps[:, k * P:(k + 1) * P], m.an[:, qt % 2, kp * P:(kp + 1) * P], m.ident)
                    mm.then_inc(s["at"], 1)

            for i in range(NI + 2):
                if i < NI:
                    scores(i)
                if 1 <= i <= NI:
                    turn(i - 1)
                if i >= 2:
                    values(i - 2)
                if i % H1 == 5 and i > H1:
                    turn_rows(i // H1 - 1)
            turn_rows(KT - 1)
            pe.wait_ge(s["atev"], 2 * KT)
            for kp in range(NP_):
                mm = pe.matmul(m.ps[0], m.w_o1[:, kp, :], m.attnT[:, kp, :], start=(kp == 0), stop=(kp == NP_ - 1))
            mm.then_inc(s["wo"], 1)


def load_latent(nc, m, d):
    loads = [(m.w_kvd, d["L1_attn_w_kv_down"]), (m.w_kvu, d["L1_attn_w_kv_up"]), (m.w_q1, d["L1_attn_w_q"]),
             (m.w_o1, d["L1_attn_w_out"].rearrange("(k p) d -> p k d", p=P))]
    with stage(nc, "lload", "loaded", "set") as (block, s):
        @block.sync
        def _(sp):
            for dst, src in loads:
                sp.dma_start(dst, src).then_inc(s["loaded"], 16)
            sp.wait_ge(s["loaded"], 16 * len(loads))

        @block.vector
        def _(dve):
            dve.memset(m.v1, 1.0).then_inc(s["set"], 1)


def token_rows(nc, m, src, dst, label):
    with stage(nc, label, "turned", "kept") as (block, s):
        @block.tensor
        def _(pe):
            for c in range(B):
                if c >= 4:
                    pe.wait_ge(s["kept"], c - 3)
                for t in range(KT):
                    mm = pe.transpose(m.ps[c % 4][:, t * P:(t + 1) * P], src[:, c * T + t * P:c * T + (t + 1) * P],
                                      m.ident)
                mm.then_inc(s["turned"], 1)

        @block.vector
        def _(dve):
            for c in range(B):
                dve.wait_ge(s["turned"], c + 1)
                dve.tensor_copy(dst[:, c * KT:(c + 1) * KT, :].rearrange("p t d -> p (t d)"), m.ps[c % 4])\
                   .then_inc(s["kept"], 1)


def token_stats(nc, m):
    with stage(nc, "stats", "dve", "sq", "root") as (block, s):
        st = lambda i: m.stats[:, :, i]
        mean_b = m.stats[:, :, 0:1].to_broadcast([P, NT, D])

        @block.vector
        def _(dve):
            dve.tensor_reduce(st(0), m.xr, AX.X, ALU.add).then_inc(s["dve"], 1)
            dve.tensor_reduce(st(2), m.xr, AX.X, ALU.min).then_inc(s["dve"], 1)
            dve.tensor_reduce(st(3), m.xr, AX.X, ALU.max).then_inc(s["dve"], 1)
            dve.wait_ge(s["sq"], 1)
            dve.tensor_reduce(m.red[:, 0, :], m.sqr, AX.X, ALU.add).then_inc(s["dve"], 1)
            dve.wait_ge(s["dve"], 4)
            dve.tensor_scalar(st(0), st(0), 1.0 / D, None, ALU.mult).then_inc(s["dve"], 1)
            dve.tensor_scalar(m.sqr, m.xr, 1e-6, None, ALU.is_lt).then_inc(s["dve"], 1)
            dve.wait_ge(s["dve"], 6)
            dve.scalar_tensor_tensor(out=m.sqr, in0=m.xr, scalar=-1e-6, in1=m.sqr, op0=ALU.is_gt, op1=ALU.mult)\
               .then_inc(s["dve"], 1)
            dve.wait_ge(s["dve"], 7)
            dve.tensor_reduce(st(5), m.sqr, AX.X, ALU.add).then_inc(s["dve"], 1)
            dve.wait_ge(s["dve"], 8)
            dve.tensor_scalar(st(5), st(5), 1.0 / D, None, ALU.mult).then_inc(s["dve"], 1)
            dve.tensor_tensor(m.sqr, m.xr, mean_b, ALU.subtract).then_inc(s["dve"], 1)
            dve.wait_ge(s["sq"], 2)
            dve.tensor_reduce(m.red[:, 1, :], m.sqr, AX.X, ALU.add).then_inc(s["dve"], 1)

        @block.scalar
        def _(act):
            act.activation(m.sqr, m.xr, ACT.Square).then_inc(s["sq"], 1)
            act.wait_ge(s["dve"], 10)
            act.activation(m.sqr, m.sqr, ACT.Square).then_inc(s["sq"], 1)
            act.activation(st(4), m.red[:, 0, :], ACT.Sqrt, bias=m.zcol).then_inc(s["root"], 1)
            act.wait_ge(s["dve"], 11)
            act.activation(st(1), m.red[:, 1, :], ACT.Sqrt, bias=m.zcol, scale=1.0 / (D - 1)).then_inc(s["root"], 1)


def router(nc, m, d):
    with stage(nc, "router", "w", "st", "stev", "h", "hid", "lg", "lgev", "nm", "sub", "exp", "sum", "ri",
               "probs") as (block, s):
        loads = [(m.r1, d["p_r1"]), (m.r1s, d["p_r1s"]), (m.r1b, d["p_r1b"]), (m.r2, d["p_r2"])]

        @block.sync
        def _(sp):
            for dst, src in loads:
                sp.dma_start(dst, src).then_inc(s["w"], 16)

        @block.tensor
        def _(pe):
            for c in range(B):
                if c >= 2:
                    pe.wait_ge(s["stev"], c - 1)
                for t in range(KT):
                    mm = pe.transpose(m.ps[c % 2][0:NSTAT, t * P:(t + 1) * P], m.stats[:, c * KT + t, :], m.ident)
                mm.then_inc(s["st"], 1)
            pe.wait_ge(s["w"], 16 * len(loads))

            def logits(c):
                pe.wait_ge(s["hid"], c + 1)
                for t in range(KT):
                    i = c * KT + t
                    mm = pe.matmul(m.ps[4 + i // 16][:, i % 16 * E:(i % 16 + 1) * E], m.rh[:, c % 2, t * P:(t + 1) * P],
                                   m.r2, start=True, stop=True)
                mm.then_inc(s["lg"], 1)

            for c in range(B):
                if c >= 2:
                    pe.wait_ge(s["hid"], c - 1)
                pe.wait_ge(s["stev"], c + 1)
                pe.matmul(m.ps[2 + c % 2][0:RH, :], m.r1, m.xn[:, c * T:(c + 1) * T], start=True, stop=False)
                pe.matmul(m.ps[2 + c % 2][0:RH, :], m.r1s, m.statT[:, c * T:(c + 1) * T], start=False, stop=True)\
                  .then_inc(s["h"], 1)
                if c:
                    logits(c - 1)
            logits(B - 1)

        @block.scalar
        def _(act):
            for c in range(B):
                act.wait_ge(s["h"], c + 1)
                if c >= 2:
                    act.wait_ge(s["lg"], c - 1)
                act.activation(m.rh[:, c % 2, :], m.ps[2 + c % 2][0:RH, :], ACT.Gelu, bias=m.r1b).then_inc(s["hid"], 1)
            act.wait_ge(s["sub"], 1)
            act.activation(m.probs, m.probs, ACT.Exp).then_inc(s["exp"], 1)

        @block.vector
        def _(dve):
            for c in range(B):
                dve.wait_ge(s["st"], c + 1)
                dve.tensor_copy(m.statT[:, c * T:(c + 1) * T], m.ps[c % 2][0:NSTAT, :]).then_inc(s["stev"], 1)
            dve.wait_ge(s["lg"], B)
            for i in range(2):
                dve.tensor_copy(m.probs[:, 16 * i:16 * i + 16, :].rearrange("p t e -> p (t e)"), m.ps[4 + i])\
                   .then_inc(s["lgev"], 1)
            dve.wait_ge(s["lgev"], 2)
            dve.tensor_reduce(m.red[:, 0, :], m.probs, AX.X, ALU.max).then_inc(s["nm"], 1)
            dve.wait_ge(s["nm"], 1)
            over = lambda a: a.unsqueeze(2).to_broadcast([P, NT, E])
            dve.tensor_tensor(m.probs, m.probs, over(m.red[:, 0, :]), ALU.subtract).then_inc(s["sub"], 1)
            dve.wait_ge(s["exp"], 1)
            dve.tensor_reduce(m.red[:, 1, :], m.probs, AX.X, ALU.add).then_inc(s["sum"], 1)
            dve.wait_ge(s["sum"], 1)
            dve.reciprocal(m.red[:, 2, :], m.red[:, 1, :]).then_inc(s["ri"], 1)
            dve.wait_ge(s["ri"], 1)
            dve.tensor_tensor(m.probs, m.probs, over(m.red[:, 2, :]), ALU.mult).then_inc(s["probs"], 1)


def route(nc, m, d):
    S4 = N // 4
    with stage(nc, "route", "io", "top", "idx", "hot", "msk", "t", "tev", "m8", "mr", "seg", "fin", "thr", "cmp",
               "back", "bev", "sl", "w") as (block, s):
        NTOP = CAP // 8

        @block.gpsimd
        def _(pool):
            pool.iota(m.eiota, [[1, E]], base=0, channel_multiplier=0,
                      allow_small_or_imprecise_dtypes=True).then_inc(s["io"], 1)
            pool.iota(m.ebase, [[0, 1]], base=0, channel_multiplier=CAP,
                      allow_small_or_imprecise_dtypes=True).then_inc(s["io"], 1)

        @block.tensor
        def _(pe):
            pe.wait_ge(s["msk"], 1)
            for i in range(B):
                if i >= 4:
                    pe.wait_ge(s["tev"], i - 3)
                for t in range(KT):
                    mm = pe.transpose(m.ps[i % 4][0:E, t * P:(t + 1) * P], m.score[:, i * KT + t, :], m.ident)
                mm.then_inc(s["t"], 1)
            pe.wait_ge(s["sl"], 1)
            for i in range(NT):
                mm = pe.transpose(m.ps[4 + i // 16][:, i % 16 * E:(i % 16 + 1) * E], m.slotE[:, i * P:(i + 1) * P],
                                  m.ident[0:E, 0:E])
            mm.then_inc(s["back"], 1)

        @block.vector
        def _(dve):
            step = [0]

            def then(ins):
                step[0] += 1
                ins.then_inc(s["w"], 1)
                dve.wait_ge(s["w"], step[0])

            for i in range(NT):
                last = dve.max(m.top8[:, i, :], m.probs[:, i, :])
            then(last)
            for i in range(NT):
                last = dve.max_index(m.idx8[:, i, :], m.top8[:, i, :], m.probs[:, i, :])
            then(last)
            then(dve.tensor_copy(m.idxf, m.idx8[:, :, 0:2]))
            dve.wait_ge(s["io"], 2)
            es = m.eiota.unsqueeze(1).to_broadcast([P, NT, E])
            for j in range(2):
                last = dve.tensor_tensor(m.hot[:, j, :, :], es, m.idxf[:, :, j:j + 1].to_broadcast([P, NT, E]),
                                         ALU.is_equal)
            then(last)
            then(dve.tensor_tensor(m.score, m.hot[:, 0, :, :], m.hot[:, 1, :, :], ALU.add))
            then(dve.tensor_tensor(m.tmpn, m.probs, m.score, ALU.mult))
            then(dve.tensor_scalar(m.score, m.score, -1.0, None, ALU.add))
            dve.tensor_tensor(m.score, m.score, m.tmpn, ALU.add).then_inc(s["msk"], 1)
            for i in range(B):
                dve.wait_ge(s["t"], i + 1)
                dve.tensor_copy(m.scoreE[:, i * T:(i + 1) * T], m.ps[i % 4][0:E, :]).then_inc(s["tev"], 1)
            dve.wait_ge(s["tev"], B)
            for q in range(4):
                last = dve.tensor_copy(m.quart[q * E:(q + 1) * E, :], m.scoreE[:, q * S4:(q + 1) * S4])
            then(last)
            for r in range(NTOP):
                then(dve.max(m.best[:, 8 * r:8 * r + 8], m.quart))
                then(dve.match_replace(out=m.quart, in_to_replace=m.best[:, 8 * r:8 * r + 8], in_values=m.quart,
                                       imm_value=-2.0))
            for q in range(4):
                last = dve.tensor_copy(m.cand[:, q * CAP:(q + 1) * CAP], m.best[q * E:(q + 1) * E, :])
            then(last)
            for r in range(NTOP):
                then(dve.max(m.b8, m.cand))
                if r < NTOP - 1:
                    then(dve.match_replace(out=m.cand, in_to_replace=m.b8, in_values=m.cand, imm_value=-2.0))
            thr = m.b8[:, 7:8]
            then(dve.tensor_scalar(m.gt, m.scoreE, thr, None, ALU.is_gt))
            dve.tensor_scalar(m.eq, m.scoreE, thr, None, ALU.is_equal)
            then(dve.tensor_reduce(m.cnt, m.gt, AX.X, ALU.add))
            then(dve.tensor_scalar(m.room, m.cnt, -1.0, float(CAP), ALU.mult, ALU.add))
            then(dve.tensor_tensor_scan(m.run, m.eq, m.eq, 0.0, ALU.add, ALU.bypass))
            then(dve.tensor_scalar(m.run, m.run, m.room, None, ALU.is_le))
            then(dve.tensor_tensor(m.run, m.run, m.eq, ALU.mult))
            then(dve.tensor_tensor(m.gt, m.gt, m.run, ALU.add))
            then(dve.tensor_scalar(m.eq, m.scoreE, 0.0, None, ALU.is_ge))
            then(dve.tensor_tensor(m.gt, m.gt, m.eq, ALU.mult))
            then(dve.tensor_tensor_scan(m.run, m.gt, m.gt, 0.0, ALU.add, ALU.bypass))
            then(dve.tensor_scalar(m.run, m.run, m.ebase, None, ALU.add))
            dve.tensor_tensor(m.slotE, m.run, m.gt, ALU.mult).then_inc(s["sl"], 1)
            dve.wait_ge(s["back"], 1)
            for i in range(2):
                last = dve.tensor_copy(m.slotN[:, 16 * i:16 * i + 16, :].rearrange("p t e -> p (t e)"), m.ps[4 + i])
            then(last)
            for j in range(2):
                then(dve.tensor_tensor(m.tmpn, m.hot[:, j, :, :], m.slotN, ALU.mult))
                then(dve.tensor_reduce(m.slot[:, j, :], m.tmpn, AX.X, ALU.add))
            then(dve.tensor_tensor(m.red[:, 0, :], m.top8[:, :, 0], m.top8[:, :, 1], ALU.add))
            then(dve.reciprocal(m.red[:, 1, :], m.red[:, 0, :]))
            for j in range(2):
                then(dve.tensor_tensor(m.wt[:, j, :], m.top8[:, :, j], m.red[:, 1, :], ALU.mult))
            then(dve.tensor_scalar(m.keep, m.slot, 1.0, None, ALU.is_ge))
            then(dve.tensor_tensor(m.wt, m.wt, m.keep, ALU.mult))
            then(dve.tensor_scalar(m.keep, m.keep, -float(SLOTS + 1), float(SLOTS), ALU.mult, ALU.add))
            then(dve.tensor_tensor(m.slot, m.slot, m.keep, ALU.add))
            then(dve.tensor_copy(m.slotu, m.slot))


def dispatch(nc, m, d):
    with stage(nc, "disp", "z", "zeroed", "sent") as (block, s):
        NZ = SLOTS // P

        @block.vector
        def _(dve):
            dve.memset(m.zrow, 0.0).then_inc(s["z"], 1)

        @block.gpsimd
        def _(pool):
            pool.wait_ge(s["z"], 1)
            pool.dma_start(d["s_in"][0:SLOTS, :].rearrange("(p a) d -> p a d", p=P),
                           m.zrow.unsqueeze(1).to_broadcast([P, NZ, D])).then_inc(s["zeroed"], 16)
            pool.dma_start(d["s_out"][SLOTS:SLOTS + 1, :], m.zrow[0:1, :]).then_inc(s["zeroed"], 16)
            pool.wait_ge(s["zeroed"], 32)
            for i in range(NT):
                for j in range(2):
                    pool.indirect_dma_start(d["s_in"], bass.IndirectOffsetOnAxis(ap=m.slotu[:, j, i:i + 1], axis=0),
                                            m.xr[:, i, :], None, bounds_check=SLOTS - 1, oob_is_err=False)\
                        .then_inc(s["sent"], 16)
            pool.wait_ge(s["sent"], 16 * 2 * NT)


def experts(nc, m, d, g):
    E2 = E // GRP
    NU = 6
    C2 = CAP - P
    with stage(nc, "moe", "x", "w", "xt", "xtev", "up", "act", "hid", "y", "yev", "out") as (block, s):
        @block.sync
        def _(sp):
            for e in range(E2):
                rows = d["s_in"][bass.ds(g * E2 * CAP + e * CAP, CAP), :]
                sp.dma_start(m.xe[:, e, 0, :], rows[0:P, :]).then_inc(s["x"], 16)
                sp.dma_start(m.xe[0:C2, e, 1, :], rows[P:CAP, :]).then_inc(s["x"], 16)
            sp.dma_start(m.aup, d["p_aup"][g, :, :]).then_inc(s["w"], 16)
            sp.dma_start(m.adn, d["p_adn"][g, :, :]).then_inc(s["w"], 16)
            for e in range(E2):
                sp.dma_start(m.wup[:, e, :], d["p_wup"][g * E2 + e, :, :]).then_inc(s["w"], 16)
                sp.dma_start(m.wdn[:, e, :, :], d["p_wdn"][g * E2 + e, :, :].rearrange("(k p) d -> p k d", p=P))\
                  .then_inc(s["w"], 16)
            for e in range(E2):
                sp.wait_ge(s["yev"], 2 * (e + 1))
                out = d["s_out"][bass.ds(g * E2 * CAP + e * CAP, CAP), :]
                sp.dma_start(out[0:P, :], m.ye[:, e, 0, :]).then_inc(s["out"], 16)
                sp.dma_start(out[P:CAP, :], m.ye[0:C2, e, 1, :]).then_inc(s["out"], 16)
            sp.wait_ge(s["out"], 16 * 2 * E2)

        @block.tensor
        def _(pe):
            pe.wait_ge(s["x"], 16 * 2 * E2)
            for e in range(E2):
                pe.transpose(m.ps[e][:, 0:P], m.xe[:, e, 0, :], m.ident)
                pe.transpose(m.ps[e][:, P:CAP], m.xe[0:C2, e, 1, :], m.ident[0:C2, 0:C2]).then_inc(s["xt"], 1)
            pe.wait_ge(s["w"], 16 * (2 + 2 * E2))
            for e in range(E2):
                pe.wait_ge(s["xtev"], e + 1)
                for k in range(3):
                    u = 3 * e + k
                    if u >= 2:
                        pe.wait_ge(s["hid"], u - 1)
                    wg = m.wup[:, e, k * P:(k + 1) * P] if k < 2 else m.aup[:, 0:P]
                    wv = m.wup[:, e, INTER + k * P:INTER + (k + 1) * P] if k < 2 else m.aup[:, P:2 * P]
                    pe.matmul(m.ps[2 + u % 2][:, 0:CAP], wg, m.xeT[:, e, :], start=True, stop=True)
                    pe.matmul(m.ps[4 + u % 2][:, 0:CAP], wv, m.xeT[:, e, :], start=True, stop=True).then_inc(s["up"], 1)
            for e in range(E2):
                pe.wait_ge(s["hid"], 3 * (e + 1))
                for part, (a, b2) in enumerate(((0, P), (P, CAP))):
                    if e:
                        pe.wait_ge(s["yev"], 2 * (e - 1) + part + 1)
                    for k in range(3):
                        w = m.wdn[:, e, k, :] if k < 2 else m.adn
                        mm = pe.matmul(m.ps[6 + part][0:b2 - a, 0:D], m.hm[:, e, k, a:b2], w, start=(k == 0),
                                       stop=(k == 2))
                    mm.then_inc(s["y"], 1)

        @block.scalar
        def _(act):
            for u in range(3 * E2):
                act.wait_ge(s["up"], u + 1)
                if u >= 2:
                    act.wait_ge(s["hid"], u - 1)
                act.activation(m.sg[:, u % 2, :], m.ps[2 + u % 2][:, 0:CAP], ACT.Silu).then_inc(s["act"], 1)

        @block.vector
        def _(dve):
            for e in range(E2):
                dve.wait_ge(s["xt"], e + 1)
                dve.tensor_copy(m.xeT[:, e, :], m.ps[e][:, 0:CAP]).then_inc(s["xtev"], 1)
            for u in range(3 * E2):
                e, k = divmod(u, 3)
                dve.wait_ge(s["act"], u + 1)
                dve.scalar_tensor_tensor(out=m.hm[:, e, k, :], in0=m.sg[:, u % 2, :], scalar=ADAPT if k == 2 else 1.0,
                                         in1=m.ps[4 + u % 2][:, 0:CAP], op0=ALU.mult, op1=ALU.mult).then_inc(s["hid"], 1)
            for e in range(E2):
                for part, n in ((0, P), (1, C2)):
                    dve.wait_ge(s["y"], 2 * e + part + 1)
                    dve.tensor_copy(m.ye[0:n, e, part, :], m.ps[6 + part][0:n, 0:D]).then_inc(s["yev"], 1)


def combine(nc, m, d):
    with stage(nc, "comb", "got0", "got1", "got2", "got3", "acc", "out") as (block, s):
        got = [s["got0"], s["got1"], s["got2"], s["got3"]]
        RING = len(got)

        @block.gpsimd
        def _(pool):
            for i in range(NT):
                if i >= RING:
                    pool.wait_ge(s["acc"], 2 * (i - RING) + 2)
                for j in range(2):
                    pool.indirect_dma_start(m.yt[:, i % RING, j, :], None, d["s_out"],
                                            bass.IndirectOffsetOnAxis(ap=m.slotu[:, j, i:i + 1], axis=0))\
                        .then_inc(got[i % RING], 16)

        @block.vector
        def _(dve):
            for i in range(NT):
                for j in range(2):
                    dve.wait_ge(got[i % RING], 32 * (i // RING + 1))
                    if j:
                        dve.wait_ge(s["acc"], 2 * i + 1)
                    dve.scalar_tensor_tensor(out=m.xo[:, i, :], in0=m.yt[:, i % RING, j, :], scalar=m.wt[:, j, i:i + 1],
                                             in1=m.xo[:, i, :], op0=ALU.mult, op1=ALU.add).then_inc(s["acc"], 1)

        @block.sync
        def _(sp):
            o = d["out"].rearrange("b (t p) d -> b p t d", p=P)
            for b in range(B):
                sp.wait_ge(s["acc"], 2 * KT * (b + 1))
                sp.dma_start(o[b], m.xo[:, b * KT:(b + 1) * KT, :]).then_inc(s["out"], 16)
            sp.wait_ge(s["out"], 16 * B)


def build(nc, d):
    d["s_in"] = nc.dram_tensor("slot_rows", (SLOTS, D), F32, kind="Internal").ap()
    d["s_out"] = nc.dram_tensor("slot_results", (SLOTS + 1, D), F32, kind="Internal").ap()
    with ExitStack() as ctx:
        m = Memory()
        times = {}

        def sb(scope, name, shape, dt=F32):
            times[name] = times.get(name, 0) + 1
            t = scope.enter_context(nc.sbuf_tensor(f"{name}_{times[name]}", shape, dt))
            return t[tuple(slice(None) for _ in shape)]

        psum = ctx.enter_context(nc.psum_tensor("banks", [P, 8, T], F32))
        m.ps = [psum[:, i, :] for i in range(8)]
        m.ps2 = [psum[:, 2 * i:2 * i + 2, :] for i in range(4)]

        m.xsum = sb(ctx, "xsum", [P, N])
        m.xn = sb(ctx, "xn", [P, N])
        m.ident = sb(ctx, "ident", [P, P])
        m.onesm = sb(ctx, "onesm", [P, P])
        m.ones = sb(ctx, "ones", [P, T])
        m.bones64 = sb(ctx, "bones64", [P, P])
        m.eps = sb(ctx, "eps", [P, 1])
        m.zcol = sb(ctx, "zcol", [P, 1])
        m.tbias = sb(ctx, "tbias", [P, 1])
        m.ident16 = sb(ctx, "ident16", [P, P], BF16)
        m.mcausal = sb(ctx, "mcausal", [P, P], BF16)
        m.mlocal = sb(ctx, "mlocal", [P, 2, 2 * P], BF16)

        with ExitStack() as front:
            m.xq = sb(front, "xq", [P, N])
            m.xc = sb(front, "xc", [P, 2, T])
            m.sq = sb(front, "sq", [P, 2, T])
            m.sd = sb(front, "sd", [P, 2, T])
            m.rs = sb(front, "rs", [P, 2, T])
            with ExitStack() as scope:
                m.xrow = sb(scope, "xrow", [P, NT, D])
                m.w_q0 = sb(scope, "w_q0", [D, D])
                m.w_k0 = sb(scope, "w_k0", [D, D])
                m.w_v0 = sb(scope, "w_v0", [D, D])
                m.w_o0 = sb(scope, "w_o0", [D, D])
                m.bones8 = sb(scope, "bones8", [P, P])
                m.hmask = sb(scope, "hmask", [P, H0])
                m.g_q0 = sb(scope, "g_q0", [P, 1])
                m.g_k0 = sb(scope, "g_k0", [P, 1])
                m.b_o0 = sb(scope, "b_o0", [P, 1])
                m.gamma0 = sb(scope, "gamma0", [P, 1])
                m.beta0 = sb(scope, "beta0", [P, 1])
                m.gq_blk = sb(scope, "gq_blk", [P, P])
                m.gk_blk = sb(scope, "gk_blk", [P, P])
                m.mcausal_f = sb(scope, "mcausal_f", [P, P])
                m.mlocal_f = sb(scope, "mlocal_f", [P, 2, 2 * P])
                m.vbd = sb(scope, "vbd", [P, KT, H0 * (P + HD0)])
                m.vp = sb(scope, "vp", [P, T])
                m.xq_b = sb(scope, "xq_b", [P, T])
                m.xn_b = sb(scope, "xn_b", [P, T])
                m.qh = sb(scope, "qh", [P, T])
                m.kh = sb(scope, "kh", [P, T])
                m.km = sb(scope, "km", [P, 3, T])
                m.tanh = sb(scope, "tanh", [P, 3, 2, T])
                m.gateq = sb(scope, "gateq", [P, T])
                m.gatek = sb(scope, "gatek", [P, T])
                m.fused = sb(scope, "fused", [P, T])
                load_constants(nc, m, d)
                load_x(nc, m, d)
                layer_norm_all(nc, m, m.xsum, m.xn, label="ln1")
                layer_norm_all(nc, m, m.xn, m.xq, m.gamma0, m.beta0, label="ln2")
                with nc.Fori(0, B) as b:
                    resonance_attention(nc, m, b)

            with ExitStack() as scope:
                m.wqkv = sb(scope, "wqkv", [P, 3 * INNER])
                m.wrot = sb(scope, "wrot", [P, 2 * INNER])
                m.wo = sb(scope, "wo", [P, HL // 2, D])
                m.w1 = sb(scope, "w1", [P, 2 * DIN])
                m.w2 = sb(scope, "w2", [P, 3, D])
                m.b1 = sb(scope, "b1", [P, 6])
                m.lnp = sb(scope, "lnp", [P, 3])
                m.qks = sb(scope, "qks", [P, 4])
                m.rot0 = sb(scope, "rot0", [P, 4, T])
                m.rot = sb(scope, "rot", [P, 4, T])
                with ExitStack() as inner:
                    m.xs = sb(inner, "xs", [P, WIN + T])
                    m.qr = sb(inner, "qr", [P, HL // 2, T])
                    m.kr = sb(inner, "kr", [P, HL // 2, WIN + T])
                    m.v = sb(inner, "v", [P, NQ, HL, HDL + 1])
                    m.t1 = sb(inner, "t1", [P, 2, T])
                    m.t2 = sb(inner, "t2", [P, 2, T])
                    m.t3 = sb(inner, "t3", [P, 2, T])
                    m.nm = sb(inner, "nm", [P, 2, 4])
                    m.ri = sb(inner, "ri", [P, 2, 4])
                    m.attnT = sb(inner, "attnT", [P, HL // 2, T])
                    m.xsh = sb(inner, "xsh", [P, 2, T])
                    m.an = m.xq[:, 0:2 * INNER].rearrange("p (a c) -> p a c", a=2)
                    m.pr, m.pt, m.ge, m.hid = m.t1, m.t2, m.t1, m.attnT[:, 0:3, :]
                    clear_local(nc, m, d)
                    with nc.Fori(0, DEPTH) as layer:
                        load_layer(nc, m, d, layer)
                        with nc.Fori(0, B) as b:
                            local_attention(nc, m, b)
                        feed_forward(nc, m)
            layer_norm_all(nc, m, m.xsum, m.xn, add=m.xn, label="ln3")

        with ExitStack() as scope:
            m.w_kvd = sb(scope, "w_kvd", [P, R1])
            m.w_kvu = sb(scope, "w_kvu", [P, 2 * HDT])
            m.w_q1 = sb(scope, "w_q1", [P, HDT])
            m.w_o1 = sb(scope, "w_o1", [P, H1 // 2, D])
            m.xn_b = sb(scope, "xn_b", [P, T])
            m.lat = sb(scope, "lat", [P, T])
            m.q1 = sb(scope, "q1", [P, H1 // 2, T])
            m.k1 = sb(scope, "k1", [P, H1 // 2, T])
            m.v1 = sb(scope, "v1", [P, KT, H1, HD1 + 1])
            m.nm = sb(scope, "nm", [P, 4])
            m.ri = sb(scope, "ri", [P, 2, 4])
            m.pr = sb(scope, "pr", [P, 3, T])
            m.pt = sb(scope, "pt", [P, 3, T])
            m.an = sb(scope, "an", [P, 2, HDT])
            m.attnT = sb(scope, "attnT", [P, H1 // 2, T])
            load_latent(nc, m, d)
            with nc.Fori(0, B) as b:
                latent_attention(nc, m, b)

        m.xr = sb(ctx, "xr", [P, NT, D])
        m.xo = sb(ctx, "xo", [P, NT, D])
        m.slot = sb(ctx, "slot", [P, 2, NT])
        m.wt = sb(ctx, "wt", [P, 2, NT])
        m.keep = sb(ctx, "keep", [P, 2, NT])
        m.red = sb(ctx, "red", [P, 3, NT])
        m.slotu = sb(ctx, "slotu", [P, 2, NT], U32)
        token_rows(nc, m, m.xn, m.xr, "xrows")
        token_rows(nc, m, m.xsum, m.xo, "orows")
        with ExitStack() as scope:
            m.probs = sb(scope, "probs", [P, NT, E])
            with ExitStack() as inner:
                m.stats = sb(inner, "stats", [P, NT, NSTAT])
                m.sqr = sb(inner, "sqr", [P, NT, D])
                m.statT = sb(inner, "statT", [NSTAT, N])
                m.r1 = sb(inner, "r1", [P, RH])
                m.r1s = sb(inner, "r1s", [NSTAT, RH])
                m.r1b = sb(inner, "r1b", [RH, 1])
                m.r2 = sb(inner, "r2", [RH, E])
                m.rh = sb(inner, "rh", [RH, 2, T])
                token_stats(nc, m)
                router(nc, m, d)
            with ExitStack() as inner:
                m.top8 = sb(inner, "top8", [P, NT, 8])
                m.idxf = sb(inner, "idxf", [P, NT, 2])
                m.eiota = sb(inner, "eiota", [P, E])
                m.ebase = sb(inner, "ebase", [E, 1])
                m.hot = sb(inner, "hot", [P, 2, NT, E])
                m.score = sb(inner, "score", [P, NT, E])
                m.tmpn = sb(inner, "tmpn", [P, NT, E])
                m.slotN = sb(inner, "slotN", [P, NT, E])
                m.scoreE = sb(inner, "scoreE", [E, N])
                m.quart = sb(inner, "quart", [P, N // 4])
                m.best = sb(inner, "best", [P, CAP])
                m.cand = sb(inner, "cand", [E, 4 * CAP])
                m.b8 = sb(inner, "b8", [E, 8])
                m.gt = sb(inner, "gt", [E, N])
                m.eq = sb(inner, "eq", [E, N])
                m.run = sb(inner, "run", [E, N])
                m.cnt = sb(inner, "cnt", [E, 1])
                m.room = sb(inner, "room", [E, 1])
                m.idx8 = sb(inner, "idx8", [P, NT, 8], U32)
                m.slotE = m.eq
                route(nc, m, d)
        with ExitStack() as scope:
            m.zrow = sb(scope, "zrow", [P, D])
            m.xe = sb(scope, "xe", [P, 2, 2, D])
            m.xeT = sb(scope, "xeT", [P, 2, CAP])
            m.aup = sb(scope, "aup", [P, 2 * AINT])
            m.adn = sb(scope, "adn", [P, D])
            m.wup = sb(scope, "wup", [P, 2, 2 * INTER])
            m.wdn = sb(scope, "wdn", [P, 2, 2, D])
            m.hm = sb(scope, "hm", [P, 2, 3, CAP])
            m.sg = sb(scope, "sg", [P, 2, CAP])
            m.ye = sb(scope, "ye", [P, 2, 2, D])
            m.yt = sb(scope, "yt", [P, 4, 2, D])
            dispatch(nc, m, d)
            with nc.Fori(0, GRP) as g:
                experts(nc, m, d, g)
            combine(nc, m, d)


def clear_local(nc, m, d):
    with stage(nc, "clear", "loaded", "set") as (block, s):
        @block.sync
        def _(sp):
            sp.dma_start(m.rot0, d["c_rot"]).then_inc(s["loaded"], 16)
            sp.wait_ge(s["loaded"], 16)

        @block.vector
        def _(dve):
            dve.memset(m.xs, 0.0)
            dve.memset(m.xsh, 0.0)
            dve.memset(m.kr, 0.0)
            dve.memset(m.v, 1.0).then_inc(s["set"], 1)


def constants():
    import numpy as np
    f = np.float32
    c = {}
    c["c_ident"] = np.eye(P, dtype=f)
    c["c_bones8"] = np.kron(np.eye(H0, dtype=f), np.ones((HD0, HD0), f))
    c["c_bones64"] = np.kron(np.eye(2, dtype=f), np.ones((HDL, HDL), f))
    c["c_hmask"] = np.kron(np.eye(H0, dtype=f), np.ones((HD0, 1), f))
    q, k = np.arange(P)[:, None], np.arange(P)[None, :]
    c["c_causal"] = np.where(k <= q, 0, MASKED).astype(f)
    band = (k >= q) & (k <= q + WIN)
    first = band & (k >= WIN)
    c["c_local"] = np.stack([np.tile(np.where(w, 0, MASKED).astype(f), (1, 2)) for w in (first, band)], 1)
    half = np.arange(0, HDL, 2, dtype=f)
    inv_freq = (1.0 / f(10000.0) ** (half / f(HDL))).astype(f)
    t = np.arange(T, dtype=f)
    freqs = t[:, None] * inv_freq[None, :]
    base = ((half + f(0.4 * HDL)) / f(1.4 * HDL)).astype(f)
    power = ((t - T // 2) / f(WIN // 2)).astype(f)
    scale = (base[None, :] ** power[:, None]).astype(f)
    cos, sin = np.cos(freqs).astype(f), np.sin(freqs).astype(f)
    inv = (f(1.0) / scale).astype(f)
    parts = [(cos * scale, cos * scale), (-sin * scale, sin * scale), (cos * inv, cos * inv), (-sin * inv, sin * inv)]
    c["c_rot"] = np.stack([np.concatenate([a.T, b2.T, a.T, b2.T], 0) for a, b2 in parts], 1).astype(f)
    return {k2: np.ascontiguousarray(v) for k2, v in c.items()}


def laid_out(x):
    import numpy as np
    a = {k: np.ascontiguousarray(v) for k, v in x.items()}
    out = {"x": a["L0_attn_x"]}
    for n in ("L0_attn_w_q", "L0_attn_w_k", "L0_attn_w_v", "L0_attn_w_o", "L0_ffn_Wqkv", "L0_ffn_Wo", "L0_ffn_W1",
              "L1_attn_w_kv_down", "L1_attn_w_kv_up", "L1_attn_w_q", "L1_attn_w_out"):
        out[n] = a[n]
    out["p_g_q"] = np.tile(a["L0_attn_g_q"], H0)[:, None]
    out["p_g_k"] = np.tile(a["L0_attn_g_k"], H0)[:, None]
    out["p_b_o"], out["p_gamma"], out["p_beta"] = (a["L0_attn_" + n][:, None] for n in ("b_o", "gamma", "beta"))
    pad = len(FK) * P - DIN
    out["p_W2"] = np.pad(a["L0_ffn_W2"], ((0, 0), (0, pad), (0, 0)))
    b1 = np.pad(a["L0_ffn_b1"].reshape(DEPTH, 2, DIN), ((0, 0), (0, 0), (0, pad)))
    out["p_b1"] = b1.reshape(DEPTH, 2 * len(FK), P).transpose(0, 2, 1)
    out["p_lnp"] = np.stack([a["L0_ffn_ln_g"], a["L0_ffn_ln_b"], a["L0_ffn_b2"]], 2)
    cols = []
    for n in ("L0_ffn_q_scale", "L0_ffn_k_scale"):
        w = a[n]
        r = np.concatenate([w[:, HDL // 2:], w[:, :HDL // 2]], 1)
        cols += [np.concatenate([w, w], 1), np.concatenate([r, r], 1)]
    out["p_qks"] = np.stack(cols, 2)
    r1 = a["L1_ffn_r1_w"].T
    out["p_r1"], out["p_r1s"] = r1[:D], r1[D:]
    out["p_r1b"], out["p_r2"] = a["L1_ffn_r1_b"][:, None], a["L1_ffn_r2_w"].T
    for short, n in (("p_wup", "w_up"), ("p_wdn", "w_down"), ("p_aup", "a_up"), ("p_adn", "a_down")):
        out[short] = a["L1_ffn_" + n].transpose(0, 2, 1)
    return {k: np.ascontiguousarray(v) for k, v in out.items()}


def kernel(**inputs):
    import numpy as np
    import concourse.bacc as bacc
    from concourse.bass_utils import run_bass_kernel_spmd

    nc = bacc.Bacc("TRN2", target_bir_lowering=False, num_devices=1)
    arrays = {**constants(), **laid_out(inputs)}
    d = {}
    for name, a in arrays.items():
        d[name] = nc.dram_tensor(name, a.shape, mybir.dt.from_np(a.dtype), kind="ExternalInput").ap()
    d["out"] = nc.dram_tensor("out", (B, T, D), F32, kind="ExternalOutput").ap()
    build(nc, d)
    r = run_bass_kernel_spmd(nc, [arrays], core_ids=[0])
    return r.results[0]["out"]
```

```python
from contextlib import ExitStack, contextmanager

import concourse.bass as bass
from concourse import mybir

F32 = mybir.dt.float32
BF16 = mybir.dt.bfloat16
U32 = mybir.dt.uint32
ALU = mybir.AluOpType
ACT = mybir.ActivationFunctionType
AX = mybir.AxisListType

P = 128
D = 128
B, T = 8, 512
N = B * T
NT = N // P
LN_EPS = 1e-5
NORM_MAX = 1e12
MASKED = -1e30

H0, HD0 = 16, 8
KT = T // P
SHARP, COLLAPSE = 15.0, 0.27

DEPTH, HL, HDL, WIN = 6, 16, 64, 32
INNER = HL * HDL
QK_SCALE = 8.0
DIN = int(D * 4 * 2 / 3)
QW = P - WIN
QT = [QW] * (T // QW) + ([T % QW] if T % QW else [])
NQ = len(QT)
G4 = HL // 4
FK = [P, P, DIN - 2 * P]

H1, HD1 = 16, 64
R1 = 128
HDT = H1 * HD1

E, TOPK, INTER, AINT = 32, 2, 256, 128
GRP = 16
CAP = int(1.25 * N / E)
SLOTS = E * CAP
RH = D // 2
NSTAT = 6
ADAPT = 0.05


class Memory:
    pass


@contextmanager
def stage(nc, label, *names):
    with ExitStack() as ctx:
        sems = {n: ctx.enter_context(nc.semaphore(f"{label}_{n}")) for n in names}
        with nc.Block() as block:
            yield block, sems
        for s in sems.values():
            nc.gpsimd.sem_clear(s)
        nc.all_engine_barrier()


def load_constants(nc, m, d):
    loads = [
        (m.ident, d["c_ident"]), (m.bones8, d["c_bones8"]), (m.heads, d["c_heads"]), (m.hmask, d["c_hmask"]),
        (m.mcausal_f, d["c_causal"]), (m.mlocal_f, d["c_local"]), (m.spread_f, d["c_spread"]),
        (m.w_q0, d["L0_attn_w_q"]), (m.w_k0, d["L0_attn_w_k"]), (m.w_v0, d["L0_attn_w_v"]), (m.w_o0, d["L0_attn_w_o"]),
        (m.g_q0, d["p_g_q"]), (m.g_k0, d["p_g_k"]), (m.b_o0, d["p_b_o"]), (m.gamma0, d["p_gamma"]), (m.beta0, d["p_beta"]),
    ]
    with stage(nc, "const", "loaded", "set", "done") as (block, s):
        @block.sync
        def _(sp):
            for dst, src in loads:
                sp.dma_start(dst, src).then_inc(s["loaded"], 16)

        @block.vector
        def _(dve):
            dve.memset(m.onesm, 1.0 / D)
            dve.memset(m.ones, 1.0)
            dve.memset(m.eps, LN_EPS)
            dve.memset(m.zcol, 0.0)
            dve.memset(m.tbias, -SHARP * COLLAPSE)
            dve.memset(m.vbd, 0.0).then_inc(s["set"], 1)
            dve.wait_ge(s["loaded"], 16 * len(loads))
            dve.tensor_copy(m.ident16, m.ident)
            dve.tensor_copy(m.mcausal, m.mcausal_f)
            dve.tensor_copy(m.spread, m.spread_f)
            dve.tensor_copy(m.mlocal, m.mlocal_f)
            dve.tensor_scalar(m.gq_blk, m.bones8, m.g_q0, None, ALU.mult)
            dve.tensor_scalar(m.gk_blk, m.bones8, m.g_k0, None, ALU.mult).then_inc(s["done"], 1)


def load_x(nc, m, d):
    with stage(nc, "loadx", "loaded", "turned", "kept") as (block, s):
        x_v = d["x"].rearrange("b (t p) d -> b p t d", p=P)

        @block.sync
        def _(sp):
            for b in range(B):
                sp.dma_start(m.xrow[:, b * KT:(b + 1) * KT, :], x_v[b]).then_inc(s["loaded"], 16)

        @block.tensor
        def _(pe):
            for b in range(B):
                pe.wait_ge(s["loaded"], 16 * B if b else 16 * B)
                if b >= 4:
                    pe.wait_ge(s["kept"], b - 3)
                for t in range(KT):
                    mm = pe.transpose(m.ps[b % 4][:, t * P:(t + 1) * P], m.xrow[:, b * KT + t, :], m.ident)
                mm.then_inc(s["turned"], 1)

        @block.vector
        def _(dve):
            for b in range(B):
                dve.wait_ge(s["turned"], b + 1)
                dve.tensor_copy(m.xsum[:, b * T:(b + 1) * T], m.ps[b % 4][:, :]).then_inc(s["kept"], 1)


def layer_norm_all(nc, m, src, dst, gamma=None, beta=None, add=None, label="ln"):
    with stage(nc, label, "summed", *NORM_SEMS) as (block, s):
        @block.tensor
        def _(pe):
            def ready(c):
                if add is not None:
                    pe.wait_ge(s["summed"], c + 1)

            norm_pe(pe, m, s, lambda c: src[:, c * T:(c + 1) * T], ready)

        @block.scalar
        def _(act):
            norm_act(act, m, s)

        @block.vector
        def _(dve):
            if add is not None:
                for c in range(B):
                    here = slice(c * T, (c + 1) * T)
                    dve.tensor_tensor(src[:, here], src[:, here], add[:, here], ALU.add).then_inc(s["summed"], 1)
                dve.wait_ge(s["summed"], B)
            norm_dve(dve, m, s, lambda c: src[:, c * T:(c + 1) * T], dst, gamma, beta)


NORM_SEMS = ("mean", "xc", "sq", "var", "sd", "rs", "diag", "rsb", "scaled", "ln")


def norm_pe(pe, m, s, src, ready):
    def variance(c):
        pe.wait_ge(s["sq"], c + 1)
        if c >= 2:
            pe.wait_ge(s["sd"], c - 1)
        for t in range(KT):
            mm = pe.matmul(m.ps[2 + c % 2][:, t:t + 1], m.sq[:, c % 2, t * P:(t + 1) * P], m.onesm[:, 0:1],
                           start=True, stop=True)
        mm.then_inc(s["var"], 1)

    def spread(c):
        pe.wait_ge(s["diag"], c + 1)
        if c >= 2:
            pe.wait_ge(s["ln"], c - 1)
        pe.matmul(m.ps[4 + c % 2], m.ones[:, 0:P], m.diag[:, c % 2, :], start=True, stop=True).then_inc(s["rsb"], 1)

    for c in range(B + 2):
        if c < B:
            ready(c)
            if c >= 2:
                pe.wait_ge(s["xc"], c - 1)
            pe.matmul(m.ps[c % 2], m.onesm, src(c), start=True, stop=True).then_inc(s["mean"], 1)
        if 1 <= c <= B:
            variance(c - 1)
        if c >= 2:
            spread(c - 2)


def norm_act(act, m, s):
    for c in range(B):
        act.wait_ge(s["xc"], c + 1)
        if c >= 2:
            act.wait_ge(s["var"], c - 1)
        act.activation(m.sq[:, c % 2, :], m.xc3[:, c % 3, :], ACT.Square).then_inc(s["sq"], 1)
        act.wait_ge(s["var"], c + 1)
        act.activation(m.sdn[:, c, :], m.ps[2 + c % 2][:, 0:KT], ACT.Sqrt, bias=m.eps).then_inc(s["sd"], 1)


def norm_dve(dve, m, s, src, dst, gamma, beta, before=None):
    def diagonal(c):
        dve.wait_ge(s["sd"], c + 1)
        dve.reciprocal(m.rsn[:, c, :], m.sdn[:, c, :]).then_inc(s["rs"], 1)
        dve.wait_ge(s["rs"], c + 1)
        if c >= 2:
            dve.wait_ge(s["rsb"], c - 1)
        dve.tensor_tensor(m.diag[:, c % 2, :].rearrange("p (t q) -> p t q", t=KT),
                          m.ident.unsqueeze(1).to_broadcast([P, KT, P]),
                          m.rsn[:, c, :].unsqueeze(2).to_broadcast([P, KT, P]), ALU.mult).then_inc(s["diag"], 1)

    def normed(c):
        out = dst[:, c * T:(c + 1) * T]
        dve.wait_ge(s["rsb"], c + 1)
        if gamma is None:
            dve.tensor_tensor(out, m.ps[4 + c % 2], m.xc3[:, c % 3, :], ALU.mult).then_inc(s["ln"], 1)
            return
        dve.scalar_tensor_tensor(out=out, in0=m.ps[4 + c % 2], scalar=gamma, in1=m.xc3[:, c % 3, :], op0=ALU.mult,
                                 op1=ALU.mult).then_inc(s["scaled"], 1)
        dve.wait_ge(s["scaled"], c + 1)
        dve.tensor_scalar(out, out, beta, None, ALU.add).then_inc(s["ln"], 1)

    for c in range(B + 2):
        if c < B:
            if before is not None:
                before(c)
            dve.wait_ge(s["mean"], c + 1)
            if c >= 3:
                dve.wait_ge(s["sq"], c - 2)
                dve.wait_ge(s["ln"], c - 2)
            dve.tensor_tensor(m.xc3[:, c % 3, :], src(c), m.ps[c % 2], ALU.subtract).then_inc(s["xc"], 1)
        if 1 <= c <= B:
            diagonal(c - 1)
        if c >= 2:
            normed(c - 2)


def resonance_attention(nc, m, b):
    here = bass.ds(b * T, T)
    pairs = [(h, u) for h in range(H0) for u in range(2)]
    NI = len(pairs)
    with stage(nc, "res", "xin", "proj", "sq", "ss", "nrm", "rn", "unit", "gate", "th", "g", "vp", "vbd",
               "km", "score", "tanh", "pv", "fused", "wo", "out") as (block, s):
        q_ps, k_ps, v_ps, ssq, ssk, gq_ps, gk_ps, acc = (m.ps[i] for i in range(8))

        @block.vector
        def _(dve):
            dve.tensor_copy(m.xq_b, m.xq[:, here]).then_inc(s["xin"], 1)
            dve.tensor_copy(m.xn_b, m.xn[:, here]).then_inc(s["xin"], 1)
            for i, (ps, unit) in enumerate(((q_ps, m.qh), (k_ps, m.kh))):
                dve.wait_ge(s["nrm"], i + 1)
                dve.reciprocal(m.rs[:, i, :], m.sd[:, i, :]).then_inc(s["rn"], 1)
                dve.wait_ge(s["rn"], i + 1)
                dve.scalar_tensor_tensor(out=unit, in0=m.rs[:, i, :], scalar=NORM_MAX, in1=ps[:, :],
                                         op0=ALU.min, op1=ALU.mult).then_inc(s["unit"], 1)
            dve.wait_ge(s["th"], 2)
            dve.tensor_scalar(m.gateq, m.xc[:, 0, :], 0.375, 0.625, ALU.mult, ALU.add).then_inc(s["g"], 1)
            dve.tensor_scalar(m.gatek, m.xc[:, 1, :], 0.1875, 0.3125, ALU.mult, ALU.add).then_inc(s["g"], 1)
            dve.wait_ge(s["g"], 2)
            dve.tensor_tensor(m.vp, v_ps[:, :], m.gatek, ALU.mult).then_inc(s["vp"], 1)
            dve.wait_ge(s["vp"], 1)
            for kt in range(KT):
                blocks = m.vbd[:, kt, :].rearrange("p (h c) -> p h c", c=P + HD0)[:, :, 0:HD0]
                dve.tensor_copy(blocks, m.vp[:, kt * P:(kt + 1) * P].rearrange("p (h c) -> p h c", c=HD0))\
                   .then_inc(s["vbd"], 1)
            for h in range(H0):
                if h >= 3:
                    dve.wait_ge(s["score"], 2 * (h - 2))
                dve.tensor_scalar(m.km[:, h % 3, :], m.kh, m.hmask[:, h:h + 1], None, ALU.mult).then_inc(s["km"], 1)
            dve.wait_ge(s["pv"], NI + 1)
            dve.tensor_tensor(m.fused, acc[:, :], m.gateq, ALU.mult).then_inc(s["fused"], 1)
            dve.wait_ge(s["wo"], 1)
            dve.scalar_tensor_tensor(out=m.xsum[:, here], in0=q_ps[:, :], scalar=m.b_o0, in1=m.xsum[:, here],
                                     op0=ALU.add, op1=ALU.add).then_inc(s["out"], 1)

        @block.scalar
        def _(act):
            for i, ps in enumerate((q_ps, k_ps)):
                act.wait_ge(s["proj"], i + 1)
                act.activation(m.sq[:, i, :], ps[:, :], ACT.Square).then_inc(s["sq"], 1)
            for i, ps in enumerate((ssq, ssk)):
                act.wait_ge(s["ss"], i + 1)
                act.activation(m.sd[:, i, :], ps[:, :], ACT.Sqrt, bias=m.zcol).then_inc(s["nrm"], 1)
            for i, ps in enumerate((gq_ps, gk_ps)):
                act.wait_ge(s["gate"], i + 1)
                act.activation(m.xc[:, i, :], ps[:, :], ACT.Tanh, scale=0.5).then_inc(s["th"], 1)
            for i in range(NI):
                act.wait_ge(s["score"], i + 1)
                if i >= 3:
                    act.wait_ge(s["pv"], i - 2)
                act.activation(m.tanh[:, i % 3, :, :], m.ps2[i % 3][:, :, :], ACT.Tanh, bias=m.tbias, scale=SHARP)\
                   .then_inc(s["tanh"], 1)

        @block.tensor
        def _(pe):
            pe.wait_ge(s["xin"], 2)
            pe.matmul(q_ps[:, :], m.w_q0, m.xq_b, start=True, stop=True).then_inc(s["proj"], 1)
            pe.matmul(k_ps[:, :], m.w_k0, m.xq_b, start=True, stop=True).then_inc(s["proj"], 1)
            for kt in range(KT):
                mm = pe.matmul(v_ps[:, kt * P:(kt + 1) * P], m.xn_b[:, kt * P:(kt + 1) * P], m.w_v0,
                               start=True, stop=True)
            mm.then_inc(s["proj"], 1)
            for i, ps in enumerate((ssq, ssk)):
                pe.wait_ge(s["sq"], i + 1)
                pe.matmul(ps[:, :], m.bones8, m.sq[:, i, :], start=True, stop=True).then_inc(s["ss"], 1)
            pe.wait_ge(s["unit"], 1)
            pe.matmul(gq_ps[:, :], m.gq_blk, m.qh, start=True, stop=True).then_inc(s["gate"], 1)
            pe.wait_ge(s["unit"], 2)
            for kt in range(KT):
                mm = pe.matmul(gk_ps[:, kt * P:(kt + 1) * P], m.kh[:, kt * P:(kt + 1) * P], m.gk_blk,
                               start=True, stop=True)
            mm.then_inc(s["gate"], 1)
            pe.wait_ge(s["vp"], 1)
            for kt in range(KT):
                mm = pe.matmul(acc[:, :], m.vp[:, kt * P:(kt + 1) * P], m.ones, start=(kt == 0), stop=False,
                               skip_group_check=True)
            mm.then_inc(s["pv"], 1)
            pe.wait_ge(s["th"], 2)

            def scores(i):
                h, u = pairs[i]
                pe.wait_ge(s["km"], h + 1)
                if i >= 3:
                    pe.wait_ge(s["tanh"], i - 2)
                for j in range(2):
                    kt = 2 * u + j
                    mm = pe.matmul(m.ps2[i % 3][:, j, :], m.km[:, h % 3, kt * P:(kt + 1) * P], m.qh,
                                   start=True, stop=True)
                mm.then_inc(s["score"], 1)

            def values(i):
                h, u = pairs[i]
                pe.wait_ge(s["tanh"], i + 1)
                pe.wait_ge(s["vbd"], KT)
                for j in range(2):
                    mm = pe.matmul(acc[:, :], m.vbd[:, 2 * u + j, h * P:(h + 1) * P], m.tanh[:, i % 3, j, :],
                                   start=False, stop=(i == NI - 1 and j == 1), skip_group_check=True)
                mm.then_inc(s["pv"], 1)

            for i in range(NI + 2):
                if i < NI:
                    scores(i)
                if i >= 2:
                    values(i - 2)
            pe.wait_ge(s["fused"], 1)
            pe.matmul(q_ps[:, :], m.w_o0, m.fused, start=True, stop=True).then_inc(s["wo"], 1)


def load_layer(nc, m, d, layer):
    with stage(nc, "layer", "loaded", "made") as (block, s):
        loads = [
            (m.wqkv, d["p_Wqkv"][layer, :, :]),
            (m.wo, d["L0_ffn_Wo"][layer, :, :].rearrange("(k p) d -> p k d", p=P)),
            (m.w1, d["L0_ffn_W1"][layer, :, :]),
            (m.w2, d["p_W2"][layer, :, :].rearrange("(k p) d -> p k d", p=P)),
            (m.b1, d["p_b1"][layer, :, :]), (m.lnp, d["p_lnp"][layer, :, :]), (m.qks, d["p_qks"][layer, :, :]),
        ]

        @block.sync
        def _(sp):
            for dst, src in loads:
                sp.dma_start(dst, src).then_inc(s["loaded"], 16)

        @block.vector
        def _(dve):
            dve.wait_ge(s["loaded"], 16 * len(loads))
            for i in range(4):
                dve.tensor_scalar(m.rot[:, i, :], m.rot0[:, i, :], m.qks[:, i // 2:i // 2 + 1], QK_SCALE if i < 2 else 1.0,
                                  ALU.mult, ALU.mult).then_inc(s["made"], 1)


def local_attention(nc, m, b):
    here = bass.ds(b * T, T)
    half = D // 2
    NU = 2 * (HL // 2)
    UG = NU // G4
    NV = 2 * NQ
    items = [(g, j) for g in range(G4) for j in range(NQ)]
    NI = len(items)
    NS = 3
    with stage(nc, "loc", "xs", "ones", "v", "vev", "a", "sq", "ss", "sd", "t1", "t2", "swap0", "swap1", "swap2", "sum", "rn", "part",
               "rt", "rtev", "bc", "unit", "score", "nm", "exp", "turn", "pta", "ptd", "pv", "ri", "norm", "at", "atev",
               "wo", "out") as (block, s):
        a_ps, n_ps, v_ps = m.ps[0:3], m.ps[4], m.ps[5:8]
        s_ps, bc_ps, pt_ps, pv_ps, at_ps = m.ps[0:NS], m.ps[3], m.ps[4:6], m.ps[6], m.ps[7]
        o_ps = bc_ps
        rt_ps = bc_ps.bitcast(BF16)[0:3 * 2 * NU, 0:T]

        def keys(j):
            return QT[j] + WIN

        def swap(n):
            return f"swap{n % 3}"

        def rows(a):
            return slice(a * HDL, (a + 1) * HDL)

        def by_act(i):
            return i % 2 == 1

        def unit_at(i):
            g, j = items[i]
            return UG * (g + 1) + j if j < UG and g + 1 < G4 else None

        @block.vector
        def _(dve):
            dve.tensor_copy(m.xs[0:half, WIN:], m.xn[0:half, here]).then_inc(s["xs"], 1)
            dve.tensor_copy(m.xs[half:D, WIN + 1:], m.xn[half:D, bass.ds(b * T, T - 1)]).then_inc(s["xs"], 1)

            for n in range(NU):
                z = n % 2
                dve.wait_ge(s["sq"], n + 1)
                if n >= 3:
                    dve.wait_ge(s[swap(n)], 32 * (n // 3))
                dve.tensor_tensor(m.t2[:, n % 3, :], a_ps[n % 3], m.rot[:, 2 * z + 1, :], ALU.mult)\
                   .then_inc(s["t2"], 1)
                if n >= 3:
                    dve.wait_ge(s["sum"], n - 2)
                dve.tensor_tensor(m.t1[:, n % 3, :], a_ps[n % 3], m.rot[:, 2 * z, :], ALU.mult).then_inc(s["t1"], 1)
            dve.wait_ge(s["sd"], 1)
            dve.reciprocal(m.rn, m.nrm).then_inc(s["rn"], 1)
            dve.wait_ge(s["rn"], 1)
            dve.tensor_scalar(m.rn, m.rn, NORM_MAX, None, ALU.min).then_inc(s["rn"], 1)
            for i in range(3):
                dve.wait_ge(s["rn"], 2 + i)
                dve.tensor_copy(m.parts[:, :, i, :], m.rn).then_inc(s["part"], 1)
                if i < 2:
                    dve.wait_ge(s["part"], i + 1)
                    dve.tensor_tensor(m.rn, m.rn, m.parts[:, :, i, :], ALU.subtract).then_inc(s["rn"], 1)
            dve.wait_ge(s["rt"], 1)
            dve.tensor_copy(m.rnT, rt_ps).then_inc(s["rtev"], 1)

            def scale(n):
                p, z = n // 2, n % 2
                dve.wait_ge(s["bc"], n + 1)
                dve.wait_ge(s["sum"], n + 1)
                if z == 0:
                    dve.tensor_tensor(m.qr[:, p, :], bc_ps, m.qr[:, p, :], ALU.mult).then_inc(s["unit"], 2)
                    return
                for a in (1, 0):
                    dve.scalar_tensor_tensor(out=m.kz[:, p, a, WIN:], in0=bc_ps, scalar=m.heads[:, a:a + 1],
                                             in1=m.kz[:, p, 0, WIN:], op0=ALU.mult, op1=ALU.mult)\
                       .then_inc(s["unit"], 1)

            def negmax(i):
                g, j = items[i]
                q, k = QT[j], keys(j)
                dve.wait_ge(s["score"], i + 1)
                if i >= NS:
                    dve.wait_ge(s["exp"], i - NS + 1)
                dve.tensor_reduce(m.nm[0:q, i % NS, :], s_ps[i % NS][0:q, 0:4 * k].rearrange("p (h k) -> p h k", h=4),
                                  AX.X, ALU.max, negate=True).then_inc(s["nm"], 1)

            def probs_t(i):
                g, j = items[i]
                q, k = QT[j], keys(j)
                if by_act(i):
                    return
                dve.wait_ge(s["turn"], i + 1)
                if i >= 2:
                    dve.wait_ge(s["pv"], i - 1)
                dve.tensor_copy(m.pt[0:k, i % 2, 0:4 * q], pt_ps[i % 2][0:k, 0:4 * q]).then_inc(s["ptd"], 1)

            def normed(i):
                g, j = items[i]
                q = QT[j]
                pv = pv_ps[0:q, 0:4 * (HDL + 1)].rearrange("p (h c) -> p h c", h=4)
                dve.wait_ge(s["pv"], i + 1)
                dve.reciprocal(m.ri[0:q, i % 2, :], pv[:, :, HDL]).then_inc(s["ri"], 1)
                dve.wait_ge(s["ri"], i + 1)
                if i >= 2:
                    dve.wait_ge(s["at"], i - 1)
                dve.tensor_tensor(m.an[0:q, i % 2, :].rearrange("p (h c) -> p h c", h=4), pv[:, :, 0:HDL],
                                  m.ri[0:q, i % 2, :].unsqueeze(2).to_broadcast([q, 4, HDL]), ALU.mult)\
                   .then_inc(s["norm"], 1)

            for n in range(UG):
                scale(n)
            for i in range(NI + 3):
                if i < NI:
                    negmax(i)
                if 2 <= i < NI + 2:
                    probs_t(i - 2)
                if i >= 3:
                    normed(i - 3)
                if i < NI and unit_at(i) is not None:
                    scale(unit_at(i))
            dve.wait_ge(s["wo"], HL // 2)
            dve.tensor_tensor(m.xn[:, here], o_ps, m.xn[:, here], ALU.add).then_inc(s["out"], 1)

        @block.sync
        def _(sp):
            for n in range(NU):
                sp.wait_ge(s["t2"], n + 1)
                if n >= 3:
                    sp.wait_ge(s["sum"], n - 2)
                for a in range(2):
                    sp.dma_start(m.t3[rows(a), n % 3, :], m.t2[rows(1 - a), n % 3, :]).then_inc(s[swap(n)], 16)

        @block.gpsimd
        def _(pool):
            pool.memset(m.v[:, :, :, HDL:HDL + 1], 1.0).then_inc(s["ones"], 1)
            for n in range(NU):
                p, z = n // 2, n % 2
                pool.wait_ge(s["t1"], n + 1)
                pool.wait_ge(s[swap(n)], 32 * (n // 3 + 1))
                if n:
                    pool.wait_ge(s["sum"], n)
                out = m.qr[:, p, :] if z == 0 else m.kz[:, p, 0, WIN:]
                pool.tensor_tensor(out, m.t1[:, n % 3, :], m.t3[:, n % 3, :], ALU.add).then_inc(s["sum"], 1)

        @block.scalar
        def _(act):
            for n in range(NU):
                act.wait_ge(s["a"], n + 1)
                if n >= 2:
                    act.wait_ge(s["ss"], n - 1)
                act.activation(m.sq[:, n % 2, :], a_ps[n % 3], ACT.Square).then_inc(s["sq"], 1)
            act.wait_ge(s["ss"], NU)
            act.activation(m.nrm, n_ps[:, 0:KT * 2 * NU].rearrange("p (t u) -> p t u", t=KT), ACT.Sqrt,
                           bias=m.zcol).then_inc(s["sd"], 1)
            for i in range(NV):
                j, c = i // 2, i % 2
                k = keys(j)
                act.wait_ge(s["v"], i + 1)
                act.activation(m.v[0:k, j, 8 * c:8 * c + 8, 0:HDL],
                               v_ps[i % 3][0:k, :].rearrange("p (h c) -> p h c", h=8), ACT.Copy).then_inc(s["vev"], 1)

            def turned_rows(i):
                g, j = items[i]
                q = QT[j]
                act.wait_ge(s["at"], i + 1)
                act.activation(m.attnT[:, 2 * g:2 * g + 2, QW * j:QW * j + q],
                               at_ps[:, 0:2 * q].rearrange("p (k q) -> p k q", k=2), ACT.Copy).then_inc(s["atev"], 1)

            def probs_t(i):
                g, j = items[i]
                q, k = QT[j], keys(j)
                if not by_act(i):
                    return
                act.wait_ge(s["turn"], i + 1)
                if i >= 2:
                    act.wait_ge(s["pv"], i - 1)
                act.activation(m.pt[0:k, i % 2, 0:4 * q], pt_ps[i % 2][0:k, 0:4 * q], ACT.Copy).then_inc(s["pta"], 1)

            for i in range(NI + 4):
                if i < NI:
                    g, j = items[i]
                    q, k = QT[j], keys(j)
                    act.wait_ge(s["nm"], i + 1)
                    if i == 0:
                        act.wait_ge(s["sum"], NU)
                    if i >= NS:
                        act.wait_ge(s["turn"], i - NS + 1)
                    for h in range(4):
                        last = act.activation(m.pr[0:q, i % NS, h * k:(h + 1) * k], s_ps[i % NS][0:q, h * k:(h + 1) * k],
                                              ACT.Exp, bias=m.nm[0:q, i % NS, h:h + 1])
                    last.then_inc(s["exp"], 1)
                if 2 <= i < NI + 2:
                    probs_t(i - 2)
                if i >= 4:
                    turned_rows(i - 4)

        @block.tensor
        def _(pe):
            def v_proj(i):
                j, c = i // 2, i % 2
                k = keys(j)
                if i >= 3:
                    pe.wait_ge(s["vev"], i - 2)
                pe.matmul(v_ps[i % 3][0:k, :], m.xs[:, QW * j:QW * j + k],
                          m.wqkv[:, 2 * INNER + 512 * c:2 * INNER + 512 * (c + 1)], start=True, stop=True)\
                  .then_inc(s["v"], 1)

            def sums(n):
                pe.wait_ge(s["sq"], n + 1)
                for t in range(KT):
                    c = (t * NU + n) * 2
                    mm = pe.matmul(n_ps[:, c:c + 2], m.sq[:, n % 2, t * P:(t + 1) * P], m.heads,
                                   start=True, stop=True)
                mm.then_inc(s["ss"], 1)

            pe.wait_ge(s["xs"], 2)
            for n in range(NU):
                p, z = n // 2, n % 2
                col = z * INNER + p * P
                if n >= 3:
                    pe.wait_ge(s["t1"], n - 2)
                pe.matmul(a_ps[n % 3], m.wqkv[:, col:col + P], m.xs[:, WIN:], start=True, stop=True)\
                  .then_inc(s["a"], 1)
                if n:
                    sums(n - 1)
            sums(NU - 1)
            for i in range(3):
                v_proj(i)
            pe.wait_ge(s["part"], 3)
            for t in range(KT):
                mm = pe.transpose(rt_ps[:, t * P:(t + 1) * P], m.parts[:, t, :, :].rearrange("p a u -> p (a u)"),
                                  m.ident16)
            mm.then_inc(s["rt"], 1)

            def spread(n):
                if n:
                    pe.wait_ge(s["unit"], 2 * n)
                pe.matmul(bc_ps, m.spread[:, n, :], m.rnT, start=True, stop=True).then_inc(s["bc"], 1)

            def scores(i):
                g, j = items[i]
                q, k = QT[j], keys(j)
                if j == 0:
                    pe.wait_ge(s["unit"], 2 * UG * (g + 1))
                if i >= NS:
                    pe.wait_ge(s["exp"], i - NS + 1)
                mask = m.mlocal[0:q, 0 if j == 0 else 1, :].rearrange("p (h k) -> p h k", h=4)[:, :, 0:k]
                pe.matmul(s_ps[i % NS][0:q, 0:4 * k], m.ident16[0:q, 0:q], mask, start=True, stop=False,
                          skip_group_check=True)
                for h in range(4):
                    p = 2 * g + h // 2
                    mm = pe.matmul(s_ps[i % NS][0:q, h * k:(h + 1) * k], m.qr[:, p, QW * j:QW * j + q],
                                   m.kz[:, p, h % 2, QW * j:QW * j + k], start=False, stop=(h == 3),
                                   skip_group_check=True)
                mm.then_inc(s["score"], 1)

            def copied(i):
                pe.wait_ge(s["pta"] if by_act(i) else s["ptd"], i // 2 + 1)

            def turn(i):
                g, j = items[i]
                q, k = QT[j], keys(j)
                pe.wait_ge(s["exp"], i + 1)
                if i >= 2:
                    copied(i - 2)
                for h in range(4):
                    mm = pe.transpose(pt_ps[i % 2][0:k, h * q:(h + 1) * q], m.pr[0:q, i % NS, h * k:(h + 1) * k],
                                      m.ident[0:q, 0:q])
                mm.then_inc(s["turn"], 1)

            def values(i):
                g, j = items[i]
                q, k = QT[j], keys(j)
                copied(i)
                if i == 0:
                    pe.wait_ge(s["ones"], 1)
                else:
                    pe.wait_ge(s["norm"], i)
                for h in range(4):
                    mm = pe.matmul(pv_ps[0:q, h * (HDL + 1):(h + 1) * (HDL + 1)],
                                   m.pt[0:k, i % 2, h * q:(h + 1) * q], m.v[0:k, j, 4 * g + h, :],
                                   start=True, stop=True)
                mm.then_inc(s["pv"], 1)

            def turn_rows(i):
                g, j = items[i]
                q = QT[j]
                pe.wait_ge(s["norm"], i + 1)
                if i:
                    pe.wait_ge(s["atev"], i)
                for k in range(2):
                    mm = pe.transpose(at_ps[:, k * q:(k + 1) * q], m.an[0:q, i % 2, k * P:(k + 1) * P],
                                      m.ident[0:q, 0:q])
                mm.then_inc(s["at"], 1)

            def project(kp):
                if kp == 0:
                    pe.wait_ge(s["unit"], 2 * NU)
                pe.wait_ge(s["atev"], NQ * (kp // 2 + 1))
                pe.matmul(o_ps, m.wo[:, kp, :], m.attnT[:, kp, :], start=(kp == 0), stop=(kp == HL // 2 - 1),
                          skip_group_check=True).then_inc(s["wo"], 1)

            pe.wait_ge(s["rtev"], 1)
            for n in range(UG):
                spread(n)
                for i in (3 + 2 * n, 4 + 2 * n):
                    v_proj(i)
            v_proj(NV - 1)
            pe.wait_ge(s["vev"], NV)
            for i in range(NI + 4):
                if i < NI:
                    scores(i)
                if 2 <= i < NI + 2:
                    turn(i - 2)
                if 3 <= i < NI + 3:
                    values(i - 3)
                if i >= 4:
                    turn_rows(i - 4)
                if i < NI and unit_at(i) is not None:
                    spread(unit_at(i))
                if 0 <= i - (G4 - 1) * NQ < HL // 2 - 2:
                    project(i - (G4 - 1) * NQ)
            for kp in range(HL // 2 - 2, HL // 2):
                project(kp)


def feed_forward(nc, m):
    half = D // 2
    NK = len(FK)
    NU = B * NK
    with stage(nc, "ffn", "zero", "xs", "g", "a", "ge", "h", "w2", "out", *NORM_SEMS) as (block, s):
        cs = [slice(c * T, (c + 1) * T) for c in range(B)]
        acc = m.ps[4:6]

        @block.tensor
        def _(pe):
            norm_pe(pe, m, s, lambda c: m.xsh[:, c % 2, :], lambda c: pe.wait_ge(s["xs"], 2 * c + 2))

            def up(u):
                c, k = divmod(u, NK)
                f = FK[k]
                if u == 0:
                    pe.wait_ge(s["ln"], B)
                    pe.wait_ge(s["sd"], B)
                if u >= 2:
                    pe.wait_ge(s["ge"], u - 1)
                pe.matmul(m.ps[u % 2][0:f, :], m.w1[:, DIN + k * P:DIN + k * P + f], m.xq[:, cs[c]],
                          start=True, stop=True).then_inc(s["g"], 1)
                if u >= 2:
                    pe.wait_ge(s["h"], u - 1)
                pe.matmul(m.ps[2 + u % 2][0:f, :], m.w1[:, k * P:k * P + f], m.xq[:, cs[c]],
                          start=True, stop=True).then_inc(s["a"], 1)

            def down(u):
                c, k = divmod(u, NK)
                f = FK[k]
                pe.wait_ge(s["h"], u + 1)
                if k == 0 and c >= 2:
                    pe.wait_ge(s["out"], c - 1)
                pe.matmul(acc[c % 2][:, :], m.w2[0:f, k, :], m.hid[0:f, u % 3, :], start=(k == 0),
                          stop=(k == NK - 1)).then_inc(s["w2"], 1)

            for u in range(NU + 2):
                if u < NU:
                    up(u)
                if u >= 2:
                    down(u - 2)

        @block.scalar
        def _(act):
            norm_act(act, m, s)
            for u in range(NU):
                k = u % NK
                f = FK[k]
                act.wait_ge(s["g"], u + 1)
                if u >= 2:
                    act.wait_ge(s["h"], u - 1)
                act.activation(m.ge[0:f, u % 2, :], m.ps[u % 2][0:f, :], ACT.Gelu, bias=m.b1[0:f, NK + k:NK + k + 1])\
                   .then_inc(s["ge"], 1)

        @block.vector
        def _(dve):
            dve.memset(m.xsh[:, :, 0:1], 0.0).then_inc(s["zero"], 1)

            def shifted(c):
                if c >= 2:
                    dve.wait_ge(s["xc"], c - 1)
                    dve.wait_ge(s["mean"], c - 1)
                if c == 0:
                    dve.wait_ge(s["zero"], 1)
                dve.tensor_copy(m.xsh[0:half, c % 2, :], m.xn[0:half, cs[c]]).then_inc(s["xs"], 1)
                dve.tensor_copy(m.xsh[half:D, c % 2, 1:T], m.xn[half:D, c * T:(c + 1) * T - 1]).then_inc(s["xs"], 1)
                dve.wait_ge(s["xs"], 2 * c + 2)

            norm_dve(dve, m, s, lambda c: m.xsh[:, c % 2, :], m.xq, m.lnp[:, 0:1], m.lnp[:, 1:2], before=shifted)

            def out(c):
                dve.wait_ge(s["w2"], NK * (c + 1))
                dve.scalar_tensor_tensor(out=m.xn[:, cs[c]], in0=acc[c % 2][:, :], scalar=m.lnp[:, 2:3],
                                         in1=m.xn[:, cs[c]], op0=ALU.add, op1=ALU.add).then_inc(s["out"], 1)

            for u in range(NU):
                c, k = divmod(u, NK)
                f = FK[k]
                dve.wait_ge(s["ge"], u + 1)
                dve.wait_ge(s["a"], u + 1)
                if u >= 3:
                    dve.wait_ge(s["w2"], u - 2)
                dve.scalar_tensor_tensor(out=m.hid[0:f, u % 3, :], in0=m.ps[2 + u % 2][0:f, :],
                                         scalar=m.b1[0:f, k:k + 1], in1=m.ge[0:f, u % 2, :],
                                         op0=ALU.add, op1=ALU.mult).then_inc(s["h"], 1)
                if k == 2 and c:
                    out(c - 1)
            out(B - 1)


def latent_attention(nc, m, b):
    here = bass.ds(b * T, T)
    NP_ = H1 // 2
    items = [(qt, h) for qt in range(KT) for h in range(H1)]
    NI = len(items)
    V0 = HDT
    with stage(nc, "lat", "xin", "lat", "latc", "v", "vev", "q", "qev", "k", "kev", "score", "nm", "exp", "turn",
               "pta", "ptd", "pv", "ri", "norm", "at", "atev", "wo", "out") as (block, s):
        a_ps, b_ps, v_ps = m.ps[0:2], m.ps[2:4], m.ps[4:6]
        s_ps, pt_ps, pv_ps, at_ps = m.ps[0:3], m.ps[3:5], m.ps[5:7], m.ps[7]
        NV = 2 * KT

        def by_act(i):
            return i % 2 == 0

        @block.vector
        def _(dve):
            dve.tensor_copy(m.xn_b, m.xn[:, here]).then_inc(s["xin"], 1)
            for p in range(NP_):
                dve.wait_ge(s["k"], p + 1)
                for a in range(2):
                    r = slice(a * HD1, (a + 1) * HD1)
                    last = dve.tensor_copy(m.k1[r, p, a, :], b_ps[p % 2][r, :])
                last.then_inc(s["kev"], 1)

            def negmax(i):
                qt, h = items[i]
                dve.wait_ge(s["score"], i + 1)
                if i >= 3:
                    dve.wait_ge(s["exp"], i - 2)
                dve.tensor_reduce(m.nm[:, i % 3:i % 3 + 1], s_ps[i % 3][:, 0:(qt + 1) * P], AX.X, ALU.max,
                                  negate=True).then_inc(s["nm"], 1)

            def probs_t(i):
                qt, h = items[i]
                if by_act(i):
                    return
                dve.wait_ge(s["turn"], i + 1)
                if i >= 3:
                    dve.wait_ge(s["pv"], i - 2)
                dve.tensor_copy(m.pt[:, i % 3, 0:(qt + 1) * P], pt_ps[i % 2][:, 0:(qt + 1) * P]).then_inc(s["ptd"], 1)

            def normed(g):
                qt, h = items[4 * g]
                pv = pv_ps[g % 2][:, 0:4 * (HD1 + 1)].rearrange("p (h c) -> p h c", h=4)
                dve.wait_ge(s["pv"], 4 * g + 4)
                dve.reciprocal(m.ri[:, g % 2, :], pv[:, :, HD1]).then_inc(s["ri"], 1)
                dve.wait_ge(s["ri"], g + 1)
                if h == 0 and qt >= 2:
                    dve.wait_ge(s["at"], 2 * (qt - 1))
                dve.tensor_tensor(m.an[:, qt % 2, h * HD1:(h + 4) * HD1].rearrange("p (h c) -> p h c", h=4),
                                  pv[:, :, 0:HD1], m.ri[:, g % 2, :].unsqueeze(2).to_broadcast([P, 4, HD1]),
                                  ALU.mult).then_inc(s["norm"], 1)

            for i in range(NI + 4):
                if i < NI:
                    negmax(i)
                if 2 <= i < NI + 2:
                    probs_t(i - 2)
                if i >= 4 and (i - 4) % 4 == 3:
                    normed((i - 4) // 4)
            dve.wait_ge(s["wo"], 1)
            dve.tensor_tensor(m.xsum[:, here], m.ps[0], m.xsum[:, here], ALU.add).then_inc(s["out"], 1)

        @block.scalar
        def _(act):
            act.wait_ge(s["lat"], 1)
            act.activation(m.lat, m.ps[7], ACT.Copy).then_inc(s["latc"], 1)
            for p in range(NP_):
                act.wait_ge(s["q"], p + 1)
                act.activation(m.q1[:, p, :], a_ps[p % 2], ACT.Copy, scale=float(HD1) ** -0.5).then_inc(s["qev"], 1)
                act.wait_ge(s["v"], p + 1)
                kt, c = p // 2, p % 2
                act.activation(m.v1[:, kt, 8 * c:8 * c + 8, 0:HD1], v_ps[p % 2].rearrange("p (h c) -> p h c", h=8),
                               ACT.Copy).then_inc(s["vev"], 1)

            def probs_t(i):
                qt, h = items[i]
                if not by_act(i):
                    return
                act.wait_ge(s["turn"], i + 1)
                if i >= 3:
                    act.wait_ge(s["pv"], i - 2)
                act.activation(m.pt[:, i % 3, 0:(qt + 1) * P], pt_ps[i % 2][:, 0:(qt + 1) * P], ACT.Copy)\
                   .then_inc(s["pta"], 1)

            def turned_rows(qt):
                for c in range(2):
                    act.wait_ge(s["at"], 2 * qt + c + 1)
                    act.activation(m.attnT[:, 4 * c:4 * c + 4, qt * P:(qt + 1) * P],
                                   at_ps.rearrange("p (k q) -> p k q", k=4), ACT.Copy).then_inc(s["atev"], 1)

            for i in range(NI + 2):
                if i < NI:
                    qt, h = items[i]
                    act.wait_ge(s["nm"], i + 1)
                    if i >= 3:
                        act.wait_ge(s["turn"], i - 2)
                    act.activation(m.pr[:, i % 3, 0:(qt + 1) * P], s_ps[i % 3][:, 0:(qt + 1) * P], ACT.Exp,
                                   bias=m.nm[:, i % 3:i % 3 + 1]).then_inc(s["exp"], 1)
                if i >= 2:
                    probs_t(i - 2)
                if i % H1 == 7 and i > H1:
                    turned_rows(i // H1 - 1)
            turned_rows(KT - 1)

        @block.tensor
        def _(pe):
            pe.wait_ge(s["xin"], 1)
            pe.matmul(m.ps[7], m.w_kvd, m.xn_b, start=True, stop=True).then_inc(s["lat"], 1)
            pe.wait_ge(s["latc"], 1)
            for p in range(NP_):
                if p >= 2:
                    pe.wait_ge(s["qev"], p - 1)
                pe.matmul(a_ps[p % 2], m.w_q1[:, p * P:(p + 1) * P], m.xn_b, start=True, stop=True).then_inc(s["q"], 1)
                if p >= 2:
                    pe.wait_ge(s["kev"], p - 1)
                pe.matmul(b_ps[p % 2], m.w_kvu[:, p * P:(p + 1) * P], m.lat, start=True, stop=True).then_inc(s["k"], 1)
                if p >= 2:
                    pe.wait_ge(s["vev"], p - 1)
                kt, c = p // 2, p % 2
                pe.matmul(v_ps[p % 2], m.lat[:, kt * P:(kt + 1) * P], m.w_kvu[:, V0 + 512 * c:V0 + 512 * (c + 1)],
                          start=True, stop=True).then_inc(s["v"], 1)

            def scores(i):
                qt, h = items[i]
                nk = (qt + 1) * P
                if i == 0:
                    pe.wait_ge(s["qev"], NP_)
                    pe.wait_ge(s["kev"], NP_)
                    pe.wait_ge(s["vev"], NV)
                if i >= 3:
                    pe.wait_ge(s["exp"], i - 2)
                pe.matmul(s_ps[i % 3][:, 0:nk], m.q1[:, h // 2, qt * P:(qt + 1) * P], m.k1[:, h // 2, h % 2, 0:nk],
                          start=True, stop=False, skip_group_check=True)
                pe.matmul(s_ps[i % 3][:, qt * P:nk], m.ident16, m.mcausal, start=False, stop=True,
                          skip_group_check=True).then_inc(s["score"], 1)

            def copied(i):
                pe.wait_ge(s["pta"] if by_act(i) else s["ptd"], i // 2 + 1)

            def turn(i):
                qt, h = items[i]
                pe.wait_ge(s["exp"], i + 1)
                if i >= 2:
                    copied(i - 2)
                for kt in range(qt + 1):
                    mm = pe.transpose(pt_ps[i % 2][:, kt * P:(kt + 1) * P], m.pr[:, i % 3, kt * P:(kt + 1) * P],
                                      m.ident)
                mm.then_inc(s["turn"], 1)

            def values(i):
                qt, h = items[i]
                copied(i)
                if h % 4 == 0 and i >= 8:
                    pe.wait_ge(s["norm"], i // 4 - 1)
                c = h % 4 * (HD1 + 1)
                for kt in range(qt + 1):
                    mm = pe.matmul(pv_ps[i // 4 % 2][:, c:c + HD1 + 1], m.pt[:, i % 3, kt * P:(kt + 1) * P], m.v1[:, kt, h, :],
                                   start=(kt == 0), stop=(kt == qt), skip_group_check=True)
                mm.then_inc(s["pv"], 1)

            def turn_rows(qt):
                pe.wait_ge(s["norm"], 4 * qt + 4)
                for c in range(2):
                    if qt or c:
                        pe.wait_ge(s["atev"], 2 * qt + c)
                    for k in range(4):
                        kp = 4 * c + k
                        mm = pe.transpose(at_ps[:, k * P:(k + 1) * P], m.an[:, qt % 2, kp * P:(kp + 1) * P], m.ident)
                    mm.then_inc(s["at"], 1)

            for i in range(NI + 3):
                if i < NI:
                    scores(i)
                if 2 <= i < NI + 2:
                    turn(i - 2)
                if i >= 3:
                    values(i - 3)
                if i % H1 == 7 and i > H1:
                    turn_rows(i // H1 - 1)
            turn_rows(KT - 1)
            pe.wait_ge(s["atev"], 2 * KT)
            for kp in range(NP_):
                mm = pe.matmul(m.ps[0], m.w_o1[:, kp, :], m.attnT[:, kp, :], start=(kp == 0), stop=(kp == NP_ - 1))
            mm.then_inc(s["wo"], 1)


def load_latent(nc, m, d):
    loads = [(m.w_kvd, d["L1_attn_w_kv_down"]), (m.w_kvu, d["L1_attn_w_kv_up"]), (m.w_q1, d["L1_attn_w_q"]),
             (m.w_o1, d["L1_attn_w_out"].rearrange("(k p) d -> p k d", p=P))]
    with stage(nc, "lload", "loaded", "set") as (block, s):
        @block.sync
        def _(sp):
            for dst, src in loads:
                sp.dma_start(dst, src).then_inc(s["loaded"], 16)
            sp.wait_ge(s["loaded"], 16 * len(loads))

        @block.vector
        def _(dve):
            dve.memset(m.k1, 0.0)
            dve.memset(m.v1, 1.0).then_inc(s["set"], 1)


def token_rows(nc, m, src, dst, label):
    with stage(nc, label, "turned", "kept") as (block, s):
        @block.tensor
        def _(pe):
            for c in range(B):
                if c >= 4:
                    pe.wait_ge(s["kept"], c - 3)
                for t in range(KT):
                    mm = pe.transpose(m.ps[c % 4][:, t * P:(t + 1) * P], src[:, c * T + t * P:c * T + (t + 1) * P],
                                      m.ident)
                mm.then_inc(s["turned"], 1)

        @block.vector
        def _(dve):
            for c in range(B):
                dve.wait_ge(s["turned"], c + 1)
                dve.tensor_copy(dst[:, c * KT:(c + 1) * KT, :].rearrange("p t d -> p (t d)"), m.ps[c % 4])\
                   .then_inc(s["kept"], 1)


def token_stats(nc, m):
    with stage(nc, "stats", "dve", "sq", "root") as (block, s):
        st = lambda i: m.stats[:, :, i]
        mean_b = m.stats[:, :, 0:1].to_broadcast([P, NT, D])

        @block.vector
        def _(dve):
            dve.tensor_reduce(st(0), m.xr, AX.X, ALU.add).then_inc(s["dve"], 1)
            dve.tensor_reduce(st(2), m.xr, AX.X, ALU.min).then_inc(s["dve"], 1)
            dve.tensor_reduce(st(3), m.xr, AX.X, ALU.max).then_inc(s["dve"], 1)
            dve.wait_ge(s["sq"], 1)
            dve.tensor_reduce(m.red[:, 0, :], m.sqr, AX.X, ALU.add).then_inc(s["dve"], 1)
            dve.wait_ge(s["dve"], 4)
            dve.tensor_scalar(st(0), st(0), 1.0 / D, None, ALU.mult).then_inc(s["dve"], 1)
            dve.tensor_scalar(m.sqr, m.xr, 1e-6, None, ALU.is_lt).then_inc(s["dve"], 1)
            dve.wait_ge(s["dve"], 6)
            dve.scalar_tensor_tensor(out=m.sqr, in0=m.xr, scalar=-1e-6, in1=m.sqr, op0=ALU.is_gt, op1=ALU.mult)\
               .then_inc(s["dve"], 1)
            dve.wait_ge(s["dve"], 7)
            dve.tensor_reduce(st(5), m.sqr, AX.X, ALU.add).then_inc(s["dve"], 1)
            dve.wait_ge(s["dve"], 8)
            dve.tensor_scalar(st(5), st(5), 1.0 / D, None, ALU.mult).then_inc(s["dve"], 1)
            dve.tensor_tensor(m.sqr, m.xr, mean_b, ALU.subtract).then_inc(s["dve"], 1)
            dve.wait_ge(s["sq"], 2)
            dve.tensor_reduce(m.red[:, 1, :], m.sqr, AX.X, ALU.add).then_inc(s["dve"], 1)

        @block.scalar
        def _(act):
            act.activation(m.sqr, m.xr, ACT.Square).then_inc(s["sq"], 1)
            act.wait_ge(s["dve"], 10)
            act.activation(m.sqr, m.sqr, ACT.Square).then_inc(s["sq"], 1)
            act.activation(st(4), m.red[:, 0, :], ACT.Sqrt, bias=m.zcol).then_inc(s["root"], 1)
            act.wait_ge(s["dve"], 11)
            act.activation(st(1), m.red[:, 1, :], ACT.Sqrt, bias=m.zcol, scale=1.0 / (D - 1)).then_inc(s["root"], 1)


def router(nc, m, d):
    with stage(nc, "router", "w", "st", "stev", "h", "hid", "lg", "lgev", "nm", "sub", "exp", "sum", "ri",
               "probs") as (block, s):
        loads = [(m.r1, d["p_r1"]), (m.r1s, d["p_r1s"]), (m.r1b, d["p_r1b"]), (m.r2, d["p_r2"])]

        @block.sync
        def _(sp):
            for dst, src in loads:
                sp.dma_start(dst, src).then_inc(s["w"], 16)

        @block.tensor
        def _(pe):
            for c in range(B):
                if c >= 2:
                    pe.wait_ge(s["stev"], c - 1)
                for t in range(KT):
                    mm = pe.transpose(m.ps[c % 2][0:NSTAT, t * P:(t + 1) * P], m.stats[:, c * KT + t, :], m.ident)
                mm.then_inc(s["st"], 1)
            pe.wait_ge(s["w"], 16 * len(loads))

            def logits(c):
                pe.wait_ge(s["hid"], c + 1)
                for t in range(KT):
                    i = c * KT + t
                    mm = pe.matmul(m.ps[4 + i // 16][:, i % 16 * E:(i % 16 + 1) * E], m.rh[:, c % 2, t * P:(t + 1) * P],
                                   m.r2, start=True, stop=True)
                mm.then_inc(s["lg"], 1)

            for c in range(B):
                if c >= 2:
                    pe.wait_ge(s["hid"], c - 1)
                pe.wait_ge(s["stev"], c + 1)
                pe.matmul(m.ps[2 + c % 2][0:RH, :], m.r1, m.xn[:, c * T:(c + 1) * T], start=True, stop=False)
                pe.matmul(m.ps[2 + c % 2][0:RH, :], m.r1s, m.statT[:, c * T:(c + 1) * T], start=False, stop=True)\
                  .then_inc(s["h"], 1)
                if c:
                    logits(c - 1)
            logits(B - 1)

        @block.scalar
        def _(act):
            for c in range(B):
                act.wait_ge(s["h"], c + 1)
                if c >= 2:
                    act.wait_ge(s["lg"], c - 1)
                act.activation(m.rh[:, c % 2, :], m.ps[2 + c % 2][0:RH, :], ACT.Gelu, bias=m.r1b).then_inc(s["hid"], 1)
            act.wait_ge(s["sub"], 1)
            act.activation(m.probs, m.probs, ACT.Exp).then_inc(s["exp"], 1)

        @block.vector
        def _(dve):
            for c in range(B):
                dve.wait_ge(s["st"], c + 1)
                dve.tensor_copy(m.statT[:, c * T:(c + 1) * T], m.ps[c % 2][0:NSTAT, :]).then_inc(s["stev"], 1)
            dve.wait_ge(s["lg"], B)
            for i in range(2):
                dve.tensor_copy(m.probs[:, 16 * i:16 * i + 16, :].rearrange("p t e -> p (t e)"), m.ps[4 + i])\
                   .then_inc(s["lgev"], 1)
            dve.wait_ge(s["lgev"], 2)
            dve.tensor_reduce(m.red[:, 0, :], m.probs, AX.X, ALU.max).then_inc(s["nm"], 1)
            dve.wait_ge(s["nm"], 1)
            over = lambda a: a.unsqueeze(2).to_broadcast([P, NT, E])
            dve.tensor_tensor(m.probs, m.probs, over(m.red[:, 0, :]), ALU.subtract).then_inc(s["sub"], 1)
            dve.wait_ge(s["exp"], 1)
            dve.tensor_reduce(m.red[:, 1, :], m.probs, AX.X, ALU.add).then_inc(s["sum"], 1)
            dve.wait_ge(s["sum"], 1)
            dve.reciprocal(m.red[:, 2, :], m.red[:, 1, :]).then_inc(s["ri"], 1)
            dve.wait_ge(s["ri"], 1)
            dve.tensor_tensor(m.probs, m.probs, over(m.red[:, 2, :]), ALU.mult).then_inc(s["probs"], 1)


def route(nc, m, d):
    S4 = N // 4
    with stage(nc, "route", "io", "top", "idx", "hot", "msk", "t", "tev", "m8", "mr", "seg", "fin", "thr", "cmp",
               "back", "bev", "sl", "w") as (block, s):
        NTOP = CAP // 8

        @block.gpsimd
        def _(pool):
            pool.iota(m.eiota, [[1, E]], base=0, channel_multiplier=0,
                      allow_small_or_imprecise_dtypes=True).then_inc(s["io"], 1)
            pool.iota(m.ebase, [[0, 1]], base=0, channel_multiplier=CAP,
                      allow_small_or_imprecise_dtypes=True).then_inc(s["io"], 1)

        @block.tensor
        def _(pe):
            pe.wait_ge(s["msk"], 1)
            for i in range(B):
                if i >= 4:
                    pe.wait_ge(s["tev"], i - 3)
                for t in range(KT):
                    mm = pe.transpose(m.ps[i % 4][0:E, t * P:(t + 1) * P], m.score[:, i * KT + t, :], m.ident)
                mm.then_inc(s["t"], 1)
            pe.wait_ge(s["sl"], 1)
            for i in range(NT):
                mm = pe.transpose(m.ps[4 + i // 16][:, i % 16 * E:(i % 16 + 1) * E], m.slotE[:, i * P:(i + 1) * P],
                                  m.ident[0:E, 0:E])
            mm.then_inc(s["back"], 1)

        @block.vector
        def _(dve):
            step = [0]

            def then(ins):
                step[0] += 1
                ins.then_inc(s["w"], 1)
                dve.wait_ge(s["w"], step[0])

            for i in range(NT):
                last = dve.max(m.top8[:, i, :], m.probs[:, i, :])
            then(last)
            for i in range(NT):
                last = dve.max_index(m.idx8[:, i, :], m.top8[:, i, :], m.probs[:, i, :])
            then(last)
            then(dve.tensor_copy(m.idxf, m.idx8[:, :, 0:2]))
            dve.wait_ge(s["io"], 2)
            es = m.eiota.unsqueeze(1).to_broadcast([P, NT, E])
            for j in range(2):
                last = dve.tensor_tensor(m.hot[:, j, :, :], es, m.idxf[:, :, j:j + 1].to_broadcast([P, NT, E]),
                                         ALU.is_equal)
            then(last)
            then(dve.tensor_tensor(m.score, m.hot[:, 0, :, :], m.hot[:, 1, :, :], ALU.add))
            then(dve.tensor_tensor(m.tmpn, m.probs, m.score, ALU.mult))
            then(dve.tensor_scalar(m.score, m.score, -1.0, None, ALU.add))
            dve.tensor_tensor(m.score, m.score, m.tmpn, ALU.add).then_inc(s["msk"], 1)
            for i in range(B):
                dve.wait_ge(s["t"], i + 1)
                dve.tensor_copy(m.scoreE[:, i * T:(i + 1) * T], m.ps[i % 4][0:E, :]).then_inc(s["tev"], 1)
            dve.wait_ge(s["tev"], B)
            for q in range(4):
                last = dve.tensor_copy(m.quart[q * E:(q + 1) * E, :], m.scoreE[:, q * S4:(q + 1) * S4])
            then(last)
            for r in range(NTOP):
                then(dve.max(m.best[:, 8 * r:8 * r + 8], m.quart))
                then(dve.match_replace(out=m.quart, in_to_replace=m.best[:, 8 * r:8 * r + 8], in_values=m.quart,
                                       imm_value=-2.0))
            for q in range(4):
                last = dve.tensor_copy(m.cand[:, q * CAP:(q + 1) * CAP], m.best[q * E:(q + 1) * E, :])
            then(last)
            for r in range(NTOP):
                then(dve.max(m.b8, m.cand))
                if r < NTOP - 1:
                    then(dve.match_replace(out=m.cand, in_to_replace=m.b8, in_values=m.cand, imm_value=-2.0))
            thr = m.b8[:, 7:8]
            then(dve.tensor_scalar(m.gt, m.scoreE, thr, None, ALU.is_gt))
            dve.tensor_scalar(m.eq, m.scoreE, thr, None, ALU.is_equal)
            then(dve.tensor_reduce(m.cnt, m.gt, AX.X, ALU.add))
            then(dve.tensor_scalar(m.room, m.cnt, -1.0, float(CAP), ALU.mult, ALU.add))
            then(dve.tensor_tensor_scan(m.run, m.eq, m.eq, 0.0, ALU.add, ALU.bypass))
            then(dve.tensor_scalar(m.run, m.run, m.room, None, ALU.is_le))
            then(dve.tensor_tensor(m.run, m.run, m.eq, ALU.mult))
            then(dve.tensor_tensor(m.gt, m.gt, m.run, ALU.add))
            then(dve.tensor_scalar(m.eq, m.scoreE, 0.0, None, ALU.is_ge))
            then(dve.tensor_tensor(m.gt, m.gt, m.eq, ALU.mult))
            then(dve.tensor_tensor_scan(m.run, m.gt, m.gt, 0.0, ALU.add, ALU.bypass))
            then(dve.tensor_scalar(m.run, m.run, m.ebase, None, ALU.add))
            dve.tensor_tensor(m.slotE, m.run, m.gt, ALU.mult).then_inc(s["sl"], 1)
            dve.wait_ge(s["back"], 1)
            for i in range(2):
                last = dve.tensor_copy(m.slotN[:, 16 * i:16 * i + 16, :].rearrange("p t e -> p (t e)"), m.ps[4 + i])
            then(last)
            for j in range(2):
                then(dve.tensor_tensor(m.tmpn, m.hot[:, j, :, :], m.slotN, ALU.mult))
                then(dve.tensor_reduce(m.slot[:, j, :], m.tmpn, AX.X, ALU.add))
            then(dve.tensor_tensor(m.red[:, 0, :], m.top8[:, :, 0], m.top8[:, :, 1], ALU.add))
            then(dve.reciprocal(m.red[:, 1, :], m.red[:, 0, :]))
            for j in range(2):
                then(dve.tensor_tensor(m.wt[:, j, :], m.top8[:, :, j], m.red[:, 1, :], ALU.mult))
            then(dve.tensor_scalar(m.keep, m.slot, 1.0, None, ALU.is_ge))
            then(dve.tensor_tensor(m.wt, m.wt, m.keep, ALU.mult))
            then(dve.tensor_scalar(m.keep, m.keep, -float(SLOTS + 1), float(SLOTS), ALU.mult, ALU.add))
            then(dve.tensor_tensor(m.slot, m.slot, m.keep, ALU.add))
            then(dve.tensor_copy(m.slotu, m.slot))


def dispatch(nc, m, d):
    with stage(nc, "disp", "z", "zeroed", "sent") as (block, s):
        NZ = SLOTS // P

        @block.vector
        def _(dve):
            dve.memset(m.zrow, 0.0).then_inc(s["z"], 1)

        @block.gpsimd
        def _(pool):
            pool.wait_ge(s["z"], 1)
            pool.dma_start(d["s_in"][0:SLOTS, :].rearrange("(p a) d -> p a d", p=P),
                           m.zrow.unsqueeze(1).to_broadcast([P, NZ, D])).then_inc(s["zeroed"], 16)
            pool.dma_start(d["s_out"][SLOTS:SLOTS + 1, :], m.zrow[0:1, :]).then_inc(s["zeroed"], 16)
            pool.wait_ge(s["zeroed"], 32)
            for i in range(NT):
                for j in range(2):
                    pool.indirect_dma_start(d["s_in"], bass.IndirectOffsetOnAxis(ap=m.slotu[:, j, i:i + 1], axis=0),
                                            m.xr[:, i, :], None, bounds_check=SLOTS - 1, oob_is_err=False)\
                        .then_inc(s["sent"], 16)
            pool.wait_ge(s["sent"], 16 * 2 * NT)


def experts(nc, m, d, g):
    E2 = E // GRP
    NU = 6
    C2 = CAP - P
    with stage(nc, "moe", "x", "w", "xt", "xtev", "up", "act", "hid", "y", "yev", "out") as (block, s):
        @block.sync
        def _(sp):
            for e in range(E2):
                rows = d["s_in"][bass.ds(g * E2 * CAP + e * CAP, CAP), :]
                sp.dma_start(m.xe[:, e, 0, :], rows[0:P, :]).then_inc(s["x"], 16)
                sp.dma_start(m.xe[0:C2, e, 1, :], rows[P:CAP, :]).then_inc(s["x"], 16)
            sp.dma_start(m.aup, d["p_aup"][g, :, :]).then_inc(s["w"], 16)
            sp.dma_start(m.adn, d["p_adn"][g, :, :]).then_inc(s["w"], 16)
            for e in range(E2):
                sp.dma_start(m.wup[:, e, :], d["p_wup"][g * E2 + e, :, :]).then_inc(s["w"], 16)
                sp.dma_start(m.wdn[:, e, :, :], d["p_wdn"][g * E2 + e, :, :].rearrange("(k p) d -> p k d", p=P))\
                  .then_inc(s["w"], 16)
            for e in range(E2):
                sp.wait_ge(s["yev"], 2 * (e + 1))
                out = d["s_out"][bass.ds(g * E2 * CAP + e * CAP, CAP), :]
                sp.dma_start(out[0:P, :], m.ye[:, e, 0, :]).then_inc(s["out"], 16)
                sp.dma_start(out[P:CAP, :], m.ye[0:C2, e, 1, :]).then_inc(s["out"], 16)
            sp.wait_ge(s["out"], 16 * 2 * E2)

        @block.tensor
        def _(pe):
            pe.wait_ge(s["x"], 16 * 2 * E2)
            for e in range(E2):
                pe.transpose(m.ps[e][:, 0:P], m.xe[:, e, 0, :], m.ident)
                pe.transpose(m.ps[e][:, P:CAP], m.xe[0:C2, e, 1, :], m.ident[0:C2, 0:C2]).then_inc(s["xt"], 1)
            pe.wait_ge(s["w"], 16 * (2 + 2 * E2))
            for e in range(E2):
                pe.wait_ge(s["xtev"], e + 1)
                for k in range(3):
                    u = 3 * e + k
                    if u >= 2:
                        pe.wait_ge(s["hid"], u - 1)
                    wg = m.wup[:, e, k * P:(k + 1) * P] if k < 2 else m.aup[:, 0:P]
                    wv = m.wup[:, e, INTER + k * P:INTER + (k + 1) * P] if k < 2 else m.aup[:, P:2 * P]
                    pe.matmul(m.ps[2 + u % 2][:, 0:CAP], wg, m.xeT[:, e, :], start=True, stop=True)
                    pe.matmul(m.ps[4 + u % 2][:, 0:CAP], wv, m.xeT[:, e, :], start=True, stop=True).then_inc(s["up"], 1)
            for e in range(E2):
                pe.wait_ge(s["hid"], 3 * (e + 1))
                for part, (a, b2) in enumerate(((0, P), (P, CAP))):
                    if e:
                        pe.wait_ge(s["yev"], 2 * (e - 1) + part + 1)
                    for k in range(3):
                        w = m.wdn[:, e, k, :] if k < 2 else m.adn
                        mm = pe.matmul(m.ps[6 + part][0:b2 - a, 0:D], m.hm[:, e, k, a:b2], w, start=(k == 0),
                                       stop=(k == 2))
                    mm.then_inc(s["y"], 1)

        @block.scalar
        def _(act):
            for u in range(3 * E2):
                act.wait_ge(s["up"], u + 1)
                if u >= 2:
                    act.wait_ge(s["hid"], u - 1)
                act.activation(m.sg[:, u % 2, :], m.ps[2 + u % 2][:, 0:CAP], ACT.Silu).then_inc(s["act"], 1)

        @block.vector
        def _(dve):
            for e in range(E2):
                dve.wait_ge(s["xt"], e + 1)
                dve.tensor_copy(m.xeT[:, e, :], m.ps[e][:, 0:CAP]).then_inc(s["xtev"], 1)
            for u in range(3 * E2):
                e, k = divmod(u, 3)
                dve.wait_ge(s["act"], u + 1)
                dve.scalar_tensor_tensor(out=m.hm[:, e, k, :], in0=m.sg[:, u % 2, :], scalar=ADAPT if k == 2 else 1.0,
                                         in1=m.ps[4 + u % 2][:, 0:CAP], op0=ALU.mult, op1=ALU.mult).then_inc(s["hid"], 1)
            for e in range(E2):
                for part, n in ((0, P), (1, C2)):
                    dve.wait_ge(s["y"], 2 * e + part + 1)
                    dve.tensor_copy(m.ye[0:n, e, part, :], m.ps[6 + part][0:n, 0:D]).then_inc(s["yev"], 1)


def combine(nc, m, d):
    with stage(nc, "comb", "got0", "got1", "got2", "got3", "acc", "out") as (block, s):
        got = [s["got0"], s["got1"], s["got2"], s["got3"]]
        RING = len(got)

        @block.gpsimd
        def _(pool):
            for i in range(NT):
                if i >= RING:
                    pool.wait_ge(s["acc"], 2 * (i - RING) + 2)
                for j in range(2):
                    pool.indirect_dma_start(m.yt[:, i % RING, j, :], None, d["s_out"],
                                            bass.IndirectOffsetOnAxis(ap=m.slotu[:, j, i:i + 1], axis=0))\
                        .then_inc(got[i % RING], 16)

        @block.vector
        def _(dve):
            for i in range(NT):
                for j in range(2):
                    dve.wait_ge(got[i % RING], 32 * (i // RING + 1))
                    if j:
                        dve.wait_ge(s["acc"], 2 * i + 1)
                    dve.scalar_tensor_tensor(out=m.xo[:, i, :], in0=m.yt[:, i % RING, j, :], scalar=m.wt[:, j, i:i + 1],
                                             in1=m.xo[:, i, :], op0=ALU.mult, op1=ALU.add).then_inc(s["acc"], 1)

        @block.sync
        def _(sp):
            o = d["out"].rearrange("b (t p) d -> b p t d", p=P)
            for b in range(B):
                sp.wait_ge(s["acc"], 2 * KT * (b + 1))
                sp.dma_start(o[b], m.xo[:, b * KT:(b + 1) * KT, :]).then_inc(s["out"], 16)
            sp.wait_ge(s["out"], 16 * B)


def build(nc, d):
    d["s_in"] = nc.dram_tensor("slot_rows", (SLOTS, D), F32, kind="Internal").ap()
    d["s_out"] = nc.dram_tensor("slot_results", (SLOTS + 1, D), F32, kind="Internal").ap()
    with ExitStack() as ctx:
        m = Memory()
        times = {}

        def sb(scope, name, shape, dt=F32):
            times[name] = times.get(name, 0) + 1
            t = scope.enter_context(nc.sbuf_tensor(f"{name}_{times[name]}", shape, dt))
            return t[tuple(slice(None) for _ in shape)]

        psum = ctx.enter_context(nc.psum_tensor("banks", [P, 8, T], F32))
        m.ps = [psum[:, i, :] for i in range(8)]
        m.ps2 = [psum[:, 2 * i:2 * i + 2, :] for i in range(4)]

        m.xsum = sb(ctx, "xsum", [P, N])
        m.xn = sb(ctx, "xn", [P, N])
        m.ident = sb(ctx, "ident", [P, P])
        m.onesm = sb(ctx, "onesm", [P, P])
        m.ones = sb(ctx, "ones", [P, T])
        m.heads = sb(ctx, "heads", [P, 2])
        m.eps = sb(ctx, "eps", [P, 1])
        m.zcol = sb(ctx, "zcol", [P, 1])
        m.tbias = sb(ctx, "tbias", [P, 1])
        m.ident16 = sb(ctx, "ident16", [P, P], BF16)
        m.spread = sb(ctx, "spread", [3 * 2 * HL, HL, P], BF16)
        m.mcausal = sb(ctx, "mcausal", [P, P], BF16)
        m.mlocal = sb(ctx, "mlocal", [P, 2, 4 * P], BF16)

        with ExitStack() as front:
            m.xq = sb(front, "xq", [P, N])
            m.xcsd = sb(front, "xcsd", [P, 4, T])
            m.sq = sb(front, "sq", [P, 2, T])
            m.rs = sb(front, "rs", [P, 2, T])
            m.sdn = sb(front, "sdn", [P, B, KT])
            m.rsn = sb(front, "rsn", [P, B, KT])
            m.xc, m.sd = m.xcsd[:, 0:2, :], m.xcsd[:, 2:4, :]
            m.xc3, m.diag = m.xcsd[:, 0:3, :], m.rs
            with ExitStack() as scope:
                m.xrow = sb(scope, "xrow", [P, NT, D])
                m.w_q0 = sb(scope, "w_q0", [D, D])
                m.w_k0 = sb(scope, "w_k0", [D, D])
                m.w_v0 = sb(scope, "w_v0", [D, D])
                m.w_o0 = sb(scope, "w_o0", [D, D])
                m.bones8 = sb(scope, "bones8", [P, P])
                m.hmask = sb(scope, "hmask", [P, H0])
                m.g_q0 = sb(scope, "g_q0", [P, 1])
                m.g_k0 = sb(scope, "g_k0", [P, 1])
                m.b_o0 = sb(scope, "b_o0", [P, 1])
                m.gamma0 = sb(scope, "gamma0", [P, 1])
                m.beta0 = sb(scope, "beta0", [P, 1])
                m.gq_blk = sb(scope, "gq_blk", [P, P])
                m.gk_blk = sb(scope, "gk_blk", [P, P])
                m.spread_f = sb(scope, "spread_f", [3 * 2 * HL, HL, P])
                m.mcausal_f = sb(scope, "mcausal_f", [P, P])
                m.mlocal_f = sb(scope, "mlocal_f", [P, 2, 4 * P])
                m.vbd = sb(scope, "vbd", [P, KT, H0 * (P + HD0)])
                m.vp = sb(scope, "vp", [P, T])
                m.xq_b = sb(scope, "xq_b", [P, T])
                m.xn_b = sb(scope, "xn_b", [P, T])
                m.qh = sb(scope, "qh", [P, T])
                m.kh = sb(scope, "kh", [P, T])
                m.km = sb(scope, "km", [P, 3, T])
                m.tanh = sb(scope, "tanh", [P, 3, 2, T])
                m.gateq = sb(scope, "gateq", [P, T])
                m.gatek = sb(scope, "gatek", [P, T])
                m.fused = sb(scope, "fused", [P, T])
                load_constants(nc, m, d)
                load_x(nc, m, d)
                layer_norm_all(nc, m, m.xsum, m.xn, label="ln1")
                layer_norm_all(nc, m, m.xn, m.xq, m.gamma0, m.beta0, label="ln2")
                with nc.Fori(0, B) as b:
                    resonance_attention(nc, m, b)

            with ExitStack() as scope:
                m.wqkv = sb(scope, "wqkv", [P, 3 * INNER])
                m.wo = sb(scope, "wo", [P, HL // 2, D])
                m.w1 = sb(scope, "w1", [P, 2 * DIN])
                m.w2 = sb(scope, "w2", [P, 3, D])
                m.b1 = sb(scope, "b1", [P, 6])
                m.lnp = sb(scope, "lnp", [P, 3])
                m.qks = sb(scope, "qks", [P, 2])
                m.rot0 = sb(scope, "rot0", [P, 4, T])
                m.rot = sb(scope, "rot", [P, 4, T])
                with ExitStack() as inner:
                    m.xs = sb(inner, "xs", [P, WIN + T])
                    m.kz = sb(inner, "kz", [P, HL // 2, 2, WIN + T])
                    m.v = sb(inner, "v", [P, NQ, HL, HDL + 1])
                    m.tt = sb(inner, "tt", [P, 4, T])
                    m.nm = sb(inner, "nm", [P, 3, 4])
                    m.ri = sb(inner, "ri", [P, 2, 4])
                    m.nrm = sb(inner, "nrm", [P, KT, 2 * HL])
                    m.rn = sb(inner, "rn", [P, KT, 2 * HL])
                    m.parts = sb(inner, "parts", [P, KT, 3, 2 * HL], BF16)
                    m.rnT = sb(inner, "rnT", [3 * 2 * HL, T], BF16)
                    m.attnT = sb(inner, "attnT", [P, HL // 2, T])
                    m.qr = m.xq.rearrange("p (a c) -> p a c", c=T)
                    m.pt, m.an = m.sd, m.rs[:, :, 0:4 * HDL]
                    m.t1, m.t2, m.pr = m.tt[:, 0:3, :], m.attnT[:, 0:3, :], m.tt[:, 0:3, :]
                    m.t3 = m.attnT[:, 3:6, :]
                    m.ge, m.hid, m.xsh = m.t1, m.attnT[:, 0:3, :], m.attnT[:, 3:5, :]
                    clear_local(nc, m, d)
                    with nc.Fori(0, DEPTH) as layer:
                        load_layer(nc, m, d, layer)
                        with nc.Fori(0, B) as b:
                            local_attention(nc, m, b)
                        feed_forward(nc, m)
            layer_norm_all(nc, m, m.xsum, m.xn, add=m.xn, label="ln3")

        with ExitStack() as scope:
            m.w_kvd = sb(scope, "w_kvd", [P, R1])
            m.w_kvu = sb(scope, "w_kvu", [P, 2 * HDT])
            m.w_q1 = sb(scope, "w_q1", [P, HDT])
            m.w_o1 = sb(scope, "w_o1", [P, H1 // 2, D])
            m.xn_b = sb(scope, "xn_b", [P, T])
            m.lat = sb(scope, "lat", [P, T])
            m.q1 = sb(scope, "q1", [P, H1 // 2, T])
            m.k1 = sb(scope, "k1", [P, H1 // 2, 2, T])
            m.v1 = sb(scope, "v1", [P, KT, H1, HD1 + 1])
            m.nm = sb(scope, "nm", [P, 4])
            m.ri = sb(scope, "ri", [P, 2, 4])
            m.pr = sb(scope, "pr", [P, 3, T])
            m.pt = sb(scope, "pt", [P, 3, T])
            m.an = sb(scope, "an", [P, 2, HDT])
            m.attnT = sb(scope, "attnT", [P, H1 // 2, T])
            load_latent(nc, m, d)
            with nc.Fori(0, B) as b:
                latent_attention(nc, m, b)

        m.xr = sb(ctx, "xr", [P, NT, D])
        m.xo = sb(ctx, "xo", [P, NT, D])
        m.slot = sb(ctx, "slot", [P, 2, NT])
        m.wt = sb(ctx, "wt", [P, 2, NT])
        m.keep = sb(ctx, "keep", [P, 2, NT])
        m.red = sb(ctx, "red", [P, 3, NT])
        m.slotu = sb(ctx, "slotu", [P, 2, NT], U32)
        token_rows(nc, m, m.xn, m.xr, "xrows")
        token_rows(nc, m, m.xsum, m.xo, "orows")
        with ExitStack() as scope:
            m.probs = sb(scope, "probs", [P, NT, E])
            with ExitStack() as inner:
                m.stats = sb(inner, "stats", [P, NT, NSTAT])
                m.sqr = sb(inner, "sqr", [P, NT, D])
                m.statT = sb(inner, "statT", [NSTAT, N])
                m.r1 = sb(inner, "r1", [P, RH])
                m.r1s = sb(inner, "r1s", [NSTAT, RH])
                m.r1b = sb(inner, "r1b", [RH, 1])
                m.r2 = sb(inner, "r2", [RH, E])
                m.rh = sb(inner, "rh", [RH, 2, T])
                token_stats(nc, m)
                router(nc, m, d)
            with ExitStack() as inner:
                m.top8 = sb(inner, "top8", [P, NT, 8])
                m.idxf = sb(inner, "idxf", [P, NT, 2])
                m.eiota = sb(inner, "eiota", [P, E])
                m.ebase = sb(inner, "ebase", [E, 1])
                m.hot = sb(inner, "hot", [P, 2, NT, E])
                m.score = sb(inner, "score", [P, NT, E])
                m.tmpn = sb(inner, "tmpn", [P, NT, E])
                m.slotN = sb(inner, "slotN", [P, NT, E])
                m.scoreE = sb(inner, "scoreE", [E, N])
                m.quart = sb(inner, "quart", [P, N // 4])
                m.best = sb(inner, "best", [P, CAP])
                m.cand = sb(inner, "cand", [E, 4 * CAP])
                m.b8 = sb(inner, "b8", [E, 8])
                m.gt = sb(inner, "gt", [E, N])
                m.eq = sb(inner, "eq", [E, N])
                m.run = sb(inner, "run", [E, N])
                m.cnt = sb(inner, "cnt", [E, 1])
                m.room = sb(inner, "room", [E, 1])
                m.idx8 = sb(inner, "idx8", [P, NT, 8], U32)
                m.slotE = m.eq
                route(nc, m, d)
        with ExitStack() as scope:
            m.zrow = sb(scope, "zrow", [P, D])
            m.xe = sb(scope, "xe", [P, 2, 2, D])
            m.xeT = sb(scope, "xeT", [P, 2, CAP])
            m.aup = sb(scope, "aup", [P, 2 * AINT])
            m.adn = sb(scope, "adn", [P, D])
            m.wup = sb(scope, "wup", [P, 2, 2 * INTER])
            m.wdn = sb(scope, "wdn", [P, 2, 2, D])
            m.hm = sb(scope, "hm", [P, 2, 3, CAP])
            m.sg = sb(scope, "sg", [P, 2, CAP])
            m.ye = sb(scope, "ye", [P, 2, 2, D])
            m.yt = sb(scope, "yt", [P, 4, 2, D])
            dispatch(nc, m, d)
            with nc.Fori(0, GRP) as g:
                experts(nc, m, d, g)
            combine(nc, m, d)


def clear_local(nc, m, d):
    with stage(nc, "clear", "loaded", "set") as (block, s):
        @block.sync
        def _(sp):
            sp.dma_start(m.rot0, d["c_rot"]).then_inc(s["loaded"], 16)
            sp.wait_ge(s["loaded"], 16)

        @block.vector
        def _(dve):
            dve.memset(m.xs, 0.0)
            dve.memset(m.kz, 0.0).then_inc(s["set"], 1)


def constants():
    import numpy as np
    f = np.float32
    c = {}
    c["c_ident"] = np.eye(P, dtype=f)
    c["c_bones8"] = np.kron(np.eye(H0, dtype=f), np.ones((HD0, HD0), f))
    c["c_heads"] = np.tile(np.kron(np.eye(2, dtype=f), np.ones((HDL // 2, 1), f)), (2, 1))
    c["c_hmask"] = np.kron(np.eye(H0, dtype=f), np.ones((HD0, 1), f))
    q, k = np.arange(P)[:, None], np.arange(P)[None, :]
    c["c_causal"] = np.where(k <= q, 0, MASKED).astype(f)
    band = (k >= q) & (k <= q + WIN)
    first = band & (k >= WIN)
    c["c_local"] = np.stack([np.tile(np.where(w, 0, MASKED).astype(f), (1, 4)) for w in (first, band)], 1)
    spread = np.zeros((3, HL, 2, HL, 2, 2, HDL // 2), f)
    for u in range(HL):
        for h in range(2):
            spread[:, u, h, u, :, h, :] = 1
    c["c_spread"] = spread.reshape(3 * 2 * HL, HL, P)
    half = np.arange(0, HDL, 2, dtype=f)
    inv_freq = (1.0 / f(10000.0) ** (half / f(HDL))).astype(f)
    t = np.arange(T, dtype=f)
    freqs = t[:, None] * inv_freq[None, :]
    base = ((half + f(0.4 * HDL)) / f(1.4 * HDL)).astype(f)
    power = ((t - T // 2) / f(WIN // 2)).astype(f)
    scale = (base[None, :] ** power[:, None]).astype(f)
    cos, sin = np.cos(freqs).astype(f), np.sin(freqs).astype(f)
    inv = (f(1.0) / scale).astype(f)
    parts = [(cos * scale, cos * scale), (sin * scale, -sin * scale), (cos * inv, cos * inv), (sin * inv, -sin * inv)]
    c["c_rot"] = np.stack([np.concatenate([a.T, a.T, b2.T, b2.T], 0) for a, b2 in parts], 1).astype(f)
    return {k2: np.ascontiguousarray(v) for k2, v in c.items()}


def laid_out(x):
    import numpy as np
    a = {k: np.ascontiguousarray(v) for k, v in x.items()}
    out = {"x": a["L0_attn_x"]}
    for n in ("L0_attn_w_q", "L0_attn_w_k", "L0_attn_w_v", "L0_attn_w_o", "L0_ffn_Wo", "L0_ffn_W1",
              "L1_attn_w_kv_down", "L1_attn_w_kv_up", "L1_attn_w_q", "L1_attn_w_out"):
        out[n] = a[n]
    w = a["L0_ffn_Wqkv"]
    qk = w[:, :, 0:2 * INNER].reshape(DEPTH, D, HL, 2, 2, HDL // 2).transpose(0, 1, 2, 4, 3, 5)
    out["p_Wqkv"] = np.concatenate([qk.reshape(DEPTH, D, 2 * INNER), w[:, :, 2 * INNER:]], 2)
    out["p_g_q"] = np.tile(a["L0_attn_g_q"], H0)[:, None]
    out["p_g_k"] = np.tile(a["L0_attn_g_k"], H0)[:, None]
    out["p_b_o"], out["p_gamma"], out["p_beta"] = (a["L0_attn_" + n][:, None] for n in ("b_o", "gamma", "beta"))
    pad = len(FK) * P - DIN
    out["p_W2"] = np.pad(a["L0_ffn_W2"], ((0, 0), (0, pad), (0, 0)))
    b1 = np.pad(a["L0_ffn_b1"].reshape(DEPTH, 2, DIN), ((0, 0), (0, 0), (0, pad)))
    out["p_b1"] = b1.reshape(DEPTH, 2 * len(FK), P).transpose(0, 2, 1)
    out["p_lnp"] = np.stack([a["L0_ffn_ln_g"], a["L0_ffn_ln_b"], a["L0_ffn_b2"]], 2)
    cols = []
    for n in ("L0_ffn_q_scale", "L0_ffn_k_scale"):
        cols.append(np.tile(a[n].reshape(DEPTH, 2, 1, HDL // 2), (1, 1, 2, 1)).reshape(DEPTH, P))
    out["p_qks"] = np.stack(cols, 2)
    r1 = a["L1_ffn_r1_w"].T
    out["p_r1"], out["p_r1s"] = r1[:D], r1[D:]
    out["p_r1b"], out["p_r2"] = a["L1_ffn_r1_b"][:, None], a["L1_ffn_r2_w"].T
    for short, n in (("p_wup", "w_up"), ("p_wdn", "w_down"), ("p_aup", "a_up"), ("p_adn", "a_down")):
        out[short] = a["L1_ffn_" + n].transpose(0, 2, 1)
    return {k: np.ascontiguousarray(v) for k, v in out.items()}


def kernel(**inputs):
    import numpy as np
    import concourse.bacc as bacc
    from concourse.bass_utils import run_bass_kernel_spmd

    nc = bacc.Bacc("TRN2", target_bir_lowering=False, num_devices=1)
    arrays = {**constants(), **laid_out(inputs)}
    d = {}
    for name, a in arrays.items():
        d[name] = nc.dram_tensor(name, a.shape, mybir.dt.from_np(a.dtype), kind="ExternalInput").ap()
    d["out"] = nc.dram_tensor("out", (B, T, D), F32, kind="ExternalOutput").ap()
    build(nc, d)
    r = run_bass_kernel_spmd(nc, [arrays], core_ids=[0])
    return r.results[0]["out"]
```

```python
from contextlib import ExitStack, contextmanager

import concourse.bass as bass
from concourse import mybir

F32 = mybir.dt.float32
BF16 = mybir.dt.bfloat16
U32 = mybir.dt.uint32
ALU = mybir.AluOpType
ACT = mybir.ActivationFunctionType
AX = mybir.AxisListType

P = 128
D = 128
B, T = 8, 512
N = B * T
NT = N // P
LN_EPS = 1e-5
NORM_MAX = 1e12
MASKED = -1e30

H0, HD0 = 16, 8
RU = 4
KT = T // P
SHARP, COLLAPSE = 15.0, 0.27

DEPTH, HL, HDL, WIN = 6, 16, 64, 32
LU = 4
INNER = HL * HDL
QK_SCALE = 8.0
DIN = int(D * 4 * 2 / 3)
QW = P - WIN
QT = [QW] * (T // QW) + ([T % QW] if T % QW else [])
NQ = len(QT)
G4 = HL // 4
FK = [P, P, DIN - 2 * P]

H1, HD1 = 16, 64
R1 = 128
HDT = H1 * HD1

E, TOPK, INTER, AINT = 32, 2, 256, 128
GRP = 16
GU = 4
CAP = int(1.25 * N / E)
SLOTS = E * CAP
RH = D // 2
NSTAT = 6
ADAPT = 0.05


class Memory:
    pass


@contextmanager
def stage(nc, label, *names):
    with ExitStack() as ctx:
        sems = {n: ctx.enter_context(nc.semaphore(f"{label}_{n}")) for n in names}
        with nc.Block() as block:
            yield block, sems
        for s in sems.values():
            nc.gpsimd.sem_clear(s)
        nc.all_engine_barrier()


def load_constants(nc, m, d):
    loads = [
        (m.ident, d["c_ident"]), (m.bones8, d["c_bones8"]), (m.heads, d["c_heads"]), (m.hmask, d["c_hmask"]),
        (m.mcausal_f, d["c_causal"]), (m.mlocal_f, d["c_local"]), (m.spread_f, d["c_spread"]),
        (m.pat, d["c_pat"]),
        (m.w_q0, d["L0_attn_w_q"]), (m.w_k0, d["L0_attn_w_k"]), (m.w_v0, d["L0_attn_w_v"]), (m.w_o0, d["L0_attn_w_o"]),
        (m.g_q0, d["p_g_q"]), (m.g_k0, d["p_g_k"]), (m.b_o0, d["p_b_o"]), (m.gamma0, d["p_gamma"]), (m.beta0, d["p_beta"]),
    ]
    with stage(nc, "const", "loaded", "set", "done") as (block, s):
        @block.sync
        def _(sp):
            for dst, src in loads:
                sp.dma_start(dst, src).then_inc(s["loaded"], 16)

        @block.vector
        def _(dve):
            dve.memset(m.onesm, 1.0 / D)
            dve.memset(m.ones, 1.0)
            dve.memset(m.eps, LN_EPS)
            dve.memset(m.zcol, 0.0)
            dve.memset(m.tbias, -SHARP * COLLAPSE)
            dve.memset(m.vbd, 0.0).then_inc(s["set"], 1)
            dve.wait_ge(s["loaded"], 16 * len(loads))
            dve.tensor_copy(m.ident16, m.ident)
            dve.tensor_copy(m.mcausal, m.mcausal_f)
            dve.tensor_copy(m.spread, m.spread_f)
            dve.tensor_copy(m.mlocal, m.mlocal_f)
            for h in range(H0):
                dve.tensor_scalar(m.select[:, :, h, :, :], m.pat, m.hmask[:, h:h + 1], None, ALU.mult)
            dve.tensor_scalar(m.gq_blk, m.bones8, m.g_q0, None, ALU.mult)
            dve.tensor_scalar(m.gk_blk, m.bones8, m.g_k0, None, ALU.mult).then_inc(s["done"], 1)


def load_x(nc, m, d):
    with stage(nc, "loadx", "loaded", "turned", "kept") as (block, s):
        x_v = d["x"].rearrange("b (t p) d -> b p t d", p=P)

        @block.sync
        def _(sp):
            for b in range(B):
                sp.dma_start(m.xrow[:, b * KT:(b + 1) * KT, :], x_v[b]).then_inc(s["loaded"], 16)

        @block.tensor
        def _(pe):
            for b in range(B):
                pe.wait_ge(s["loaded"], 16 * B if b else 16 * B)
                if b >= 4:
                    pe.wait_ge(s["kept"], b - 3)
                for t in range(KT):
                    mm = pe.transpose(m.ps[b % 4][:, t * P:(t + 1) * P], m.xrow[:, b * KT + t, :], m.ident)
                mm.then_inc(s["turned"], 1)

        @block.vector
        def _(dve):
            for b in range(B):
                dve.wait_ge(s["turned"], b + 1)
                dve.tensor_copy(m.xsum[:, b * T:(b + 1) * T], m.ps[b % 4][:, :]).then_inc(s["kept"], 1)


def layer_norm_all(nc, m, src, dst, gamma=None, beta=None, add=None, label="ln"):
    with stage(nc, label, "summed", *NORM_SEMS) as (block, s):
        def chunk(c):
            return src[:, c * T:(c + 1) * T]

        @block.tensor
        def _(pe):
            def ready(c):
                if add is not None:
                    pe.wait_ge(s["summed"], c + 1)

            mean, variance, spread = norm_pe(pe, m, s, chunk, ready)
            for c in range(B + 2):
                if c < B:
                    mean(c)
                if 1 <= c <= B:
                    variance(c - 1)
                if c >= 2:
                    spread(c - 2)

        @block.scalar
        def _(act):
            square, deviation = norm_act(act, m, s)
            for c in range(B):
                square(c)
                deviation(c)

        @block.vector
        def _(dve):
            if add is not None:
                for c in range(B):
                    here = slice(c * T, (c + 1) * T)
                    dve.tensor_tensor(src[:, here], src[:, here], add[:, here], ALU.add).then_inc(s["summed"], 1)
                dve.wait_ge(s["summed"], B)
            centered, diagonal, normed = norm_dve(dve, m, s, chunk, dst, gamma, beta)
            for c in range(B + 2):
                if c < B:
                    centered(c)
                if 1 <= c <= B:
                    diagonal(c - 1)
                if c >= 2:
                    normed(c - 2)


NORM_SEMS = ("mean", "xc", "sq", "var", "sd", "rs", "diag", "rsb", "scaled", "ln")
NORM_BANKS = ((0, 1), (2, 3), (4, 5))


def norm_pe(pe, m, s, src, ready, banks=NORM_BANKS):
    mean_at, var_at, spread_at = banks
    nb = len(mean_at)

    def mean(c):
        ready(c)
        if c >= nb:
            pe.wait_ge(s["xc"], c - nb + 1)
        pe.matmul(m.ps[mean_at[c % nb]], m.onesm, src(c), start=True, stop=True).then_inc(s["mean"], 1)

    def variance(c):
        pe.wait_ge(s["sq"], c + 1)
        if c >= nb:
            pe.wait_ge(s["sd"], c - nb + 1)
            if var_at == spread_at:
                pe.wait_ge(s["ln"], c - nb + 1)
        for t in range(KT):
            mm = pe.matmul(m.ps[var_at[c % nb]][:, t:t + 1], m.sq[:, c % 2, t * P:(t + 1) * P], m.onesm[:, 0:1],
                           start=True, stop=True)
        mm.then_inc(s["var"], 1)

    def spread(c):
        pe.wait_ge(s["diag"], c + 1)
        if c >= nb:
            pe.wait_ge(s["ln"], c - nb + 1)
        pe.matmul(m.ps[spread_at[c % nb]], m.ones[:, 0:P], m.diag[:, c % 2, :], start=True, stop=True)\
          .then_inc(s["rsb"], 1)

    return mean, variance, spread


def norm_act(act, m, s, banks=NORM_BANKS):
    var_at = banks[1]

    def square(c):
        act.wait_ge(s["xc"], c + 1)
        if c >= 2:
            act.wait_ge(s["var"], c - 1)
        act.activation(m.sq[:, c % 2, :], m.xc3[:, c % 3, :], ACT.Square).then_inc(s["sq"], 1)

    def deviation(c):
        act.wait_ge(s["var"], c + 1)
        act.activation(m.sdn[:, c, :], m.ps[var_at[c % len(var_at)]][:, 0:KT], ACT.Sqrt, bias=m.eps)\
           .then_inc(s["sd"], 1)

    return square, deviation


def norm_dve(dve, m, s, src, dst, gamma, beta, banks=NORM_BANKS):
    mean_at, _, spread_at = banks
    nb = len(mean_at)

    def centered(c):
        dve.wait_ge(s["mean"], c + 1)
        if c >= 3:
            dve.wait_ge(s["sq"], c - 2)
            dve.wait_ge(s["ln"], c - 2)
        dve.tensor_tensor(m.xc3[:, c % 3, :], src(c), m.ps[mean_at[c % nb]], ALU.subtract).then_inc(s["xc"], 1)

    def diagonal(c):
        dve.wait_ge(s["sd"], c + 1)
        dve.reciprocal(m.rsn[:, c, :], m.sdn[:, c, :]).then_inc(s["rs"], 1)
        dve.wait_ge(s["rs"], c + 1)
        if c >= 2:
            dve.wait_ge(s["rsb"], c - 1)
        dve.tensor_tensor(m.diag[:, c % 2, :].rearrange("p (t q) -> p t q", t=KT),
                          m.ident.unsqueeze(1).to_broadcast([P, KT, P]),
                          m.rsn[:, c, :].unsqueeze(2).to_broadcast([P, KT, P]), ALU.mult).then_inc(s["diag"], 1)

    def normed(c):
        out, rsb = dst[:, c * T:(c + 1) * T], m.ps[spread_at[c % nb]]
        dve.wait_ge(s["rsb"], c + 1)
        if gamma is None:
            dve.tensor_tensor(out, rsb, m.xc3[:, c % 3, :], ALU.mult).then_inc(s["ln"], 1)
            return
        dve.scalar_tensor_tensor(out=out, in0=rsb, scalar=gamma, in1=m.xc3[:, c % 3, :], op0=ALU.mult,
                                 op1=ALU.mult).then_inc(s["scaled"], 1)
        dve.wait_ge(s["scaled"], c + 1)
        dve.tensor_scalar(out, out, beta, None, ALU.add).then_inc(s["ln"], 1)

    return centered, diagonal, normed


def resonance_attention(nc, m, b):
    NI = H0 * 2
    K9 = 9 * HD0
    NB = 2 * H0
    with stage(nc, "res", "xin", "proj", "sq", "ss", "nrm", "rn", "unit", "gate", "th", "g", "vp", "vbd",
               "split", "built", "stack", "score", "tanh", "sum", "pv", "fused", "wo", "out") as (block, s):
        def bank(r, name):
            at = dict(q=0, k=1, v=2, ssq=3, ssk=4, gq=5, gk=6) if r == 0 else dict(q=4, k=4, v=4, ssq=5, ssk=5, gq=4, gk=5)
            return m.ps[at[name]]

        built_ps, acc, o_ps = m.ps[6][0:K9, :], m.ps[7], m.ps[5]

        def here(r):
            return bass.ds((b * RU + r) * T, T)

        @block.vector
        def _(dve):
            def copied(r):
                if r:
                    dve.wait_ge(s["proj"], 3 * r)
                dve.tensor_copy(m.xq_b, m.xq[:, here(r)]).then_inc(s["xin"], 1)
                dve.tensor_copy(m.xn_b, m.xn[:, here(r)]).then_inc(s["xin"], 1)

            def unit(r, i):
                out = (m.qh, m.kh)[i]
                dve.wait_ge(s["nrm"], 2 * r + i + 1)
                dve.reciprocal(m.rs[:, i, :], m.sd[:, i, :]).then_inc(s["rn"], 1)
                if r:
                    dve.wait_ge(s["gate"], 2 * r)
                dve.wait_ge(s["rn"], 2 * r + i + 1)
                dve.scalar_tensor_tensor(out=out, in0=m.rs[:, i, :], scalar=NORM_MAX, in1=bank(r, "qk"[i]),
                                         op0=ALU.min, op1=ALU.mult).then_inc(s["unit"], 1)

            def split(r, i):
                src, part, rest, n = (m.qh, m.kh)[i], m.parts0[:, r % 2, i, :, :], m.rest[:, i, :], 8 * r + 4 * i
                dve.wait_ge(s["unit"], 2 * r + i + 1)
                dve.tensor_copy(part[:, 0, :], src).then_inc(s["split"], 1)
                dve.wait_ge(s["split"], n + 1)
                dve.tensor_tensor(rest, src, part[:, 0, :], ALU.subtract).then_inc(s["split"], 1)
                dve.wait_ge(s["split"], n + 2)
                dve.tensor_copy(part[:, 1, :], rest).then_inc(s["split"], 1)
                dve.wait_ge(s["split"], n + 3)
                dve.tensor_tensor(part[:, 2, :], rest, part[:, 1, :], ALU.subtract).then_inc(s["split"], 1)

            def gates(r):
                dve.wait_ge(s["th"], 2 * r + 2)
                dve.tensor_scalar(m.gateq[:, r % 2, :], m.xc[:, 0, :], 0.375, 0.625, ALU.mult, ALU.add)\
                   .then_inc(s["g"], 1)
                dve.tensor_scalar(m.gatek, m.xc[:, 1, :], 0.1875, 0.3125, ALU.mult, ALU.add).then_inc(s["g"], 1)

            def gated(r):
                dve.wait_ge(s["g"], 2 * r + 2)
                dve.wait_ge(s["proj"], 3 * r + 3)
                if r:
                    dve.wait_ge(s["sum"], r)
                dve.tensor_tensor(m.vp, bank(r, "v"), m.gatek, ALU.mult).then_inc(s["vp"], 1)

            steps = {1: copied, 4: lambda r: unit(r, 0), 6: lambda r: split(r, 0), 8: lambda r: unit(r, 1),
                     10: lambda r: split(r, 1), 13: gates, 14: gated}

            def stacked(r, j):
                h, z = j // 2, j % 2
                if r or h >= 2:
                    dve.wait_ge(s["score"], r * NI + 2 * (h - 1))
                dve.wait_ge(s["built"], NB * r + j + 1)
                dve.tensor_copy(m.stack[0:K9, z, h % 2, :], built_ps).then_inc(s["stack"], 1)

            def fused(r):
                dve.wait_ge(s["pv"], NI * (r + 1))
                dve.tensor_tensor(m.fused, acc, m.gateq[:, r % 2, :], ALU.mult).then_inc(s["fused"], 1)

            def added(r):
                dve.wait_ge(s["wo"], r + 1)
                dve.scalar_tensor_tensor(out=m.xsum[:, here(r)], in0=o_ps, scalar=m.b_o0, in1=m.xsum[:, here(r)],
                                         op0=ALU.add, op1=ALU.add).then_inc(s["out"], 1)

            for step in steps.values():
                step(0)
            for r in range(RU):
                if r:
                    fused(r - 1)
                stacked(r, 0)
                dve.wait_ge(s["vp"], r + 1)
                for kt in range(KT):
                    blocks = m.vbd[:, kt, :].rearrange("p (h c) -> p h c", c=P + HD0)[:, :, 0:HD0]
                    dve.tensor_copy(blocks, m.vp[:, kt * P:(kt + 1) * P].rearrange("p (h c) -> p h c", c=HD0))\
                       .then_inc(s["vbd"], 1)
                stacked(r, 1)
                for i in range(NI):
                    if i + 2 < NB:
                        stacked(r, i + 2)
                    if i == 0 and r:
                        added(r - 1)
                    if i in steps and r + 1 < RU:
                        steps[i](r + 1)
            fused(RU - 1)
            added(RU - 1)

        @block.scalar
        def _(act):
            def square(r, i):
                act.wait_ge(s["proj"], 3 * r + i + 1)
                if r:
                    act.wait_ge(s["ss"], 2 * (r - 1) + i + 1)
                act.activation(m.sq[:, i, :], bank(r, "qk"[i]), ACT.Square).then_inc(s["sq"], 1)

            def root(r, i):
                act.wait_ge(s["ss"], 2 * r + i + 1)
                if r:
                    act.wait_ge(s["rn"], 2 * (r - 1) + i + 1)
                act.activation(m.sd[:, i, :], bank(r, ("ssq", "ssk")[i]), ACT.Sqrt, bias=m.zcol).then_inc(s["nrm"], 1)

            def gate(r, i):
                act.wait_ge(s["gate"], 2 * r + i + 1)
                if r:
                    act.wait_ge(s["g"], 2 * r)
                act.activation(m.xc[:, i, :], bank(r, ("gq", "gk")[i]), ACT.Tanh, scale=0.5).then_inc(s["th"], 1)

            steps = {2: (square, 0), 3: (root, 0), 6: (square, 1), 7: (root, 1), 10: (gate, 0), 11: (gate, 1)}
            for step, i in steps.values():
                step(0, i)
            for r in range(RU):
                for i in range(NI):
                    n = r * NI + i
                    act.wait_ge(s["score"], n + 1)
                    if n >= 3:
                        act.wait_ge(s["pv"], n - 2)
                    act.activation(m.tanh[:, n % 3, :, :], m.ps2[n % 2], ACT.Tanh, bias=m.tbias, scale=SHARP)\
                       .then_inc(s["tanh"], 1)
                    if i in steps and r + 1 < RU:
                        step, a = steps[i]
                        step(r + 1, a)

        @block.tensor
        def _(pe):
            def project(r, i):
                pe.wait_ge(s["xin"], 2 * r + 2)
                if r and i:
                    pe.wait_ge(s["unit"], 2 * r + 1)
                pe.matmul(bank(r, "qk"[i]), (m.w_q0, m.w_k0)[i], m.xq_b, start=True, stop=True).then_inc(s["proj"], 1)

            def squares(r, i):
                pe.wait_ge(s["sq"], 2 * r + i + 1)
                if r:
                    pe.wait_ge(s["nrm"], 2 * r + i)
                    if i == 0 and r > 1:
                        pe.wait_ge(s["out"], r - 1)
                pe.matmul(bank(r, ("ssq", "ssk")[i]), m.bones8, m.sq[:, i, :], start=True, stop=True)\
                  .then_inc(s["ss"], 1)

            def gate_q(r, _):
                pe.wait_ge(s["unit"], 2 * r + (2 if r else 1))
                pe.matmul(bank(r, "gq"), m.gq_blk, m.qh, start=True, stop=True).then_inc(s["gate"], 1)

            def gate_k(r, _):
                pe.wait_ge(s["unit"], 2 * r + 2)
                pe.wait_ge(s["nrm"], 2 * r + 2)
                for kt in range(KT):
                    mm = pe.matmul(bank(r, "gk")[:, kt * P:(kt + 1) * P], m.kh[:, kt * P:(kt + 1) * P], m.gk_blk,
                                   start=True, stop=True)
                mm.then_inc(s["gate"], 1)

            def project_v(r, _):
                if r:
                    pe.wait_ge(s["th"], 2 * r + 1)
                for kt in range(KT):
                    mm = pe.matmul(bank(r, "v")[:, kt * P:(kt + 1) * P], m.xn_b[:, kt * P:(kt + 1) * P], m.w_v0,
                                   start=True, stop=True)
                mm.then_inc(s["proj"], 1)

            steps = {2: (project, 0), 3: (squares, 0), 6: (project, 1), 7: (squares, 1), 10: (gate_q, 0),
                     11: (gate_k, 0), 12: (project_v, 0)}

            def build(r, j):
                h, z = j // 2, j % 2
                if j == 0:
                    pe.wait_ge(s["split"], 8 * (r + 1))
                if r or j:
                    pe.wait_ge(s["stack"], NB * r + j)
                for a in range(3):
                    mm = pe.matmul(built_ps, m.select[:, z, h, a, :], m.parts0[:, r % 2, z, a, :], start=(a == 0),
                                   stop=(a == 2))
                mm.then_inc(s["built"], 1)

            def scores(r, i):
                h, u = i // 2, i % 2
                n = r * NI + i
                pe.wait_ge(s["stack"], NB * r + 2 * h + 2)
                if n >= 2:
                    pe.wait_ge(s["tanh"], n - 1)
                for j in range(2):
                    kt = 2 * u + j
                    mm = pe.matmul(m.ps2[n % 2][:, j, :], m.stack[0:K9, 1, h % 2, kt * P:(kt + 1) * P],
                                   m.stack[0:K9, 0, h % 2, :], start=True, stop=True)
                mm.then_inc(s["score"], 1)

            def values(r, i):
                h, u = i // 2, i % 2
                n = r * NI + i
                pe.wait_ge(s["tanh"], n + 1)
                pe.wait_ge(s["vbd"], KT * (r + 1))
                for j in range(2):
                    mm = pe.matmul(acc, m.vbd[:, 2 * u + j, h * P:(h + 1) * P], m.tanh[:, n % 3, j, :],
                                   start=False, stop=(i == NI - 1 and j == 1), skip_group_check=True)
                mm.then_inc(s["pv"], 1)

            def out(r):
                pe.wait_ge(s["fused"], r + 1)
                pe.matmul(o_ps, m.w_o0, m.fused, start=True, stop=True).then_inc(s["wo"], 1)

            project(0, 0)
            project(0, 1)
            project_v(0, 0)
            squares(0, 0)
            squares(0, 1)
            gate_q(0, 0)
            gate_k(0, 0)
            for r in range(RU):
                pe.wait_ge(s["th"], 2 * (r + 1))
                build(r, 0)
                pe.wait_ge(s["vp"], r + 1)
                if r:
                    pe.wait_ge(s["fused"], r)
                for kt in range(KT):
                    mm = pe.matmul(acc, m.vp[:, kt * P:(kt + 1) * P], m.ones, start=(kt == 0), stop=False,
                                   skip_group_check=True)
                mm.then_inc(s["sum"], 1)
                build(r, 1)
                if r:
                    out(r - 1)
                for i in range(NI + 1):
                    if i < NI:
                        scores(r, i)
                    if i + 2 < NB:
                        build(r, i + 2)
                    if i in steps and r + 1 < RU:
                        step, a = steps[i]
                        step(r + 1, a)
                    if i:
                        values(r, i - 1)
            out(RU - 1)


def attention_loads(m, d, layer):
    return [(m.wqkv, d["p_Wqkv"][layer, :, :]), (m.qks, d["p_qks"][layer, :, :]),
            (m.wo, d["p_Wo"][layer, :, :].rearrange("(k p) d -> p k d", p=P))]


def rotary_tables(dve, m):
    for i in range(4):
        last = dve.tensor_scalar(m.rot[:, i, :], m.rot0[:, i, :], m.qks[:, i // 2:i // 2 + 1],
                                 QK_SCALE if i < 2 else 1.0, ALU.mult, ALU.mult)
    return last


def load_first(nc, m, d):
    with stage(nc, "layer", "loaded", "made") as (block, s):
        loads = attention_loads(m, d, 0)

        @block.sync
        def _(sp):
            for dst, src in loads:
                sp.dma_start(dst, src).then_inc(s["loaded"], 16)

        @block.vector
        def _(dve):
            dve.wait_ge(s["loaded"], 16 * len(loads))
            rotary_tables(dve, m).then_inc(s["made"], 1)


def local_attention(nc, m, b):
    half = D // 2
    NU = 2 * (HL // 2)
    UG = NU // G4
    NV = 2 * NQ
    items = [(g, j) for g in range(G4) for j in range(NQ)]
    NI = len(items)
    NS = 3
    NO = HL // 2
    with stage(nc, "loc", "xs", "ones", "v", "vev", "a", "sq", "ss", "sd", "t1", "t2", "swap0", "swap1", "swap2", "sum", "rn", "part",
               "rt", "rtev", "bc", "unit", "score", "nm", "exp", "turn", "pta", "ptd", "pv", "ri", "norm", "at", "atev",
               "wo", "out") as (block, s):
        a_ps, n_ps, v_ps = m.ps[0:3], m.ps[4], m.ps[5:8]
        s_ps, bc_ps, pt_ps, pv_ps, at_ps = m.ps[0:NS], m.ps[3], m.ps[4:6], m.ps[6], m.ps[7]
        o_ps = bc_ps
        rt_ps = bc_ps.bitcast(BF16)[0:3 * 2 * NU, 0:T]

        def keys(j):
            return QT[j] + WIN

        def swap(n):
            return f"swap{n % 3}"

        def rows(a):
            return slice(a * HDL, (a + 1) * HDL)

        v_beside = (0, 1, 2)
        v_left = range(len(v_beside), NV)

        def by_act(i):
            return i % 2 == 1

        def copies(i):
            return sum(by_act(j) == by_act(i) for j in range(i + 1))

        def unit_at(i):
            g, j = items[i % NI]
            return UG * (g + 1) + j if j < UG and g + 1 < G4 else None

        @block.vector
        def _(dve):
            def shifted(r):
                if r:
                    dve.wait_ge(s["v"], NV * r)
                at = (b * LU + r) * T
                dve.tensor_copy(m.xs[0:half, WIN:], m.xn[0:half, bass.ds(at, T)]).then_inc(s["xs"], 1)
                dve.tensor_copy(m.xs[half:D, WIN + 1:], m.xn[half:D, bass.ds(at, T - 1)]).then_inc(s["xs"], 1)

            def rotary(n):
                z = n % 2
                if n and n % NU == 0:
                    dve.wait_ge(s["turn"], NI * (n // NU))
                    dve.wait_ge(s["wo"], NO * (n // NU) - 2)
                dve.wait_ge(s["sq"], n + 1)
                if n >= 3:
                    dve.wait_ge(s[swap(n)], 32 * (n // 3))
                dve.tensor_tensor(m.t2[:, n % 3, :], a_ps[n % 3], m.rot[:, 2 * z + 1, :], ALU.mult)\
                   .then_inc(s["t2"], 1)
                if n >= 3:
                    dve.wait_ge(s["sum"], n - 2)
                dve.tensor_tensor(m.t1[:, n % 3, :], a_ps[n % 3], m.rot[:, 2 * z, :], ALU.mult).then_inc(s["t1"], 1)

            def reciprocal_norms(r):
                dve.wait_ge(s["sd"], r + 1)
                dve.reciprocal(m.rn, m.nrm).then_inc(s["rn"], 1)
                dve.wait_ge(s["rn"], 4 * r + 1)
                dve.tensor_scalar(m.rn, m.rn, NORM_MAX, None, ALU.min).then_inc(s["rn"], 1)
                for i in range(3):
                    dve.wait_ge(s["rn"], 4 * r + 2 + i)
                    dve.tensor_copy(m.parts[:, :, i, :], m.rn).then_inc(s["part"], 1)
                    if i < 2:
                        dve.wait_ge(s["part"], 3 * r + i + 1)
                        dve.tensor_tensor(m.rn, m.rn, m.parts[:, :, i, :], ALU.subtract).then_inc(s["rn"], 1)
                dve.wait_ge(s["rt"], r + 1)
                dve.tensor_copy(m.rnT, rt_ps).then_inc(s["rtev"], 1)

            def scale(n):
                p, z = n % NU // 2, n % 2
                dve.wait_ge(s["bc"], n + 1)
                dve.wait_ge(s["sum"], n + 1)
                if z == 0:
                    dve.tensor_tensor(m.qr[:, p, :], bc_ps, m.qr[:, p, :], ALU.mult).then_inc(s["unit"], 2)
                    return
                for a in (1, 0):
                    dve.scalar_tensor_tensor(out=m.kz[:, p, a, WIN:], in0=bc_ps, scalar=m.heads[:, a:a + 1],
                                             in1=m.kz[:, p, 0, WIN:], op0=ALU.mult, op1=ALU.mult)\
                       .then_inc(s["unit"], 1)

            def negmax(i):
                g, j = items[i % NI]
                q, k = QT[j], keys(j)
                dve.wait_ge(s["score"], i + 1)
                if i >= NS:
                    dve.wait_ge(s["exp"], i - NS + 1)
                dve.tensor_reduce(m.nm[0:q, i % NS, :], s_ps[i % NS][0:q, 0:4 * k].rearrange("p (h k) -> p h k", h=4),
                                  AX.X, ALU.max, negate=True).then_inc(s["nm"], 1)

            def probs_t(i):
                g, j = items[i % NI]
                q, k = QT[j], keys(j)
                if by_act(i):
                    return
                dve.wait_ge(s["turn"], i + 1)
                if i >= 2:
                    dve.wait_ge(s["pv"], i - 1)
                dve.tensor_copy(m.pt[0:k, i % 2, 0:4 * q], pt_ps[i % 2][0:k, 0:4 * q]).then_inc(s["ptd"], 1)

            def normed(i):
                g, j = items[i % NI]
                q = QT[j]
                pv = pv_ps[0:q, 0:4 * (HDL + 1)].rearrange("p (h c) -> p h c", h=4)
                dve.wait_ge(s["pv"], i + 1)
                dve.reciprocal(m.ri[0:q, i % 2, :], pv[:, :, HDL]).then_inc(s["ri"], 1)
                dve.wait_ge(s["ri"], i + 1)
                if i >= 2:
                    dve.wait_ge(s["at"], i - 1)
                dve.tensor_tensor(m.an[0:q, i % 2, :].rearrange("p (h c) -> p h c", h=4), pv[:, :, 0:HDL],
                                  m.ri[0:q, i % 2, :].unsqueeze(2).to_broadcast([q, 4, HDL]), ALU.mult)\
                   .then_inc(s["norm"], 1)

            def add(r):
                here = bass.ds((b * LU + r) * T, T)
                dve.wait_ge(s["wo"], NO * (r + 1))
                dve.tensor_tensor(m.xn[:, here], o_ps, m.xn[:, here], ALU.add).then_inc(s["out"], 1)

            shifted(0)
            for r in range(LU):
                i0, n0 = r * NI, r * NU
                for n in range(1 if r else 0, NU):
                    rotary(n0 + n)
                    if n == 3 and r:
                        add(r - 1)
                reciprocal_norms(r)
                for n in range(UG):
                    scale(n0 + n)
                for i in range(NI + 3):
                    if i < NI:
                        negmax(i0 + i)
                    if 2 <= i < NI + 2:
                        probs_t(i0 + i - 2)
                    if i >= 3:
                        normed(i0 + i - 3)
                    if i < NI and unit_at(i) is not None:
                        scale(n0 + unit_at(i))
                    if i == NI - NS and r + 1 < LU:
                        shifted(r + 1)
                if r + 1 < LU:
                    rotary(n0 + NU)
            add(LU - 1)

        @block.sync
        def _(sp):
            for n in range(LU * NU):
                sp.wait_ge(s["t2"], n + 1)
                if n >= 3:
                    sp.wait_ge(s["sum"], n - 2)
                for a in range(2):
                    sp.dma_start(m.t3[rows(a), n % 3, :], m.t2[rows(1 - a), n % 3, :]).then_inc(s[swap(n)], 16)

        @block.gpsimd
        def _(pool):
            pool.memset(m.v[:, :, :, HDL:HDL + 1], 1.0).then_inc(s["ones"], 1)
            for n in range(LU * NU):
                p, z = n % NU // 2, n % 2
                if n and n % NU == 0:
                    pool.wait_ge(s["score"], NI * (n // NU))
                pool.wait_ge(s["t1"], n + 1)
                pool.wait_ge(s[swap(n)], 32 * (n // 3 + 1))
                if n:
                    pool.wait_ge(s["sum"], n)
                out = m.qr[:, p, :] if z == 0 else m.kz[:, p, 0, WIN:]
                pool.tensor_tensor(out, m.t1[:, n % 3, :], m.t3[:, n % 3, :], ALU.add).then_inc(s["sum"], 1)

        @block.scalar
        def _(act):
            def square(n):
                act.wait_ge(s["a"], n + 1)
                if n >= 2:
                    act.wait_ge(s["ss"], n - 1)
                act.activation(m.sq[:, n % 2, :], a_ps[n % 3], ACT.Square).then_inc(s["sq"], 1)

            def values(i):
                j, c = i % NV // 2, i % 2
                k = keys(j)
                act.wait_ge(s["v"], i + 1)
                act.activation(m.v[0:k, j, 8 * c:8 * c + 8, 0:HDL],
                               v_ps[i % 3][0:k, :].rearrange("p (h c) -> p h c", h=8), ACT.Copy).then_inc(s["vev"], 1)

            def turned_rows(i):
                g, j = items[i % NI]
                q = QT[j]
                act.wait_ge(s["at"], i + 1)
                act.activation(m.attnT[:, 2 * g:2 * g + 2, QW * j:QW * j + q],
                               at_ps[:, 0:2 * q].rearrange("p (k q) -> p k q", k=2), ACT.Copy).then_inc(s["atev"], 1)

            def probs_t(i):
                g, j = items[i % NI]
                q, k = QT[j], keys(j)
                if not by_act(i):
                    return
                act.wait_ge(s["turn"], i + 1)
                if i >= 2:
                    act.wait_ge(s["pv"], i - 1)
                act.activation(m.pt[0:k, i % 2, 0:4 * q], pt_ps[i % 2][0:k, 0:4 * q], ACT.Copy).then_inc(s["pta"], 1)

            def exps(i):
                g, j = items[i % NI]
                q, k = QT[j], keys(j)
                act.wait_ge(s["nm"], i + 1)
                if i % NI == 0:
                    act.wait_ge(s["sum"], NU * (i // NI + 1))
                    if i:
                        act.wait_ge(s["wo"], NO * (i // NI))
                if i >= NS:
                    act.wait_ge(s["turn"], i - NS + 1)
                for h in range(4):
                    last = act.activation(m.pr[0:q, i % NS, h * k:(h + 1) * k], s_ps[i % NS][0:q, h * k:(h + 1) * k],
                                          ACT.Exp, bias=m.nm[0:q, i % NS, h:h + 1])
                last.then_inc(s["exp"], 1)

            for r in range(LU):
                i0, n0 = r * NI, r * NU
                for n in range(NU):
                    if r == 0 or n >= 2:
                        square(n0 + n)
                    if n in v_beside:
                        values(r * NV + v_beside.index(n))
                act.wait_ge(s["ss"], n0 + NU)
                act.activation(m.nrm, n_ps[:, 0:KT * 2 * NU].rearrange("p (t u) -> p t u", t=KT), ACT.Sqrt,
                               bias=m.zcol).then_inc(s["sd"], 1)
                for i in v_left:
                    values(r * NV + i)
                for i in range(NI + 4):
                    if i < NI:
                        exps(i0 + i)
                    if 2 <= i < NI + 2:
                        probs_t(i0 + i - 2)
                    if i >= 4:
                        turned_rows(i0 + i - 4)
                    if i >= NI + 2 and r + 1 < LU:
                        square(n0 + NU + i - NI - 2)

        @block.tensor
        def _(pe):
            def proj(n):
                p, z = n % NU // 2, n % 2
                col = z * INNER + p * P
                if n % NU == 0:
                    pe.wait_ge(s["xs"], 2 * (n // NU + 1))
                if n >= 3:
                    pe.wait_ge(s["t1"], n - 2)
                if n >= NU and n % NU < 3:
                    pe.wait_ge(s["exp"], NI * (n // NU))
                pe.matmul(a_ps[n % 3], m.wqkv[:, col:col + P], m.xs[:, WIN:], start=True, stop=True)\
                  .then_inc(s["a"], 1)

            def v_proj(i):
                j, c = i % NV // 2, i % 2
                k = keys(j)
                if i >= 3:
                    pe.wait_ge(s["vev"], i - 2)
                pe.matmul(v_ps[i % 3][0:k, :], m.xs[:, QW * j:QW * j + k],
                          m.wqkv[:, 2 * INNER + 512 * c:2 * INNER + 512 * (c + 1)], start=True, stop=True)\
                  .then_inc(s["v"], 1)

            def sums(n):
                pe.wait_ge(s["sq"], n + 1)
                for t in range(KT):
                    c = (t * NU + n % NU) * 2
                    mm = pe.matmul(n_ps[:, c:c + 2], m.sq[:, n % 2, t * P:(t + 1) * P], m.heads,
                                   start=True, stop=True)
                mm.then_inc(s["ss"], 1)

            def spread(n):
                if n:
                    pe.wait_ge(s["unit"], 2 * n)
                pe.matmul(bc_ps, m.spread[:, n % NU, :], m.rnT, start=True, stop=True).then_inc(s["bc"], 1)

            def scores(i):
                g, j = items[i % NI]
                q, k = QT[j], keys(j)
                if j == 0:
                    pe.wait_ge(s["unit"], 2 * (NU * (i // NI) + UG * (g + 1)))
                if i >= NS:
                    pe.wait_ge(s["exp"], i - NS + 1)
                mask = m.mlocal[0:q, 0 if j == 0 else 1, :].rearrange("p (h k) -> p h k", h=4)[:, :, 0:k]
                pe.matmul(s_ps[i % NS][0:q, 0:4 * k], m.ident16[0:q, 0:q], mask, start=True, stop=False,
                          skip_group_check=True)
                for h in range(4):
                    p = 2 * g + h // 2
                    mm = pe.matmul(s_ps[i % NS][0:q, h * k:(h + 1) * k], m.qr[:, p, QW * j:QW * j + q],
                                   m.kz[:, p, h % 2, QW * j:QW * j + k], start=False, stop=(h == 3),
                                   skip_group_check=True)
                mm.then_inc(s["score"], 1)

            def copied(i):
                pe.wait_ge(s["pta"] if by_act(i) else s["ptd"], copies(i))

            def turn(i):
                g, j = items[i % NI]
                q, k = QT[j], keys(j)
                pe.wait_ge(s["exp"], i + 1)
                if i >= 2:
                    copied(i - 2)
                for h in range(4):
                    mm = pe.transpose(pt_ps[i % 2][0:k, h * q:(h + 1) * q], m.pr[0:q, i % NS, h * k:(h + 1) * k],
                                      m.ident[0:q, 0:q])
                mm.then_inc(s["turn"], 1)

            def values(i):
                g, j = items[i % NI]
                q, k = QT[j], keys(j)
                copied(i)
                if i == 0:
                    pe.wait_ge(s["ones"], 1)
                else:
                    pe.wait_ge(s["norm"], i)
                for h in range(4):
                    mm = pe.matmul(pv_ps[0:q, h * (HDL + 1):(h + 1) * (HDL + 1)],
                                   m.pt[0:k, i % 2, h * q:(h + 1) * q], m.v[0:k, j, 4 * g + h, :],
                                   start=True, stop=True)
                mm.then_inc(s["pv"], 1)

            def turn_rows(i):
                g, j = items[i % NI]
                q = QT[j]
                pe.wait_ge(s["norm"], i + 1)
                if i:
                    pe.wait_ge(s["atev"], i)
                for k in range(2):
                    mm = pe.transpose(at_ps[:, k * q:(k + 1) * q], m.an[0:q, i % 2, k * P:(k + 1) * P],
                                      m.ident[0:q, 0:q])
                mm.then_inc(s["at"], 1)

            def project(r, kp):
                if kp == 0:
                    pe.wait_ge(s["unit"], 2 * NU * (r + 1))
                pe.wait_ge(s["atev"], r * NI + NQ * (kp // 2 + 1))
                pe.matmul(o_ps, m.wo[:, kp, :], m.attnT[:, kp, :], start=(kp == 0), stop=(kp == NO - 1),
                          skip_group_check=True).then_inc(s["wo"], 1)

            for r in range(LU):
                i0, n0, v0 = r * NI, r * NU, r * NV
                for n in range(NU):
                    if r == 0 or n >= 3:
                        proj(n0 + n)
                    if n in v_beside:
                        v_proj(v0 + v_beside.index(n))
                    if n:
                        sums(n0 + n - 1)
                sums(n0 + NU - 1)
                for i in v_left[:NV - len(v_beside) - 4]:
                    v_proj(v0 + i)
                pe.wait_ge(s["part"], 3 * (r + 1))
                if r:
                    pe.wait_ge(s["out"], r)
                for t in range(KT):
                    mm = pe.transpose(rt_ps[:, t * P:(t + 1) * P], m.parts[:, t, :, :].rearrange("p a u -> p (a u)"),
                                      m.ident16)
                mm.then_inc(s["rt"], 1)
                pe.wait_ge(s["rtev"], r + 1)
                for n in range(UG):
                    spread(n0 + n)
                    if n < 4:
                        v_proj(v0 + v_left[n - 4])
                pe.wait_ge(s["vev"], v0 + NV)
                for i in range(NI + 4):
                    if i < NI:
                        scores(i0 + i)
                    if 2 <= i < NI + 2:
                        turn(i0 + i - 2)
                    if 3 <= i < NI + 3:
                        values(i0 + i - 3)
                    if i >= 4:
                        turn_rows(i0 + i - 4)
                    if i < NI and unit_at(i) is not None:
                        spread(n0 + unit_at(i))
                    if 0 <= i - (G4 - 1) * NQ < NO - 2:
                        project(r, i - (G4 - 1) * NQ)
                    if i > NI and r + 1 < LU:
                        proj(n0 + NU + i - NI - 1)
                for kp in range(NO - 2, NO):
                    project(r, kp)


def feed_forward(nc, m, d, layer):
    half = D // 2
    NK = len(FK)
    NU = B * NK
    banks = ((6,), (7,), (7,))
    with stage(nc, "ffn", "w", "next", "rot", "zero", "xs", "g", "a", "ge", "h", "w2", "out", *NORM_SEMS) as (block, s):
        cs = [slice(c * T, (c + 1) * T) for c in range(B)]
        acc = m.ps[4:6]
        loads = [(m.lnp, d["p_lnp"][layer, :, :]), (m.b1, d["p_b1"][layer, :, :]), (m.w1, d["L0_ffn_W1"][layer, :, :]),
                 (m.w2, d["p_W2"][layer, :, :].rearrange("(k p) d -> p k d", p=P))]
        nexts = attention_loads(m, d, layer + 1)

        def shifted_at(c):
            return m.xsh[:, c % 2, :]

        @block.sync
        def _(sp):
            for dst, src in loads:
                sp.dma_start(dst, src).then_inc(s["w"], 16)
            for dst, src in nexts:
                sp.dma_start(dst, src).then_inc(s["next"], 16)

        @block.tensor
        def _(pe):
            mean, variance, spread = norm_pe(pe, m, s, shifted_at, lambda c: pe.wait_ge(s["xs"], 2 * c + 2), banks)

            def up(u):
                c, k = divmod(u, NK)
                f = FK[k]
                if k == 0:
                    pe.wait_ge(s["ln"], c + 1)
                if u >= 2:
                    pe.wait_ge(s["ge"], u - 1)
                pe.matmul(m.ps[u % 2][0:f, :], m.w1[:, DIN + k * P:DIN + k * P + f], m.xq[:, cs[c]],
                          start=True, stop=True).then_inc(s["g"], 1)
                if u >= 2:
                    pe.wait_ge(s["h"], u - 1)
                pe.matmul(m.ps[2 + u % 2][0:f, :], m.w1[:, k * P:k * P + f], m.xq[:, cs[c]],
                          start=True, stop=True).then_inc(s["a"], 1)

            def down(u):
                c, k = divmod(u, NK)
                f = FK[k]
                pe.wait_ge(s["h"], u + 1)
                if k == 0 and c >= 2:
                    pe.wait_ge(s["out"], c - 1)
                pe.matmul(acc[c % 2][:, :], m.w2[0:f, k, :], m.hid[0:f, u % 3, :], start=(k == 0),
                          stop=(k == NK - 1)).then_inc(s["w2"], 1)

            mean(0)
            variance(0)
            mean(1)
            spread(0)
            variance(1)
            pe.wait_ge(s["w"], 16 * len(loads))
            for u in range(NU + 2):
                c, k = divmod(u, NK)
                if u < NU:
                    up(u)
                if k == 1 and c + 1 < B:
                    spread(c + 1)
                if k == 1 and c + 2 < B:
                    mean(c + 2)
                if u >= 2:
                    down(u - 2)
                if k == 2 and c + 2 < B:
                    variance(c + 2)

        @block.scalar
        def _(act):
            square, deviation = norm_act(act, m, s, banks)
            for c in range(2):
                square(c)
                deviation(c)
            act.wait_ge(s["w"], 16 * len(loads))
            for u in range(NU):
                c, k = divmod(u, NK)
                f = FK[k]
                act.wait_ge(s["g"], u + 1)
                if u >= 2:
                    act.wait_ge(s["h"], u - 1)
                act.activation(m.ge[0:f, u % 2, :], m.ps[u % 2][0:f, :], ACT.Gelu, bias=m.b1[0:f, NK + k:NK + k + 1])\
                   .then_inc(s["ge"], 1)
                if k == 1 and c + 2 < B:
                    square(c + 2)
                if k == 2 and c + 2 < B:
                    deviation(c + 2)

        @block.vector
        def _(dve):
            centered, diagonal, normed = norm_dve(dve, m, s, shifted_at, m.xq, m.lnp[:, 0:1], m.lnp[:, 1:2], banks)

            def shifted(c):
                if c >= 2:
                    dve.wait_ge(s["xc"], c - 1)
                    dve.wait_ge(s["mean"], c - 1)
                dve.tensor_copy(m.xsh[0:half, c % 2, :], m.xn[0:half, cs[c]]).then_inc(s["xs"], 1)
                dve.tensor_copy(m.xsh[half:D, c % 2, 1:T], m.xn[half:D, c * T:(c + 1) * T - 1]).then_inc(s["xs"], 1)

            def hidden(u):
                k = u % NK
                f = FK[k]
                dve.wait_ge(s["ge"], u + 1)
                dve.wait_ge(s["a"], u + 1)
                if u >= 3:
                    dve.wait_ge(s["w2"], u - 2)
                dve.scalar_tensor_tensor(out=m.hid[0:f, u % 3, :], in0=m.ps[2 + u % 2][0:f, :],
                                         scalar=m.b1[0:f, k:k + 1], in1=m.ge[0:f, u % 2, :],
                                         op0=ALU.add, op1=ALU.mult).then_inc(s["h"], 1)

            def out(c):
                dve.wait_ge(s["w2"], NK * (c + 1))
                dve.scalar_tensor_tensor(out=m.xn[:, cs[c]], in0=acc[c % 2][:, :], scalar=m.lnp[:, 2:3],
                                         in1=m.xn[:, cs[c]], op0=ALU.add, op1=ALU.add).then_inc(s["out"], 1)

            dve.memset(m.xsh[:, :, 0:1], 0.0).then_inc(s["zero"], 1)
            dve.wait_ge(s["zero"], 1)
            shifted(0)
            shifted(1)
            for c in range(2):
                dve.wait_ge(s["xs"], 2 * c + 2)
                centered(c)
            diagonal(0)
            dve.wait_ge(s["w"], 16 * len(loads))
            normed(0)
            shifted(2)
            for c in range(B):
                hidden(NK * c)
                if c + 1 < B:
                    diagonal(c + 1)
                    normed(c + 1)
                if c + 2 < B:
                    dve.wait_ge(s["xs"], 2 * (c + 2) + 2)
                    centered(c + 2)
                for k in range(1, NK):
                    hidden(NK * c + k)
                if c + 3 < B:
                    shifted(c + 3)
                if c:
                    out(c - 1)
            out(B - 1)
            dve.wait_ge(s["next"], 16 * len(nexts))
            rotary_tables(dve, m).then_inc(s["rot"], 1)


def latent_attention(nc, m, d, b):
    here = bass.ds(b * T, T)
    NP_ = H1 // 2
    items = [(qt, h) for qt in range(KT) for h in range(H1)]
    NI = len(items)
    V0 = HDT
    with stage(nc, "lat", "xin", "lat", "latc", "v", "vev", "q", "qev", "k", "kev", "score", "nm", "exp", "turn",
               "pta", "ptd", "pv", "ri", "norm", "at", "atev", "wo", "out", "ids", "sent") as (block, s):
        a_ps, b_ps, v_ps = m.ps[0:2], m.ps[2:4], m.ps[4:6]
        s_ps, pt_ps, pv_ps, at_ps = m.ps[0:3], m.ps[3:5], m.ps[5:7], m.ps[7]
        NV = 2 * KT

        def by_act(i):
            return i % 2 == 0

        @block.gpsimd
        def _(pool):
            pool.wait_ge(s["ids"], 1)
            for t in range(KT):
                for j in range(2):
                    pool.indirect_dma_start(d["s_in"], bass.IndirectOffsetOnAxis(ap=m.slotb[:, j, t:t + 1], axis=0),
                                            m.xrb[:, t, :], None,
                                            bounds_check=SLOTS - 1, oob_is_err=False).then_inc(s["sent"], 16)
            pool.wait_ge(s["sent"], 16 * 2 * KT)
            pool.dma_reset()

        @block.vector
        def _(dve):
            dve.tensor_copy(m.xn_b, m.xn[:, here]).then_inc(s["xin"], 1)
            dve.tensor_copy(m.xrb, m.xr[:, bass.ds(b * KT, KT), :])
            dve.tensor_copy(m.slotb, m.slotu[:, :, bass.ds(b * KT, KT)]).then_inc(s["ids"], 1)
            for p in range(NP_):
                dve.wait_ge(s["k"], p + 1)
                for a in range(2):
                    r = slice(a * HD1, (a + 1) * HD1)
                    last = dve.tensor_copy(m.k1[r, p, a, :], b_ps[p % 2][r, :])
                last.then_inc(s["kev"], 1)

            def negmax(i):
                qt, h = items[i]
                dve.wait_ge(s["score"], i + 1)
                if i >= 3:
                    dve.wait_ge(s["exp"], i - 2)
                dve.tensor_reduce(m.nm[:, i % 3:i % 3 + 1], s_ps[i % 3][:, 0:(qt + 1) * P], AX.X, ALU.max,
                                  negate=True).then_inc(s["nm"], 1)

            def probs_t(i):
                qt, h = items[i]
                if by_act(i):
                    return
                dve.wait_ge(s["turn"], i + 1)
                if i >= 3:
                    dve.wait_ge(s["pv"], i - 2)
                dve.tensor_copy(m.pt[:, i % 3, 0:(qt + 1) * P], pt_ps[i % 2][:, 0:(qt + 1) * P]).then_inc(s["ptd"], 1)

            def normed(g):
                qt, h = items[4 * g]
                pv = pv_ps[g % 2][:, 0:4 * (HD1 + 1)].rearrange("p (h c) -> p h c", h=4)
                dve.wait_ge(s["pv"], 4 * g + 4)
                dve.reciprocal(m.ri[:, g % 2, :], pv[:, :, HD1]).then_inc(s["ri"], 1)
                dve.wait_ge(s["ri"], g + 1)
                if h == 0 and qt >= 2:
                    dve.wait_ge(s["at"], 2 * (qt - 1))
                dve.tensor_tensor(m.an[:, qt % 2, h * HD1:(h + 4) * HD1].rearrange("p (h c) -> p h c", h=4),
                                  pv[:, :, 0:HD1], m.ri[:, g % 2, :].unsqueeze(2).to_broadcast([P, 4, HD1]),
                                  ALU.mult).then_inc(s["norm"], 1)

            for i in range(NI + 4):
                if i < NI:
                    negmax(i)
                if 2 <= i < NI + 2:
                    probs_t(i - 2)
                if i >= 4 and (i - 4) % 4 == 3:
                    normed((i - 4) // 4)
            dve.wait_ge(s["wo"], 1)
            dve.tensor_tensor(m.xsum[:, here], m.ps[0], m.xsum[:, here], ALU.add).then_inc(s["out"], 1)

        @block.scalar
        def _(act):
            act.wait_ge(s["lat"], 1)
            act.activation(m.lat, m.ps[7], ACT.Copy).then_inc(s["latc"], 1)
            for p in range(NP_):
                act.wait_ge(s["q"], p + 1)
                act.activation(m.q1[:, p, :], a_ps[p % 2], ACT.Copy, scale=float(HD1) ** -0.5).then_inc(s["qev"], 1)
                act.wait_ge(s["v"], p + 1)
                kt, c = p // 2, p % 2
                act.activation(m.v1[:, kt, 8 * c:8 * c + 8, 0:HD1], v_ps[p % 2].rearrange("p (h c) -> p h c", h=8),
                               ACT.Copy).then_inc(s["vev"], 1)

            def probs_t(i):
                qt, h = items[i]
                if not by_act(i):
                    return
                act.wait_ge(s["turn"], i + 1)
                if i >= 3:
                    act.wait_ge(s["pv"], i - 2)
                act.activation(m.pt[:, i % 3, 0:(qt + 1) * P], pt_ps[i % 2][:, 0:(qt + 1) * P], ACT.Copy)\
                   .then_inc(s["pta"], 1)

            def turned_rows(qt):
                for c in range(2):
                    act.wait_ge(s["at"], 2 * qt + c + 1)
                    act.activation(m.attnT[:, 4 * c:4 * c + 4, qt * P:(qt + 1) * P],
                                   at_ps.rearrange("p (k q) -> p k q", k=4), ACT.Copy).then_inc(s["atev"], 1)

            for i in range(NI + 2):
                if i < NI:
                    qt, h = items[i]
                    act.wait_ge(s["nm"], i + 1)
                    if i >= 3:
                        act.wait_ge(s["turn"], i - 2)
                    act.activation(m.pr[:, i % 3, 0:(qt + 1) * P], s_ps[i % 3][:, 0:(qt + 1) * P], ACT.Exp,
                                   bias=m.nm[:, i % 3:i % 3 + 1]).then_inc(s["exp"], 1)
                if i >= 2:
                    probs_t(i - 2)
                if i % H1 == 7 and i > H1:
                    turned_rows(i // H1 - 1)
            turned_rows(KT - 1)

        @block.tensor
        def _(pe):
            pe.wait_ge(s["xin"], 1)
            pe.matmul(m.ps[7], m.w_kvd, m.xn_b, start=True, stop=True).then_inc(s["lat"], 1)
            pe.wait_ge(s["latc"], 1)
            for p in range(NP_):
                if p >= 2:
                    pe.wait_ge(s["qev"], p - 1)
                pe.matmul(a_ps[p % 2], m.w_q1[:, p * P:(p + 1) * P], m.xn_b, start=True, stop=True).then_inc(s["q"], 1)
                if p >= 2:
                    pe.wait_ge(s["kev"], p - 1)
                pe.matmul(b_ps[p % 2], m.w_kvu[:, p * P:(p + 1) * P], m.lat, start=True, stop=True).then_inc(s["k"], 1)
                if p >= 2:
                    pe.wait_ge(s["vev"], p - 1)
                kt, c = p // 2, p % 2
                pe.matmul(v_ps[p % 2], m.lat[:, kt * P:(kt + 1) * P], m.w_kvu[:, V0 + 512 * c:V0 + 512 * (c + 1)],
                          start=True, stop=True).then_inc(s["v"], 1)

            def scores(i):
                qt, h = items[i]
                nk = (qt + 1) * P
                if i == 0:
                    pe.wait_ge(s["qev"], NP_)
                    pe.wait_ge(s["kev"], NP_)
                    pe.wait_ge(s["vev"], NV)
                if i >= 3:
                    pe.wait_ge(s["exp"], i - 2)
                pe.matmul(s_ps[i % 3][:, 0:nk], m.q1[:, h // 2, qt * P:(qt + 1) * P], m.k1[:, h // 2, h % 2, 0:nk],
                          start=True, stop=False, skip_group_check=True)
                pe.matmul(s_ps[i % 3][:, qt * P:nk], m.ident16, m.mcausal, start=False, stop=True,
                          skip_group_check=True).then_inc(s["score"], 1)

            def copied(i):
                pe.wait_ge(s["pta"] if by_act(i) else s["ptd"], i // 2 + 1)

            def turn(i):
                qt, h = items[i]
                pe.wait_ge(s["exp"], i + 1)
                if i >= 2:
                    copied(i - 2)
                for kt in range(qt + 1):
                    mm = pe.transpose(pt_ps[i % 2][:, kt * P:(kt + 1) * P], m.pr[:, i % 3, kt * P:(kt + 1) * P],
                                      m.ident)
                mm.then_inc(s["turn"], 1)

            def values(i):
                qt, h = items[i]
                copied(i)
                if h % 4 == 0 and i >= 8:
                    pe.wait_ge(s["norm"], i // 4 - 1)
                c = h % 4 * (HD1 + 1)
                for kt in range(qt + 1):
                    mm = pe.matmul(pv_ps[i // 4 % 2][:, c:c + HD1 + 1], m.pt[:, i % 3, kt * P:(kt + 1) * P], m.v1[:, kt, h, :],
                                   start=(kt == 0), stop=(kt == qt), skip_group_check=True)
                mm.then_inc(s["pv"], 1)

            def turn_rows(qt):
                pe.wait_ge(s["norm"], 4 * qt + 4)
                for c in range(2):
                    if qt or c:
                        pe.wait_ge(s["atev"], 2 * qt + c)
                    for k in range(4):
                        kp = 4 * c + k
                        mm = pe.transpose(at_ps[:, k * P:(k + 1) * P], m.an[:, qt % 2, kp * P:(kp + 1) * P], m.ident)
                    mm.then_inc(s["at"], 1)

            for i in range(NI + 3):
                if i < NI:
                    scores(i)
                if 2 <= i < NI + 2:
                    turn(i - 2)
                if i >= 3:
                    values(i - 3)
                if i % H1 == 7 and i > H1:
                    turn_rows(i // H1 - 1)
            turn_rows(KT - 1)
            pe.wait_ge(s["atev"], 2 * KT)
            for kp in range(NP_):
                mm = pe.matmul(m.ps[0], m.w_o1[:, kp, :], m.attnT[:, kp, :], start=(kp == 0), stop=(kp == NP_ - 1))
            mm.then_inc(s["wo"], 1)


def load_latent(nc, m, d):
    loads = [(m.w_kvd, d["L1_attn_w_kv_down"]), (m.w_kvu, d["L1_attn_w_kv_up"]), (m.w_q1, d["L1_attn_w_q"]),
             (m.w_o1, d["L1_attn_w_out"].rearrange("(k p) d -> p k d", p=P))]
    with stage(nc, "lload", "loaded", "set", "z", "zeroed") as (block, s):
        @block.gpsimd
        def _(pool):
            pool.memset(m.zrow, 0.0).then_inc(s["z"], 1)
            pool.wait_ge(s["z"], 1)
            pool.dma_start(d["s_in"][0:SLOTS, :].rearrange("(p a) d -> p a d", p=P),
                           m.zrow.unsqueeze(1).to_broadcast([P, SLOTS // P, D])).then_inc(s["zeroed"], 16)
            pool.dma_start(d["s_out"][SLOTS:SLOTS + 1, :], m.zrow[0:1, :]).then_inc(s["zeroed"], 16)
            pool.wait_ge(s["zeroed"], 32)

        @block.sync
        def _(sp):
            for dst, src in loads:
                sp.dma_start(dst, src).then_inc(s["loaded"], 16)
            sp.wait_ge(s["loaded"], 16 * len(loads))

        @block.vector
        def _(dve):
            dve.memset(m.k1, 0.0)
            dve.memset(m.v1, 1.0).then_inc(s["set"], 1)


def token_rows(nc, m, src, dst, label):
    with stage(nc, label, "turned", "kept") as (block, s):
        @block.tensor
        def _(pe):
            for c in range(B):
                if c >= 4:
                    pe.wait_ge(s["kept"], c - 3)
                for t in range(KT):
                    mm = pe.transpose(m.ps[c % 4][:, t * P:(t + 1) * P], src[:, c * T + t * P:c * T + (t + 1) * P],
                                      m.ident)
                mm.then_inc(s["turned"], 1)

        @block.vector
        def _(dve):
            for c in range(B):
                dve.wait_ge(s["turned"], c + 1)
                dve.tensor_copy(dst[:, c * KT:(c + 1) * KT, :].rearrange("p t d -> p (t d)"), m.ps[c % 4])\
                   .then_inc(s["kept"], 1)


def token_stats(nc, m):
    with stage(nc, "stats", "dve", "sq", "root") as (block, s):
        st = lambda i: m.stats[:, :, i]
        mean_b = m.stats[:, :, 0:1].to_broadcast([P, NT, D])

        @block.vector
        def _(dve):
            dve.tensor_reduce(st(0), m.xr, AX.X, ALU.add).then_inc(s["dve"], 1)
            dve.tensor_reduce(st(2), m.xr, AX.X, ALU.min).then_inc(s["dve"], 1)
            dve.tensor_reduce(st(3), m.xr, AX.X, ALU.max).then_inc(s["dve"], 1)
            dve.wait_ge(s["sq"], 1)
            dve.tensor_reduce(m.red[:, 0, :], m.sqr, AX.X, ALU.add).then_inc(s["dve"], 1)
            dve.wait_ge(s["dve"], 4)
            dve.tensor_scalar(st(0), st(0), 1.0 / D, None, ALU.mult).then_inc(s["dve"], 1)
            dve.tensor_scalar(m.sqr, m.xr, 1e-6, None, ALU.is_lt).then_inc(s["dve"], 1)
            dve.wait_ge(s["dve"], 6)
            dve.scalar_tensor_tensor(out=m.sqr, in0=m.xr, scalar=-1e-6, in1=m.sqr, op0=ALU.is_gt, op1=ALU.mult)\
               .then_inc(s["dve"], 1)
            dve.wait_ge(s["dve"], 7)
            dve.tensor_reduce(st(5), m.sqr, AX.X, ALU.add).then_inc(s["dve"], 1)
            dve.wait_ge(s["dve"], 8)
            dve.tensor_scalar(st(5), st(5), 1.0 / D, None, ALU.mult).then_inc(s["dve"], 1)
            dve.tensor_tensor(m.sqr, m.xr, mean_b, ALU.subtract).then_inc(s["dve"], 1)
            dve.wait_ge(s["sq"], 2)
            dve.tensor_reduce(m.red[:, 1, :], m.sqr, AX.X, ALU.add).then_inc(s["dve"], 1)

        @block.scalar
        def _(act):
            act.activation(m.sqr, m.xr, ACT.Square).then_inc(s["sq"], 1)
            act.wait_ge(s["dve"], 10)
            act.activation(m.sqr, m.sqr, ACT.Square).then_inc(s["sq"], 1)
            act.activation(st(4), m.red[:, 0, :], ACT.Sqrt, bias=m.zcol).then_inc(s["root"], 1)
            act.wait_ge(s["dve"], 11)
            act.activation(st(1), m.red[:, 1, :], ACT.Sqrt, bias=m.zcol, scale=1.0 / (D - 1)).then_inc(s["root"], 1)


def router(nc, m, d):
    with stage(nc, "router", "w", "st", "stev", "h", "hid", "lg", "lgev", "nm", "sub", "exp", "sum", "ri",
               "probs") as (block, s):
        loads = [(m.r1, d["p_r1"]), (m.r1s, d["p_r1s"]), (m.r1b, d["p_r1b"]), (m.r2, d["p_r2"])]

        @block.sync
        def _(sp):
            for dst, src in loads:
                sp.dma_start(dst, src).then_inc(s["w"], 16)

        @block.tensor
        def _(pe):
            for c in range(B):
                if c >= 2:
                    pe.wait_ge(s["stev"], c - 1)
                for t in range(KT):
                    mm = pe.transpose(m.ps[c % 2][0:NSTAT, t * P:(t + 1) * P], m.stats[:, c * KT + t, :], m.ident)
                mm.then_inc(s["st"], 1)
            pe.wait_ge(s["w"], 16 * len(loads))

            def logits(c):
                pe.wait_ge(s["hid"], c + 1)
                for t in range(KT):
                    i = c * KT + t
                    mm = pe.matmul(m.ps[4 + i // 16][:, i % 16 * E:(i % 16 + 1) * E], m.rh[:, c % 2, t * P:(t + 1) * P],
                                   m.r2, start=True, stop=True)
                mm.then_inc(s["lg"], 1)

            for c in range(B):
                if c >= 2:
                    pe.wait_ge(s["hid"], c - 1)
                pe.wait_ge(s["stev"], c + 1)
                pe.matmul(m.ps[2 + c % 2][0:RH, :], m.r1, m.xn[:, c * T:(c + 1) * T], start=True, stop=False)
                pe.matmul(m.ps[2 + c % 2][0:RH, :], m.r1s, m.statT[:, c * T:(c + 1) * T], start=False, stop=True)\
                  .then_inc(s["h"], 1)
                if c:
                    logits(c - 1)
            logits(B - 1)

        @block.scalar
        def _(act):
            for c in range(B):
                act.wait_ge(s["h"], c + 1)
                if c >= 2:
                    act.wait_ge(s["lg"], c - 1)
                act.activation(m.rh[:, c % 2, :], m.ps[2 + c % 2][0:RH, :], ACT.Gelu, bias=m.r1b).then_inc(s["hid"], 1)
            act.wait_ge(s["sub"], 1)
            act.activation(m.probs, m.probs, ACT.Exp).then_inc(s["exp"], 1)

        @block.vector
        def _(dve):
            for c in range(B):
                dve.wait_ge(s["st"], c + 1)
                dve.tensor_copy(m.statT[:, c * T:(c + 1) * T], m.ps[c % 2][0:NSTAT, :]).then_inc(s["stev"], 1)
            dve.wait_ge(s["lg"], B)
            for i in range(2):
                dve.tensor_copy(m.probs[:, 16 * i:16 * i + 16, :].rearrange("p t e -> p (t e)"), m.ps[4 + i])\
                   .then_inc(s["lgev"], 1)
            dve.wait_ge(s["lgev"], 2)
            dve.tensor_reduce(m.red[:, 0, :], m.probs, AX.X, ALU.max).then_inc(s["nm"], 1)
            dve.wait_ge(s["nm"], 1)
            over = lambda a: a.unsqueeze(2).to_broadcast([P, NT, E])
            dve.tensor_tensor(m.probs, m.probs, over(m.red[:, 0, :]), ALU.subtract).then_inc(s["sub"], 1)
            dve.wait_ge(s["exp"], 1)
            dve.tensor_reduce(m.red[:, 1, :], m.probs, AX.X, ALU.add).then_inc(s["sum"], 1)
            dve.wait_ge(s["sum"], 1)
            dve.reciprocal(m.red[:, 2, :], m.red[:, 1, :]).then_inc(s["ri"], 1)
            dve.wait_ge(s["ri"], 1)
            dve.tensor_tensor(m.probs, m.probs, over(m.red[:, 2, :]), ALU.mult).then_inc(s["probs"], 1)


def route(nc, m, d):
    S4 = N // 4
    with stage(nc, "route", "io", "top", "idx", "hot", "msk", "t", "tev", "m8", "mr", "seg", "fin", "thr", "cmp",
               "back", "bev", "sl", "w") as (block, s):
        NTOP = CAP // 8

        @block.gpsimd
        def _(pool):
            pool.iota(m.eiota, [[1, E]], base=0, channel_multiplier=0,
                      allow_small_or_imprecise_dtypes=True).then_inc(s["io"], 1)
            pool.iota(m.ebase, [[0, 1]], base=0, channel_multiplier=CAP,
                      allow_small_or_imprecise_dtypes=True).then_inc(s["io"], 1)

        @block.tensor
        def _(pe):
            pe.wait_ge(s["msk"], 1)
            for i in range(B):
                if i >= 4:
                    pe.wait_ge(s["tev"], i - 3)
                for t in range(KT):
                    mm = pe.transpose(m.ps[i % 4][0:E, t * P:(t + 1) * P], m.score[:, i * KT + t, :], m.ident)
                mm.then_inc(s["t"], 1)
            pe.wait_ge(s["sl"], 1)
            for i in range(NT):
                mm = pe.transpose(m.ps[4 + i // 16][:, i % 16 * E:(i % 16 + 1) * E], m.slotE[:, i * P:(i + 1) * P],
                                  m.ident[0:E, 0:E])
            mm.then_inc(s["back"], 1)

        @block.vector
        def _(dve):
            step = [0]

            def then(ins):
                step[0] += 1
                ins.then_inc(s["w"], 1)
                dve.wait_ge(s["w"], step[0])

            for i in range(NT):
                last = dve.max(m.top8[:, i, :], m.probs[:, i, :])
            then(last)
            for i in range(NT):
                last = dve.max_index(m.idx8[:, i, :], m.top8[:, i, :], m.probs[:, i, :])
            then(last)
            then(dve.tensor_copy(m.idxf, m.idx8[:, :, 0:2]))
            dve.wait_ge(s["io"], 2)
            es = m.eiota.unsqueeze(1).to_broadcast([P, NT, E])
            for j in range(2):
                last = dve.tensor_tensor(m.hot[:, j, :, :], es, m.idxf[:, :, j:j + 1].to_broadcast([P, NT, E]),
                                         ALU.is_equal)
            then(last)
            then(dve.tensor_tensor(m.score, m.hot[:, 0, :, :], m.hot[:, 1, :, :], ALU.add))
            then(dve.tensor_tensor(m.tmpn, m.probs, m.score, ALU.mult))
            then(dve.tensor_scalar(m.score, m.score, -1.0, None, ALU.add))
            dve.tensor_tensor(m.score, m.score, m.tmpn, ALU.add).then_inc(s["msk"], 1)
            for i in range(B):
                dve.wait_ge(s["t"], i + 1)
                dve.tensor_copy(m.scoreE[:, i * T:(i + 1) * T], m.ps[i % 4][0:E, :]).then_inc(s["tev"], 1)
            dve.wait_ge(s["tev"], B)
            for q in range(4):
                last = dve.tensor_copy(m.quart[q * E:(q + 1) * E, :], m.scoreE[:, q * S4:(q + 1) * S4])
            then(last)
            for r in range(NTOP):
                then(dve.max(m.best[:, 8 * r:8 * r + 8], m.quart))
                then(dve.match_replace(out=m.quart, in_to_replace=m.best[:, 8 * r:8 * r + 8], in_values=m.quart,
                                       imm_value=-2.0))
            for q in range(4):
                last = dve.tensor_copy(m.cand[:, q * CAP:(q + 1) * CAP], m.best[q * E:(q + 1) * E, :])
            then(last)
            for r in range(NTOP):
                then(dve.max(m.b8, m.cand))
                if r < NTOP - 1:
                    then(dve.match_replace(out=m.cand, in_to_replace=m.b8, in_values=m.cand, imm_value=-2.0))
            thr = m.b8[:, 7:8]
            then(dve.tensor_scalar(m.gt, m.scoreE, thr, None, ALU.is_gt))
            dve.tensor_scalar(m.eq, m.scoreE, thr, None, ALU.is_equal)
            then(dve.tensor_reduce(m.cnt, m.gt, AX.X, ALU.add))
            then(dve.tensor_scalar(m.room, m.cnt, -1.0, float(CAP), ALU.mult, ALU.add))
            then(dve.tensor_tensor_scan(m.run, m.eq, m.eq, 0.0, ALU.add, ALU.bypass))
            then(dve.tensor_scalar(m.run, m.run, m.room, None, ALU.is_le))
            then(dve.tensor_tensor(m.run, m.run, m.eq, ALU.mult))
            then(dve.tensor_tensor(m.gt, m.gt, m.run, ALU.add))
            then(dve.tensor_scalar(m.eq, m.scoreE, 0.0, None, ALU.is_ge))
            then(dve.tensor_tensor(m.gt, m.gt, m.eq, ALU.mult))
            then(dve.tensor_tensor_scan(m.run, m.gt, m.gt, 0.0, ALU.add, ALU.bypass))
            then(dve.tensor_scalar(m.run, m.run, m.ebase, None, ALU.add))
            dve.tensor_tensor(m.slotE, m.run, m.gt, ALU.mult).then_inc(s["sl"], 1)
            dve.wait_ge(s["back"], 1)
            for i in range(2):
                last = dve.tensor_copy(m.slotN[:, 16 * i:16 * i + 16, :].rearrange("p t e -> p (t e)"), m.ps[4 + i])
            then(last)
            for j in range(2):
                then(dve.tensor_tensor(m.tmpn, m.hot[:, j, :, :], m.slotN, ALU.mult))
                then(dve.tensor_reduce(m.slot[:, j, :], m.tmpn, AX.X, ALU.add))
            then(dve.tensor_tensor(m.red[:, 0, :], m.top8[:, :, 0], m.top8[:, :, 1], ALU.add))
            then(dve.reciprocal(m.red[:, 1, :], m.red[:, 0, :]))
            for j in range(2):
                then(dve.tensor_tensor(m.wt[:, j, :], m.top8[:, :, j], m.red[:, 1, :], ALU.mult))
            then(dve.tensor_scalar(m.keep, m.slot, 1.0, None, ALU.is_ge))
            then(dve.tensor_tensor(m.wt, m.wt, m.keep, ALU.mult))
            then(dve.tensor_scalar(m.keep, m.keep, -float(SLOTS + 1), float(SLOTS), ALU.mult, ALU.add))
            then(dve.tensor_tensor(m.slot, m.slot, m.keep, ALU.add))
            then(dve.tensor_copy(m.slotu, m.slot))


def experts(nc, m, d, i):
    E2 = E // GRP
    NX = GU * E2
    NP_ = 3
    C2 = CAP - P
    parts = ((0, P), (P, CAP))
    with stage(nc, "moe", *[f"load{n}" for n in range(GU)], "xt", "xtev", "up", "act", "hid", "y", "yev", "out0",
               "out1") as (block, s):
        def slot_rows(t, n, part):
            rows = t[bass.ds((i * GU + n) * E2 * CAP, E2 * CAP), :].rearrange("(e r) d -> r e d", e=E2)
            return rows[parts[part][0]:parts[part][1], :, :]

        @block.sync
        def _(sp):
            for n in range(GU):
                g = i * GU + n
                for dst, src in (
                    (m.xe[:, n, 0, :, :], slot_rows(d["s_in"], n, 0)),
                    (m.xe[0:C2, n, 1, :, :], slot_rows(d["s_in"], n, 1)),
                    (m.wup[:, n, :, :], d["p_wup"][bass.ds(g * E2, E2), :, :].rearrange("e p c -> p e c")),
                    (m.aup[:, n, :], d["p_aup"][g, :, :]),
                    (m.wdn[:, n, :, :], d["p_wdn"][bass.ds(g * E2, E2), :, :].rearrange("e (k p) d -> p (e k) d", p=P)),
                    (m.adn[:, n, :], d["p_adn"][g, :, :]),
                ):
                    sp.dma_start(dst, src).then_inc(s[f"load{n}"], 16)
            for n in range(GU):
                sp.wait_ge(s["yev"], 2 * E2 * (n + 1))
                for part in range(2):
                    sp.dma_start(slot_rows(d["s_out"], n, part), m.ye[0:parts[part][1] - parts[part][0], n % 2, part, :, :])\
                      .then_inc(s[f"out{n % 2}"], 16)
            for z in range(2):
                sp.wait_ge(s[f"out{z}"], 16 * 2 * (GU // 2))

        @block.tensor
        def _(pe):
            def turn(x):
                n, e = divmod(x, E2)
                pe.wait_ge(s[f"load{n}"], 16 * 6)
                if x >= 2:
                    pe.wait_ge(s["xtev"], x - 1)
                pe.transpose(m.ps[x % 2][:, 0:P], m.xe[:, n, 0, e, :], m.ident)
                pe.transpose(m.ps[x % 2][:, P:CAP], m.xe[0:C2, n, 1, e, :], m.ident[0:C2, 0:C2]).then_inc(s["xt"], 1)

            def up(x):
                n, e = divmod(x, E2)
                pe.wait_ge(s["xtev"], x + 1)
                for k in range(NP_):
                    u = NP_ * x + k
                    if u >= 2:
                        pe.wait_ge(s["hid"], u - 1)
                    wg = m.wup[:, n, e, k * P:(k + 1) * P] if k < 2 else m.aup[:, n, 0:P]
                    wv = m.wup[:, n, e, INTER + k * P:INTER + (k + 1) * P] if k < 2 else m.aup[:, n, P:2 * P]
                    pe.matmul(m.ps[2 + u % 2][:, 0:CAP], wg, m.xeT[:, x % 2, :], start=True, stop=True)
                    pe.matmul(m.ps[4 + u % 2][:, 0:CAP], wv, m.xeT[:, x % 2, :], start=True, stop=True)\
                      .then_inc(s["up"], 1)

            def down(x):
                n, e = divmod(x, E2)
                pe.wait_ge(s["hid"], NP_ * (x + 1))
                for part, (a, b2) in enumerate(parts):
                    if x:
                        pe.wait_ge(s["yev"], 2 * (x - 1) + part + 1)
                    for k in range(NP_):
                        w = m.wdn[:, n, 2 * e + k, :] if k < 2 else m.adn[:, n, :]
                        mm = pe.matmul(m.ps[6 + part][0:b2 - a, 0:D], m.hm[:, x % 2, k, a:b2], w, start=(k == 0),
                                       stop=(k == NP_ - 1))
                    mm.then_inc(s["y"], 1)

            turn(0)
            for x in range(NX + 1):
                if x + 1 < NX:
                    turn(x + 1)
                if x < NX:
                    up(x)
                if x:
                    down(x - 1)

        @block.scalar
        def _(act):
            for u in range(NP_ * NX):
                act.wait_ge(s["up"], u + 1)
                if u >= 2:
                    act.wait_ge(s["hid"], u - 1)
                act.activation(m.sg[:, u % 2, :], m.ps[2 + u % 2][:, 0:CAP], ACT.Silu).then_inc(s["act"], 1)

        @block.vector
        def _(dve):
            def turned(x):
                dve.wait_ge(s["xt"], x + 1)
                if x >= 2:
                    dve.wait_ge(s["up"], NP_ * (x - 1))
                dve.tensor_copy(m.xeT[:, x % 2, :], m.ps[x % 2][:, 0:CAP]).then_inc(s["xtev"], 1)

            turned(0)
            for x in range(NX + 1):
                if x + 1 < NX:
                    turned(x + 1)
                for k in range(NP_ if x < NX else 0):
                    dve.wait_ge(s["act"], NP_ * x + k + 1)
                    if x >= 2 and k == 0:
                        dve.wait_ge(s["y"], 2 * (x - 1))
                    dve.scalar_tensor_tensor(out=m.hm[:, x % 2, k, :], in0=m.sg[:, (NP_ * x + k) % 2, :],
                                             scalar=ADAPT if k == 2 else 1.0,
                                             in1=m.ps[4 + (NP_ * x + k) % 2][:, 0:CAP], op0=ALU.mult,
                                             op1=ALU.mult).then_inc(s["hid"], 1)
                if x:
                    n, e = divmod(x - 1, E2)
                    if e == 0 and n >= 2:
                        dve.wait_ge(s[f"out{n % 2}"], 16 * 2 * (n // 2))
                    for part, (a, b2) in enumerate(parts):
                        dve.wait_ge(s["y"], 2 * (x - 1) + part + 1)
                        dve.tensor_copy(m.ye[0:b2 - a, n % 2, part, e, :], m.ps[6 + part][0:b2 - a, 0:D])\
                           .then_inc(s["yev"], 1)


def combine(nc, m, d):
    with stage(nc, "comb", "got0", "got1", "got2", "got3", "acc", "out") as (block, s):
        got = [s["got0"], s["got1"], s["got2"], s["got3"]]
        RING = len(got)

        @block.gpsimd
        def _(pool):
            for i in range(NT):
                if i >= RING:
                    pool.wait_ge(s["acc"], 2 * (i - RING) + 2)
                for j in range(2):
                    pool.indirect_dma_start(m.yt[:, i % RING, j, :], None, d["s_out"],
                                            bass.IndirectOffsetOnAxis(ap=m.slotu[:, j, i:i + 1], axis=0))\
                        .then_inc(got[i % RING], 16)

        @block.vector
        def _(dve):
            for i in range(NT):
                for j in range(2):
                    dve.wait_ge(got[i % RING], 32 * (i // RING + 1))
                    if j:
                        dve.wait_ge(s["acc"], 2 * i + 1)
                    dve.scalar_tensor_tensor(out=m.xo[:, i, :], in0=m.yt[:, i % RING, j, :], scalar=m.wt[:, j, i:i + 1],
                                             in1=m.xo[:, i, :], op0=ALU.mult, op1=ALU.add).then_inc(s["acc"], 1)

        @block.sync
        def _(sp):
            o = d["out"].rearrange("b (t p) d -> b p t d", p=P)
            for b in range(B):
                sp.wait_ge(s["acc"], 2 * KT * (b + 1))
                sp.dma_start(o[b], m.xo[:, b * KT:(b + 1) * KT, :]).then_inc(s["out"], 16)
            sp.wait_ge(s["out"], 16 * B)


def build(nc, d):
    d["s_in"] = nc.dram_tensor("slot_rows", (SLOTS, D), F32, kind="Internal").ap()
    d["s_out"] = nc.dram_tensor("slot_results", (SLOTS + 1, D), F32, kind="Internal").ap()
    with ExitStack() as ctx:
        m = Memory()
        times = {}

        def sb(scope, name, shape, dt=F32):
            times[name] = times.get(name, 0) + 1
            t = scope.enter_context(nc.sbuf_tensor(f"{name}_{times[name]}", shape, dt))
            return t[tuple(slice(None) for _ in shape)]

        psum = ctx.enter_context(nc.psum_tensor("banks", [P, 8, T], F32))
        m.ps = [psum[:, i, :] for i in range(8)]
        m.ps2 = [psum[:, 2 * i:2 * i + 2, :] for i in range(4)]

        m.xsum = sb(ctx, "xsum", [P, N])
        m.xn = sb(ctx, "xn", [P, N])
        m.ident = sb(ctx, "ident", [P, P])
        m.onesm = sb(ctx, "onesm", [P, P])
        m.ones = sb(ctx, "ones", [P, T])
        m.heads = sb(ctx, "heads", [P, 2])
        m.eps = sb(ctx, "eps", [P, 1])
        m.zcol = sb(ctx, "zcol", [P, 1])
        m.tbias = sb(ctx, "tbias", [P, 1])
        m.ident16 = sb(ctx, "ident16", [P, P], BF16)
        m.spread = sb(ctx, "spread", [3 * 2 * HL, HL, P], BF16)
        m.mcausal = sb(ctx, "mcausal", [P, P], BF16)
        m.mlocal = sb(ctx, "mlocal", [P, 2, 4 * P], BF16)

        with ExitStack() as front:
            m.xq = sb(front, "xq", [P, N])
            m.xcsd = sb(front, "xcsd", [P, 4, T])
            m.sq = sb(front, "sq", [P, 2, T])
            m.rs = sb(front, "rs", [P, 2, T])
            m.sdn = sb(front, "sdn", [P, B, KT])
            m.rsn = sb(front, "rsn", [P, B, KT])
            m.xc, m.sd = m.xcsd[:, 0:2, :], m.xcsd[:, 2:4, :]
            m.xc3, m.diag = m.xcsd[:, 0:3, :], m.rs
            with ExitStack() as scope:
                m.xrow = sb(scope, "xrow", [P, NT, D])
                m.w_q0 = sb(scope, "w_q0", [D, D])
                m.w_k0 = sb(scope, "w_k0", [D, D])
                m.w_v0 = sb(scope, "w_v0", [D, D])
                m.w_o0 = sb(scope, "w_o0", [D, D])
                m.bones8 = sb(scope, "bones8", [P, P])
                m.hmask = sb(scope, "hmask", [P, H0])
                m.g_q0 = sb(scope, "g_q0", [P, 1])
                m.g_k0 = sb(scope, "g_k0", [P, 1])
                m.b_o0 = sb(scope, "b_o0", [P, 1])
                m.gamma0 = sb(scope, "gamma0", [P, 1])
                m.beta0 = sb(scope, "beta0", [P, 1])
                m.gq_blk = sb(scope, "gq_blk", [P, P])
                m.gk_blk = sb(scope, "gk_blk", [P, P])
                m.spread_f = sb(scope, "spread_f", [3 * 2 * HL, HL, P])
                m.mcausal_f = sb(scope, "mcausal_f", [P, P])
                m.mlocal_f = sb(scope, "mlocal_f", [P, 2, 4 * P])
                m.vbd = sb(scope, "vbd", [P, KT, H0 * (P + HD0)])
                m.vp = sb(scope, "vp", [P, T])
                m.xq_b = sb(scope, "xq_b", [P, T])
                m.xn_b = sb(scope, "xn_b", [P, T])
                m.qh = sb(scope, "qh", [P, T])
                m.kh = sb(scope, "kh", [P, T])
                m.rest = sb(scope, "rest", [P, 2, T])
                m.parts0 = sb(scope, "parts0", [P, 2, 2, 3, T], BF16)
                m.stack = sb(scope, "stack", [P, 2, 2, T], BF16)
                m.pat = sb(scope, "pat", [P, 2, 3, 9 * HD0])
                m.select = sb(scope, "select", [P, 2, H0, 3, 9 * HD0], BF16)
                m.tanh = sb(scope, "tanh", [P, 3, 2, T])
                m.gateq = sb(scope, "gateq", [P, 2, T])
                m.gatek = sb(scope, "gatek", [P, T])
                m.fused = sb(scope, "fused", [P, T])
                load_constants(nc, m, d)
                load_x(nc, m, d)
                layer_norm_all(nc, m, m.xsum, m.xn, label="ln1")
                layer_norm_all(nc, m, m.xn, m.xq, m.gamma0, m.beta0, label="ln2")
                with nc.Fori(0, B // RU) as b:
                    resonance_attention(nc, m, b)

            with ExitStack() as scope:
                m.wqkv = sb(scope, "wqkv", [P, 3 * INNER])
                m.wo = sb(scope, "wo", [P, HL // 2, D])
                m.w1 = sb(scope, "w1", [P, 2 * DIN])
                m.w2 = sb(scope, "w2", [P, 3, D])
                m.b1 = sb(scope, "b1", [P, 6])
                m.lnp = sb(scope, "lnp", [P, 3])
                m.qks = sb(scope, "qks", [P, 2])
                m.rot0 = sb(scope, "rot0", [P, 4, T])
                m.rot = sb(scope, "rot", [P, 4, T])
                with ExitStack() as inner:
                    m.xs = sb(inner, "xs", [P, WIN + T])
                    m.kz = sb(inner, "kz", [P, HL // 2, 2, WIN + T])
                    m.v = sb(inner, "v", [P, NQ, HL, HDL + 1])
                    m.tt = sb(inner, "tt", [P, 4, T])
                    m.nm = sb(inner, "nm", [P, 3, 4])
                    m.ri = sb(inner, "ri", [P, 2, 4])
                    m.nrm = sb(inner, "nrm", [P, KT, 2 * HL])
                    m.rn = sb(inner, "rn", [P, KT, 2 * HL])
                    m.parts = sb(inner, "parts", [P, KT, 3, 2 * HL], BF16)
                    m.rnT = sb(inner, "rnT", [3 * 2 * HL, T], BF16)
                    m.attnT = sb(inner, "attnT", [P, HL // 2, T])
                    m.qr = m.xq.rearrange("p (a c) -> p a c", c=T)
                    m.pt, m.an = m.sd, m.rs[:, :, 0:4 * HDL]
                    m.t1, m.t2, m.pr = m.tt[:, 0:3, :], m.attnT[:, 0:3, :], m.tt[:, 0:3, :]
                    m.t3 = m.attnT[:, 3:6, :]
                    m.ge, m.hid, m.xsh = m.t1, m.attnT[:, 0:3, :], m.attnT[:, 3:5, :]
                    clear_local(nc, m, d)
                    load_first(nc, m, d)
                    with nc.Fori(0, DEPTH) as layer:
                        with nc.Fori(0, B // LU) as b:
                            local_attention(nc, m, b)
                        feed_forward(nc, m, d, layer)
            layer_norm_all(nc, m, m.xsum, m.xn, add=m.xn, label="ln3")

        m.xr = sb(ctx, "xr", [P, NT, D])
        m.slot = sb(ctx, "slot", [P, 2, NT])
        m.wt = sb(ctx, "wt", [P, 2, NT])
        m.keep = sb(ctx, "keep", [P, 2, NT])
        m.red = sb(ctx, "red", [P, 3, NT])
        m.slotu = sb(ctx, "slotu", [P, 2, NT], U32)
        token_rows(nc, m, m.xn, m.xr, "xrows")
        with ExitStack() as scope:
            m.probs = sb(scope, "probs", [P, NT, E])
            with ExitStack() as inner:
                m.stats = sb(inner, "stats", [P, NT, NSTAT])
                m.sqr = sb(inner, "sqr", [P, NT, D])
                m.statT = sb(inner, "statT", [NSTAT, N])
                m.r1 = sb(inner, "r1", [P, RH])
                m.r1s = sb(inner, "r1s", [NSTAT, RH])
                m.r1b = sb(inner, "r1b", [RH, 1])
                m.r2 = sb(inner, "r2", [RH, E])
                m.rh = sb(inner, "rh", [RH, 2, T])
                token_stats(nc, m)
                router(nc, m, d)
            with ExitStack() as inner:
                m.top8 = sb(inner, "top8", [P, NT, 8])
                m.idxf = sb(inner, "idxf", [P, NT, 2])
                m.eiota = sb(inner, "eiota", [P, E])
                m.ebase = sb(inner, "ebase", [E, 1])
                m.hot = sb(inner, "hot", [P, 2, NT, E])
                m.score = sb(inner, "score", [P, NT, E])
                m.tmpn = sb(inner, "tmpn", [P, NT, E])
                m.slotN = sb(inner, "slotN", [P, NT, E])
                m.scoreE = sb(inner, "scoreE", [E, N])
                m.quart = sb(inner, "quart", [P, N // 4])
                m.best = sb(inner, "best", [P, CAP])
                m.cand = sb(inner, "cand", [E, 4 * CAP])
                m.b8 = sb(inner, "b8", [E, 8])
                m.gt = sb(inner, "gt", [E, N])
                m.eq = sb(inner, "eq", [E, N])
                m.run = sb(inner, "run", [E, N])
                m.cnt = sb(inner, "cnt", [E, 1])
                m.room = sb(inner, "room", [E, 1])
                m.idx8 = sb(inner, "idx8", [P, NT, 8], U32)
                m.slotE = m.eq
                route(nc, m, d)
        with ExitStack() as scope:
            m.zrow = sb(scope, "zrow", [P, D])
            m.xrb = sb(scope, "xrb", [P, KT, D])
            m.slotb = sb(scope, "slotb", [P, 2, KT], U32)
            m.w_kvd = sb(scope, "w_kvd", [P, R1])
            m.w_kvu = sb(scope, "w_kvu", [P, 2 * HDT])
            m.w_q1 = sb(scope, "w_q1", [P, HDT])
            m.w_o1 = sb(scope, "w_o1", [P, H1 // 2, D])
            m.xn_b = sb(scope, "xn_b", [P, T])
            m.lat = sb(scope, "lat", [P, T])
            m.q1 = sb(scope, "q1", [P, H1 // 2, T])
            m.k1 = sb(scope, "k1", [P, H1 // 2, 2, T])
            m.v1 = sb(scope, "v1", [P, KT, H1, HD1 + 1])
            m.nm = sb(scope, "nm", [P, 4])
            m.ri = sb(scope, "ri", [P, 2, 4])
            m.pr = sb(scope, "pr", [P, 3, T])
            m.pt = sb(scope, "pt", [P, 3, T])
            m.an = sb(scope, "an", [P, 2, HDT])
            m.attnT = sb(scope, "attnT", [P, H1 // 2, T])
            load_latent(nc, m, d)
            with nc.Fori(0, B) as b:
                latent_attention(nc, m, d, b)

        m.xo = sb(ctx, "xo", [P, NT, D])
        token_rows(nc, m, m.xsum, m.xo, "orows")
        with ExitStack() as scope:
            m.xe = sb(scope, "xe", [P, GU, 2, 2, D])
            m.xeT = sb(scope, "xeT", [P, 2, CAP])
            m.aup = sb(scope, "aup", [P, GU, 2 * AINT])
            m.adn = sb(scope, "adn", [P, GU, D])
            m.wup = sb(scope, "wup", [P, GU, 2, 2 * INTER])
            m.wdn = sb(scope, "wdn", [P, GU, 4, D])
            m.hm = sb(scope, "hm", [P, 2, 3, CAP])
            m.sg = sb(scope, "sg", [P, 2, CAP])
            m.ye = sb(scope, "ye", [P, 2, 2, 2, D])
            m.yt = sb(scope, "yt", [P, 4, 2, D])
            with nc.Fori(0, GRP // GU) as i:
                experts(nc, m, d, i)
            combine(nc, m, d)


def clear_local(nc, m, d):
    with stage(nc, "clear", "loaded", "set") as (block, s):
        @block.sync
        def _(sp):
            sp.dma_start(m.rot0, d["c_rot"]).then_inc(s["loaded"], 16)
            sp.wait_ge(s["loaded"], 16)

        @block.vector
        def _(dve):
            dve.memset(m.xs, 0.0)
            dve.memset(m.kz, 0.0).then_inc(s["set"], 1)


def constants():
    import numpy as np
    f = np.float32
    c = {}
    c["c_ident"] = np.eye(P, dtype=f)
    c["c_bones8"] = np.kron(np.eye(H0, dtype=f), np.ones((HD0, HD0), f))
    c["c_heads"] = np.tile(np.kron(np.eye(2, dtype=f), np.ones((HDL // 2, 1), f)), (2, 1))
    c["c_hmask"] = np.kron(np.eye(H0, dtype=f), np.ones((HD0, 1), f))
    pat = np.zeros((H0, HD0, 2, 3, 3, 3, HD0), f)
    for a in range(3):
        for i in range(HD0):
            pat[:, i, 0, a, a, :, i] = 1
            pat[:, i, 1, a, :, a, i] = 1
    c["c_pat"] = pat.reshape(P, 2, 3, 9 * HD0)
    q, k = np.arange(P)[:, None], np.arange(P)[None, :]
    c["c_causal"] = np.where(k <= q, 0, MASKED).astype(f)
    band = (k >= q) & (k <= q + WIN)
    first = band & (k >= WIN)
    c["c_local"] = np.stack([np.tile(np.where(w, 0, MASKED).astype(f), (1, 4)) for w in (first, band)], 1)
    spread = np.zeros((3, HL, 2, HL, 2, 2, HDL // 2), f)
    for u in range(HL):
        for h in range(2):
            spread[:, u, h, u, :, h, :] = 1
    c["c_spread"] = spread.reshape(3 * 2 * HL, HL, P)
    half = np.arange(0, HDL, 2, dtype=f)
    inv_freq = (1.0 / f(10000.0) ** (half / f(HDL))).astype(f)
    t = np.arange(T, dtype=f)
    freqs = t[:, None] * inv_freq[None, :]
    base = ((half + f(0.4 * HDL)) / f(1.4 * HDL)).astype(f)
    power = ((t - T // 2) / f(WIN // 2)).astype(f)
    scale = (base[None, :] ** power[:, None]).astype(f)
    cos, sin = np.cos(freqs).astype(f), np.sin(freqs).astype(f)
    inv = (f(1.0) / scale).astype(f)
    parts = [(cos * scale, cos * scale), (sin * scale, -sin * scale), (cos * inv, cos * inv), (sin * inv, -sin * inv)]
    c["c_rot"] = np.stack([np.concatenate([a.T, a.T, b2.T, b2.T], 0) for a, b2 in parts], 1).astype(f)
    return {k2: np.ascontiguousarray(v) for k2, v in c.items()}


def laid_out(x):
    import numpy as np
    a = {k: np.ascontiguousarray(v) for k, v in x.items()}
    out = {"x": a["L0_attn_x"]}
    for n in ("L0_attn_w_q", "L0_attn_w_k", "L0_attn_w_v", "L0_attn_w_o", "L0_ffn_W1",
              "L1_attn_w_kv_down", "L1_attn_w_kv_up", "L1_attn_w_q", "L1_attn_w_out"):
        out[n] = a[n]
    w = a["L0_ffn_Wqkv"]
    qk = w[:, :, 0:2 * INNER].reshape(DEPTH, D, HL, 2, 2, HDL // 2).transpose(0, 1, 2, 4, 3, 5)
    behind = ((0, 1), (0, 0), (0, 0))
    out["p_Wqkv"] = np.pad(np.concatenate([qk.reshape(DEPTH, D, 2 * INNER), w[:, :, 2 * INNER:]], 2), behind)
    out["p_Wo"] = np.pad(a["L0_ffn_Wo"], behind)
    out["p_g_q"] = np.tile(a["L0_attn_g_q"], H0)[:, None]
    out["p_g_k"] = np.tile(a["L0_attn_g_k"], H0)[:, None]
    out["p_b_o"], out["p_gamma"], out["p_beta"] = (a["L0_attn_" + n][:, None] for n in ("b_o", "gamma", "beta"))
    pad = len(FK) * P - DIN
    out["p_W2"] = np.pad(a["L0_ffn_W2"], ((0, 0), (0, pad), (0, 0)))
    b1 = np.pad(a["L0_ffn_b1"].reshape(DEPTH, 2, DIN), ((0, 0), (0, 0), (0, pad)))
    out["p_b1"] = b1.reshape(DEPTH, 2 * len(FK), P).transpose(0, 2, 1)
    out["p_lnp"] = np.stack([a["L0_ffn_ln_g"], a["L0_ffn_ln_b"], a["L0_ffn_b2"]], 2)
    cols = []
    for n in ("L0_ffn_q_scale", "L0_ffn_k_scale"):
        cols.append(np.tile(a[n].reshape(DEPTH, 2, 1, HDL // 2), (1, 1, 2, 1)).reshape(DEPTH, P))
    out["p_qks"] = np.pad(np.stack(cols, 2), behind)
    r1 = a["L1_ffn_r1_w"].T
    out["p_r1"], out["p_r1s"] = r1[:D], r1[D:]
    out["p_r1b"], out["p_r2"] = a["L1_ffn_r1_b"][:, None], a["L1_ffn_r2_w"].T
    for short, n in (("p_wup", "w_up"), ("p_wdn", "w_down"), ("p_aup", "a_up"), ("p_adn", "a_down")):
        out[short] = a["L1_ffn_" + n].transpose(0, 2, 1)
    return {k: np.ascontiguousarray(v) for k, v in out.items()}


def kernel(**inputs):
    import numpy as np
    import concourse.bacc as bacc
    from concourse.bass_utils import run_bass_kernel_spmd

    nc = bacc.Bacc("TRN2", target_bir_lowering=False, num_devices=1)
    arrays = {**constants(), **laid_out(inputs)}
    d = {}
    for name, a in arrays.items():
        d[name] = nc.dram_tensor(name, a.shape, mybir.dt.from_np(a.dtype), kind="ExternalInput").ap()
    d["out"] = nc.dram_tensor("out", (B, T, D), F32, kind="ExternalOutput").ap()
    build(nc, d)
    r = run_bass_kernel_spmd(nc, [arrays], core_ids=[0])
    return r.results[0]["out"]
```
